# Optimizing a Trainium2 kernel written in Bass

```python
import numpy as np
import jax
import jax.numpy as jnp

def _softmax(x, axis=-1):
    return jax.nn.softmax(x, axis=axis)

def _gelu(x):
    return jax.nn.gelu(x, approximate=True)

def _silu(x):
    return jax.nn.silu(x)

def _sigmoid(x):
    return jax.nn.sigmoid(x)

def _layernorm(x, axis=-1, eps=1e-05):
    m = jnp.mean(x, axis=axis, keepdims=True)
    v = jnp.var(x, axis=axis, keepdims=True)
    return (x - m) / jnp.sqrt(v + eps)

def _scatter_add(tgt, idx, src, axis=0):
    return tgt.at[idx].add(src)

def _segment_sum(src, seg, n):
    return jax.ops.segment_sum(src, seg, n)
kernel_name = 'mk_gnn_resnorm_d4_gnn_r8_f1b6bf'

def setup_inputs(seed: int=0):
    np.random.seed(seed)
    _w = jnp.asarray

    def _rec_inputs():
        import jax
        import jax.numpy as jnp
        _gk = jax.random.key(seed)
        x = -0.000202 + 1 * jax.random.normal(jax.random.fold_in(_gk, 1), (6250, 128), jnp.float32)
        src = jax.random.randint(jax.random.fold_in(_gk, 2), (100000,), 0, 6250, jnp.int32)
        dst = jax.random.randint(jax.random.fold_in(_gk, 3), (100000,), 0, 6250, jnp.int32)
        _o = jnp.argsort(dst, stable=True)
        src = src[_o]
        dst = dst[_o]
        edge_attr_128 = -4.21973e-05 + 0.999841 * jax.random.normal(jax.random.fold_in(_gk, 13), (100000, 128), jnp.float32)
        return (x, src, dst, edge_attr_128)
    x, src, dst, edge_attr_128 = _rec_inputs()

    def _L0_gnn_setup():
        import jax, jax.numpy as jnp
        import numpy as np
        N = 6250
        E = 75000
        D = 128
        G = 64
        GN_EPS = 1e-05

        def graph_norm(x, batch, weight, bias, mean_scale):
            ones = jnp.ones((x.shape[0],), dtype=x.dtype)
            cnt = jnp.maximum(jax.ops.segment_sum(ones, batch, num_segments=G), 1.0)[:, None]
            mean = jax.ops.segment_sum(x, batch, num_segments=G) / cnt
            out = x - mean[batch] * mean_scale
            var = jax.ops.segment_sum(out * out, batch, num_segments=G) / cnt
            std = jnp.sqrt(var + GN_EPS)
            return weight * out / std[batch] + bias
        key = jax.random.key(seed)
        ks = jax.random.split(key, 10)
        node_h = jax.random.normal(ks[0], (N, D), dtype=jnp.float32)
        edge_attr = jax.random.normal(ks[1], (E, D), dtype=jnp.float32)
        batch = jnp.sort(jax.random.randint(ks[2], (N,), 0, G)).astype(jnp.int64)
        edge_index = jax.random.randint(ks[3], (2, E), 0, N).astype(jnp.int64)
        w1 = jax.random.normal(ks[4], (D, D), dtype=jnp.float32) * 0.02
        b1 = jnp.zeros((D,), dtype=jnp.float32)
        we = jax.random.normal(ks[5], (D, D), dtype=jnp.float32) * 0.02
        be = jnp.zeros((D,), dtype=jnp.float32)
        eps = jnp.zeros((), dtype=jnp.float32)
        gn_weight = jnp.ones((D,), dtype=jnp.float32)
        gn_bias = jnp.zeros((D,), dtype=jnp.float32)
        gn_mean_scale = jnp.ones((D,), dtype=jnp.float32)
        return {'node_h': node_h, 'edge_attr': edge_attr, 'batch': batch, 'edge_index': edge_index, 'w1': w1, 'b1': b1, 'we': we, 'be': be, 'eps': eps, 'gn_weight': gn_weight, 'gn_bias': gn_bias, 'gn_mean_scale': gn_mean_scale}
    _L0_gnn_all = _L0_gnn_setup()
    _L0_gnn_in = {k: v for k, v in _L0_gnn_all.items() if k in ('w1', 'b1', 'we', 'be', 'eps', 'gn_weight', 'gn_bias', 'gn_mean_scale')}
    del _L0_gnn_all

    def _L1_gnn_setup():
        import jax, jax.numpy as jnp
        import numpy as np
        N_NODES = 6250
        N_EDGES = 100000
        DIM = 128
        key = jax.random.key(seed)
        k1, k2, k3, k4, k5, k6 = jax.random.split(key, 6)
        x = jax.random.normal(k1, (N_NODES, DIM), dtype=jnp.float32)
        edge_index = jax.random.randint(k2, (2, N_EDGES), 0, N_NODES, dtype=jnp.int64)
        W_w = jax.random.normal(k3, (DIM, DIM), dtype=jnp.float32) * (1.0 / np.sqrt(DIM))
        W_b = jax.random.normal(k4, (DIM,), dtype=jnp.float32) * 0.01
        a_w = jax.random.normal(k5, (2 * DIM, 1), dtype=jnp.float32) * (1.0 / np.sqrt(2 * DIM))
        a_b = jax.random.normal(k6, (1,), dtype=jnp.float32) * 0.01
        return {'x': x, 'edge_index': edge_index, 'W_w': W_w, 'W_b': W_b, 'a_w': a_w, 'a_b': a_b}
    _L1_gnn_all = _L1_gnn_setup()
    _L1_gnn_in = {k: v for k, v in _L1_gnn_all.items() if k in ('W_w', 'W_b', 'a_w', 'a_b')}
    del _L1_gnn_all

    def _L2_gnn_setup():
        import jax, jax.numpy as jnp
        import numpy as np
        N, E = (6250, 100000)
        IN_DIM, H, D = (128, 8, 16)
        key = jax.random.key(seed)
        ks = jax.random.split(key, 9)
        s = 1.0 / np.sqrt(IN_DIM)
        return {'h': jax.random.normal(ks[0], (N, IN_DIM), dtype=jnp.float32), 'Wq': jax.random.normal(ks[1], (IN_DIM, H * D), dtype=jnp.float32) * s, 'bq': jnp.zeros((H * D,), dtype=jnp.float32), 'Wk': jax.random.normal(ks[2], (IN_DIM, H * D), dtype=jnp.float32) * s, 'bk': jnp.zeros((H * D,), dtype=jnp.float32), 'Wv': jax.random.normal(ks[3], (IN_DIM, H * D), dtype=jnp.float32) * s, 'bv': jnp.zeros((H * D,), dtype=jnp.float32), 'src': jax.random.randint(ks[4], (E,), 0, N, dtype=jnp.int32), 'dst': jax.random.randint(ks[5], (E,), 0, N, dtype=jnp.int32)}
    _L2_gnn_all = _L2_gnn_setup()
    _L2_gnn_in = {k: v for k, v in _L2_gnn_all.items() if k in ('Wq', 'bq', 'Wk', 'bk', 'Wv', 'bv')}
    del _L2_gnn_all

    def _L3_gnn_setup():
        import jax, jax.numpy as jnp
        import numpy as np
        N, E = (6250, 50000)
        OBJ_D, REL_D, EFF_D, HID = (128, 128, 128, 256)

        def _mlp_params(key, in_d, hid, out_d, scale=0.02):
            k1, k2 = jax.random.split(key)
            return (jax.random.normal(k1, (in_d, hid), jnp.float32) * scale, jnp.zeros((hid,), jnp.float32), jax.random.normal(k2, (hid, out_d), jnp.float32) * scale, jnp.zeros((out_d,), jnp.float32))

        def _mlp(x, w1, b1, w2, b2):
            h = jax.nn.relu(x @ w1 + b1)
            return h @ w2 + b2
        key = jax.random.key(seed)
        ks = jax.random.split(key, 7)
        objects = jax.random.normal(ks[0], (N, OBJ_D), jnp.float32)
        relations = jax.random.normal(ks[1], (E, REL_D), jnp.float32)
        senders = jax.random.randint(ks[2], (E,), 0, N, jnp.int32)
        receivers = jax.random.randint(ks[3], (E,), 0, N, jnp.int32)
        re_w1, re_b1, re_w2, re_b2 = _mlp_params(ks[4], 2 * OBJ_D + REL_D, HID, EFF_D)
        oe_w1, oe_b1, oe_w2, oe_b2 = _mlp_params(ks[5], OBJ_D, HID, EFF_D)
        ea_w1, ea_b1, ea_w2, ea_b2 = _mlp_params(ks[6], EFF_D + OBJ_D, HID, OBJ_D)
        return dict(objects=objects, relations=relations, senders=senders, receivers=receivers, re_w1=re_w1, re_b1=re_b1, re_w2=re_w2, re_b2=re_b2, oe_w1=oe_w1, oe_b1=oe_b1, oe_w2=oe_w2, oe_b2=oe_b2, ea_w1=ea_w1, ea_b1=ea_b1, ea_w2=ea_w2, ea_b2=ea_b2)
    _L3_gnn_all = _L3_gnn_setup()
    _L3_gnn_in = {k: v for k, v in _L3_gnn_all.items() if k in ('re_w1', 're_b1', 're_w2', 're_b2', 'oe_w1', 'oe_b1', 'oe_w2', 'oe_b2', 'ea_w1', 'ea_b1', 'ea_w2', 'ea_b2')}
    del _L3_gnn_all
    return {'x': x, 'src': src, 'dst': dst, 'edge_attr_128': edge_attr_128, 'L0_gnn_w1': _L0_gnn_in['w1'], 'L0_gnn_b1': _L0_gnn_in['b1'], 'L0_gnn_we': _L0_gnn_in['we'], 'L0_gnn_be': _L0_gnn_in['be'], 'L0_gnn_eps': _L0_gnn_in['eps'], 'L0_gnn_gn_weight': _L0_gnn_in['gn_weight'], 'L0_gnn_gn_bias': _L0_gnn_in['gn_bias'], 'L0_gnn_gn_mean_scale': _L0_gnn_in['gn_mean_scale'], 'L1_gnn_W_w': _L1_gnn_in['W_w'], 'L1_gnn_W_b': _L1_gnn_in['W_b'], 'L1_gnn_a_w': _L1_gnn_in['a_w'], 'L1_gnn_a_b': _L1_gnn_in['a_b'], 'L2_gnn_Wq': _L2_gnn_in['Wq'], 'L2_gnn_bq': _L2_gnn_in['bq'], 'L2_gnn_Wk': _L2_gnn_in['Wk'], 'L2_gnn_bk': _L2_gnn_in['bk'], 'L2_gnn_Wv': _L2_gnn_in['Wv'], 'L2_gnn_bv': _L2_gnn_in['bv'], 'L3_gnn_re_w1': _L3_gnn_in['re_w1'], 'L3_gnn_re_b1': _L3_gnn_in['re_b1'], 'L3_gnn_re_w2': _L3_gnn_in['re_w2'], 'L3_gnn_re_b2': _L3_gnn_in['re_b2'], 'L3_gnn_oe_w1': _L3_gnn_in['oe_w1'], 'L3_gnn_oe_b1': _L3_gnn_in['oe_b1'], 'L3_gnn_oe_w2': _L3_gnn_in['oe_w2'], 'L3_gnn_oe_b2': _L3_gnn_in['oe_b2'], 'L3_gnn_ea_w1': _L3_gnn_in['ea_w1'], 'L3_gnn_ea_b1': _L3_gnn_in['ea_b1'], 'L3_gnn_ea_w2': _L3_gnn_in['ea_w2'], 'L3_gnn_ea_b2': _L3_gnn_in['ea_b2']}

def reference(x, src, dst, edge_attr_128, L0_gnn_w1, L0_gnn_b1, L0_gnn_we, L0_gnn_be, L0_gnn_eps, L0_gnn_gn_weight, L0_gnn_gn_bias, L0_gnn_gn_mean_scale, L1_gnn_W_w, L1_gnn_W_b, L1_gnn_a_w, L1_gnn_a_b, L2_gnn_Wq, L2_gnn_bq, L2_gnn_Wk, L2_gnn_bk, L2_gnn_Wv, L2_gnn_bv, L3_gnn_re_w1, L3_gnn_re_b1, L3_gnn_re_w2, L3_gnn_re_b2, L3_gnn_oe_w1, L3_gnn_oe_b1, L3_gnn_oe_w2, L3_gnn_oe_b2, L3_gnn_ea_w1, L3_gnn_ea_b1, L3_gnn_ea_w2, L3_gnn_ea_b2):
    import jax
    import jax.numpy as jnp

    def _L0_gnn_ref(node_h, edge_attr, batch, edge_index, w1, b1, we, be, eps, gn_weight, gn_bias, gn_mean_scale):
        import jax, jax.numpy as jnp
        import numpy as np
        N = 6250
        E = 75000
        D = 128
        G = 64
        GN_EPS = 1e-05

        def graph_norm(x, batch, weight, bias, mean_scale):
            ones = jnp.ones((x.shape[0],), dtype=x.dtype)
            cnt = jnp.maximum(jax.ops.segment_sum(ones, batch, num_segments=G), 1.0)[:, None]
            mean = jax.ops.segment_sum(x, batch, num_segments=G) / cnt
            out = x - mean[batch] * mean_scale
            var = jax.ops.segment_sum(out * out, batch, num_segments=G) / cnt
            std = jnp.sqrt(var + GN_EPS)
            return weight * out / std[batch] + bias
        h = node_h @ w1.T + b1
        src, dst = (edge_index[0], edge_index[1])
        msg = jax.nn.silu(h[src] + (edge_attr @ we.T + be))
        agg = jax.ops.segment_sum(msg, dst, num_segments=N)
        conv = (1.0 + eps) * h + agg
        out = jax.nn.silu(conv)
        return graph_norm(out + node_h, batch, gn_weight, gn_bias, gn_mean_scale)

    def _L1_gnn_ref(x, edge_index, W_w, W_b, a_w, a_b):
        import jax, jax.numpy as jnp
        import numpy as np
        N_NODES = 6250
        N_EDGES = 100000
        DIM = 128
        h = x @ W_w + W_b
        row, col = (edge_index[0], edge_index[1])
        a_src, a_dst = (a_w[:DIM], a_w[DIM:])
        e = h[row] @ a_src + h[col] @ a_dst + a_b
        e = jax.nn.leaky_relu(e, negative_slope=0.01)
        attention = jax.nn.softmax(e, axis=0)
        msg = attention * h[col]
        out = jax.ops.segment_sum(msg, row, num_segments=N_NODES)
        return out

    def _L2_gnn_ref(h, Wq, bq, Wk, bk, Wv, bv, src, dst):
        import jax, jax.numpy as jnp
        import numpy as np
        N, E = (6250, 100000)
        IN_DIM, H, D = (128, 8, 16)
        n = h.shape[0]
        Q = (h @ Wq + bq).reshape(n, H, D)
        K = (h @ Wk + bk).reshape(n, H, D)
        V = (h @ Wv + bv).reshape(n, H, D)
        score = jnp.einsum('ehd,ehd->eh', K[src], Q[dst]) / jnp.sqrt(jnp.asarray(D, h.dtype))
        score = jnp.clip(score, -5.0, 5.0)
        smax = jax.ops.segment_max(score, dst, num_segments=n)
        ex = jnp.exp(score - smax[dst])
        denom = jax.ops.segment_sum(ex, dst, num_segments=n)
        a = ex / denom[dst]
        m = V[src] * a[:, :, None]
        wV = jax.ops.segment_sum(m, dst, num_segments=n)
        return wV.reshape(n, H * D)

    def _L3_gnn_ref(objects, relations, senders, receivers, re_w1, re_b1, re_w2, re_b2, oe_w1, oe_b1, oe_w2, oe_b2, ea_w1, ea_b1, ea_w2, ea_b2):
        import jax, jax.numpy as jnp
        import numpy as np
        N, E = (6250, 50000)
        OBJ_D, REL_D, EFF_D, HID = (128, 128, 128, 256)

        def _mlp_params(key, in_d, hid, out_d, scale=0.02):
            k1, k2 = jax.random.split(key)
            return (jax.random.normal(k1, (in_d, hid), jnp.float32) * scale, jnp.zeros((hid,), jnp.float32), jax.random.normal(k2, (hid, out_d), jnp.float32) * scale, jnp.zeros((out_d,), jnp.float32))

        def _mlp(x, w1, b1, w2, b2):
            h = jax.nn.relu(x @ w1 + b1)
            return h @ w2 + b2
        _obj_enc = _mlp(objects, oe_w1, oe_b1, oe_w2, oe_b2)
        rel_inputs = jnp.concatenate([objects[senders], objects[receivers], relations], axis=-1)
        rel_effects = _mlp(rel_inputs, re_w1, re_b1, re_w2, re_b2)
        agg_effects = jax.ops.segment_sum(rel_effects, receivers, num_segments=objects.shape[0])
        effect_inputs = jnp.concatenate([objects, agg_effects], axis=-1)
        updated_objects = _mlp(effect_inputs, ea_w1, ea_b1, ea_w2, ea_b2)
        return updated_objects
    edge_index = jnp.stack([src, dst])
    batch0 = jnp.zeros((6250,), jnp.int32)
    x = _layernorm(x + _L0_gnn_ref(x, edge_attr_128, batch0, edge_index, L0_gnn_w1, L0_gnn_b1, L0_gnn_we, L0_gnn_be, L0_gnn_eps, L0_gnn_gn_weight, L0_gnn_gn_bias, L0_gnn_gn_mean_scale), axis=-1)
    x = _layernorm(x + _L1_gnn_ref(x, edge_index, L1_gnn_W_w, L1_gnn_W_b, L1_gnn_a_w, L1_gnn_a_b), axis=-1)
    x = _layernorm(x + _L2_gnn_ref(x, L2_gnn_Wq, L2_gnn_bq, L2_gnn_Wk, L2_gnn_bk, L2_gnn_Wv, L2_gnn_bv, src, dst), axis=-1)
    x = _layernorm(x + _L3_gnn_ref(x, edge_attr_128, src, dst, L3_gnn_re_w1, L3_gnn_re_b1, L3_gnn_re_w2, L3_gnn_re_b2, L3_gnn_oe_w1, L3_gnn_oe_b1, L3_gnn_oe_w2, L3_gnn_oe_b2, L3_gnn_ea_w1, L3_gnn_ea_b1, L3_gnn_ea_w2, L3_gnn_ea_b2), axis=-1)
    return x

_drawn_inputs = setup_inputs


def setup_inputs(seed=0):
    import zlib

    import numpy as np

    out = dict(_drawn_inputs(seed))
    spreads = {'L0_gnn_b1': (0.0, 0.1),
     'L0_gnn_be': (0.0, 0.1),
     'L0_gnn_gn_weight': (1.0, 0.2),
     'L0_gnn_gn_bias': (0.0, 0.1),
     'L0_gnn_gn_mean_scale': (1.0, 0.2),
     'L2_gnn_bq': (0.0, 0.303),
     'L2_gnn_bk': (0.0, 2.0),
     'L2_gnn_bv': (0.0, 0.1),
     'L3_gnn_re_b1': (0.0, 0.531),
     'L3_gnn_re_b2': (0.0, 0.1),
     'L3_gnn_oe_b1': (0.0, 0.1),
     'L3_gnn_oe_b2': (0.0, 0.1),
     'L3_gnn_ea_b1': (0.0, 0.412),
     'L3_gnn_ea_b2': (0.0, 0.1)}
    factors = {'L1_gnn_W_w': 26.559, 'L1_gnn_W_b': 64.0, 'L1_gnn_a_w': 26.433}
    for name, (base, spread) in spreads.items():
        noise = np.random.default_rng([zlib.crc32(name.encode()), seed]).standard_normal(out[name].shape)
        drawn = base * np.exp(spread * noise) if base else spread * noise
        out[name] = jnp.asarray(drawn.astype(out[name].dtype))
    for name, factor in factors.items():
        out[name] = (out[name] * factor).astype(out[name].dtype)
    return out
```

```python
from contextlib import ExitStack

import numpy as np

import concourse.bass as bass
from concourse import mybir
from concourse.alu_op_type import AluOpType as ALU

F32 = mybir.dt.float32
BF16 = mybir.dt.bfloat16
I32 = mybir.dt.int32
ACT = mybir.ActivationFunctionType
AX = mybir.AxisListType

P = 128
N, E, D = 6250, 100000, 128
HID = 256
HEADS, HD = 8, 16
NT = 50
NP = NT * P
RT = (N + P - 1) // P
ET = (E + P - 1) // P
EP = ET * P
PAD_NODE = RT * P - 1
G = 4
GROUPS = 4
U = G * GROUPS
ITERS = -(-(ET + RT - 1) // U)
STEPS = ITERS * U
SB = -(-(STEPS + U) // P)
ST = SB * P
ACCS = 4
AROWS = NP + P
EPS = 1e-5
NEG = -3.0e38


def semaphores(nc, c, prefix):
    taken = []

    def take(name):
        taken.append(nc.alloc_semaphore(prefix + name))
        return taken[-1]

    def give_back():
        nc.clear_and_free_semaphores(taken)
        nc.all_engine_barrier()

    c.callback(give_back)
    return take


class Kit:
    pass


def pipeline(eng, iters, per, *stages, lags=None, loads=0):
    lags = lags or range(len(stages))
    last = max(lags)
    begin = loads if loads >= last else per + loads
    rounds = (iters * per - begin) // per

    def fixed(turns):
        for t in turns:
            for stage, lag in zip(stages, lags):
                if 0 <= t - lag < iters * per:
                    stage(*divmod(t - lag, per))

    fixed(range(begin))
    with eng.Fori(0, rounds) as m:
        for t in range(begin, begin + per):
            for stage, lag in zip(stages, lags):
                stage(m + (t - lag) // per, (t - lag) % per)
    fixed(range(begin + rounds * per, iters * per + last))


def load_steps(nc, eng, row, first, top):
    _, vals = nc.values_load_multi_w_load_instructions(
        row[0:1, bass.ds(first, U)], engines=[eng.engine], min_val=0, max_val=top,
        skip_runtime_bounds_check_because="the step table is clamped to this range when it is made")
    return vals


def phase_tables(nc, k):
    with ExitStack() as c:
        sb = lambda n, s, d: c.enter_context(nc.sbuf_tensor(n, s, d))
        sem = semaphores(nc, c, "t_")
        ends = sb("t_ends", [1, 2, ET], I32)
        tiles = sb("t_tiles", [1, 2, ET], I32)
        tf = sb("t_tf", [1, 2, ET], F32)
        length = sb("t_length", [1, ET], F32)
        nought = sb("t_nought", [1, ET], F32)
        upto = sb("t_upto", [1, ET], F32)
        pair = sb("t_pair", [1, 2, ET], F32)
        shift = sb("t_shift", [1, ET + 1], F32)
        wide = sb("t_wide", [P, 2, ET], F32)
        junk = sb("t_junk", [P, ET], F32)
        step_i = sb("t_step_i", [P, SB], I32)
        step_no = sb("t_step_no", [P, SB], F32)
        at_edge = sb("t_at_edge", [P, SB], F32)
        at_node = sb("t_at_node", [P, SB], F32)
        edge_i = sb("t_edge_i", [P, SB], I32)
        ek = sb("t_ek", [P, 2, SB], I32)
        base = sb("t_base", [P, SB], F32)
        srcg = sb("t_srcg", [P, SB, P], I32)
        dstg = sb("t_dstg", [P, SB, P], I32)
        srcf = sb("t_srcf", [P, SB, P], F32)
        relf = sb("t_relf", [P, SB, P], F32)
        relh = sb("t_relh", [P, SB, P], BF16)
        lof = sb("t_lof", [P, SB, P], BF16)
        hi_idx = sb("t_hi_idx", [P, ST], I32)
        loi = sb("t_loi", [P, SB, P], I32)
        loaded, spread, rows, gathered = sem("loaded"), sem("spread"), sem("rows"), k.gathered
        chain, stored, turned, const, got = sem("chain"), sem("stored"), sem("turned"), sem("const"), sem("got")
        conv, tables = sem("conv"), sem("tables")
        with nc.Block() as block:
            @block.sync
            def _(sp):
                with nc.allow_non_contiguous_dma(reason="first and last edge of each tile"):
                    for n, col in ((0, 0), (1, P - 1)):
                        sp.dma_start(ends[0:1, n, :], k.dst[:, col:col + 1].rearrange("e o -> o e")).then_inc(loaded, 16)
                sp.wait_ge(rows, 1)
                sp.dma_start(k.row_dram, pair[0:1, :, :].rearrange("o a e -> o (a e)")).then_inc(stored, 16)
                sp.wait_ge(stored, 16)
                sp.dma_start(wide[:].rearrange("p a e -> p (a e)"), k.row_dram.to_broadcast([P, 2 * ET])).then_inc(spread, 16)
                sp.wait_ge(tables, 1)
                with nc.allow_non_contiguous_dma(reason="a column per block of steps"):
                    for n in range(2):
                        sp.dma_start(k.ek_dram[n].rearrange("(j p) -> p j", p=P), ek[:, n, :]).then_inc(stored, 16)
                sp.wait_ge(stored, 48)
                for n in range(2):
                    sp.dma_start(k.ek[n][0:1, :], k.ek_dram[n:n + 1, :]).then_inc(got, 16)
                sp.wait_ge(conv, 3)
                sp.dma_start(k.rel_rows.rearrange("(j p) e -> p j e", p=P), relh[:]).then_inc(stored, 16)
                sp.dma_start(k.src_rows.rearrange("(j p) e -> p j e", p=P), srcf[:]).then_inc(stored, 16)
                sp.dma_start(k.lo_rows.rearrange("(j p) e -> p j e", p=P), lof[:]).then_inc(stored, 16)
                sp.wait_ge(stored, 96)
                sp.wait_ge(got, 32)

            @block.gpsimd
            def _(g):
                g.iota(step_i[:], pattern=[[P, SB]], base=0, channel_multiplier=1).then_inc(const, 1)
                g.iota(k.lane_i[:], pattern=[[1, P]], base=0, channel_multiplier=0).then_inc(const, 1)
                g.iota(k.part_i[:], pattern=[[0, 1]], base=0, channel_multiplier=1).then_inc(const, 1)
                g.iota(k.trash_i[:], pattern=[[0, G]], base=NP, channel_multiplier=1).then_inc(const, 1)
                for j in range(SB):
                    if j == 0:
                        g.wait_ge(tables, 1)
                    for t, (to, of) in enumerate(((srcg, k.src), (dstg, k.dst))):
                        g.indirect_dma_start(out=to[:, j, :], out_offset=None, in_=of,
                                             in_offset=bass.IndirectOffsetOnAxis(ap=edge_i[:, j:j + 1], axis=0)
                                             ).then_inc(gathered, 16)

            @block.vector
            def _(v):
                n = [0]

                def link(ins):
                    n[0] += 1
                    ins.then_inc(chain, 1)
                    v.wait_ge(chain, n[0])

                v.wait_ge(const, 4)
                link(v.tensor_copy(step_no[:], step_i[:]))
                link(v.tensor_copy(k.lane[:], k.lane_i[:]))
                link(v.tensor_copy(k.part[:], k.part_i[:]))
                link(v.tensor_copy(k.trash[:], k.trash_i[:]))
                link(v.tensor_scalar(k.ident[:], k.lane[:], k.part[:, 0:1], None, ALU.is_equal))
                link(v.tensor_scalar(k.before[:], k.lane[:], k.part[:, 0:1], None, ALU.is_lt))
                link(v.memset(k.ones[:], 1.0))
                link(v.memset(nought[:], 0.0))
                link(v.memset(k.is_node[:], 0.0))
                link(v.tensor_scalar(k.is_node[:, 0:1], k.part[:, 0:1], float(N - (RT - 1) * P), None, ALU.is_lt))
                v.wait_ge(loaded, 32)
                link(v.tensor_scalar(tiles[:], ends[:], 7, None, ALU.arith_shift_right))
                link(v.tensor_copy(tf[:], tiles[:]))
                link(v.tensor_tensor(length[:], tf[:, 1, :], tf[:, 0, :], ALU.subtract))
                link(v.tensor_scalar(length[:], length[:], 1.0, None, ALU.add))
                link(v.tensor_tensor_scan(upto[:], length[:], nought[:], 0.0, ALU.add, ALU.add))
                link(v.tensor_tensor(pair[:, 0, :], upto[:], length[:], ALU.subtract))
                link(v.memset(shift[:, 0:1], 0.0))
                link(v.tensor_tensor(shift[:, 1:ET + 1], tf[:, 0, :], pair[:, 0, :], ALU.subtract))
                link(v.tensor_tensor(pair[:, 1, :], shift[:, 1:ET + 1], shift[:, 0:ET], ALU.subtract))
                v.sem_inc(rows, 1)
                v.wait_ge(spread, 16)
                for j in range(SB):
                    link(v.tensor_scalar(junk[:], wide[:, 0, :], step_no[:, j:j + 1], 0.0, ALU.is_le, ALU.add,
                                         accum_out=at_edge[:, j:j + 1]))
                    link(v.scalar_tensor_tensor(out=junk[:], in0=wide[:, 0, :], scalar=step_no[:, j:j + 1], in1=wide[:, 1, :],
                                                op0=ALU.is_le, op1=ALU.mult, accum_out=at_node[:, j:j + 1]))
                link(v.tensor_scalar(edge_i[:], at_edge[:], -1.0, None, ALU.add))
                link(v.tensor_tensor(at_node[:], at_node[:], step_no[:], ALU.add))
                link(v.tensor_scalar(base[:], at_node[:], -float(P), None, ALU.mult))
                link(v.tensor_copy(ek[:, 0, :], edge_i[:]))
                link(v.tensor_scalar(ek[:, 1, :], at_node[:], float(RT - 1), None, ALU.min))
                v.sem_inc(tables, 1)
                v.wait_ge(gathered, 16 * 2 * SB)
                link(v.tensor_scalar(loi[:], srcg[:], P - 1, None, ALU.bitwise_and))
                link(v.tensor_copy(lof[:], loi[:]))
                link(v.tensor_copy(srcf[:], srcg[:]))
                for j in range(SB):
                    link(v.tensor_scalar(relf[:, j, :], dstg[:, j, :], base[:, j:j + 1], None, ALU.add))
                link(v.tensor_copy(relh[:], relf[:]))
                v.sem_inc(conv, 3)
                for j in range(SB):
                    v.wait_ge(turned, 2 * j + 2)
                    link(v.tensor_copy(k.rel_cols[:, j * P:(j + 1) * P], k.psum[:, 2 * (j % 2), 0:P]))
                    link(v.tensor_copy(k.src_cols[:, j * P:(j + 1) * P], k.psum[:, 2 * (j % 2) + 1, 0:P]))
                    v.sem_inc(k.turn_free, 1)
                link(v.tensor_copy(k.src_idx[:], k.src_cols[:]))
                link(v.tensor_scalar(hi_idx[:], k.src_idx[:], 7, None, ALU.arith_shift_right))
                link(v.tensor_copy(k.hi_cols[:], hi_idx[:]))

            @block.tensor
            def _(pe):
                pe.wait_ge(conv, 3)
                for j in range(SB):
                    if j >= 2:
                        pe.wait_ge(k.turn_free, j - 1)
                    pe.transpose(k.psum[:, 2 * (j % 2), 0:P], relf[:, j, :], k.ident[:]).then_inc(turned, 1)
                    pe.transpose(k.psum[:, 2 * (j % 2) + 1, 0:P], srcf[:, j, :], k.ident[:]).then_inc(turned, 1)


def phase_linear(nc, k, name, X, W, cols, bias, OUT):
    with ExitStack() as c:
        sb = lambda n, s, d: c.enter_context(nc.sbuf_tensor(name + n, s, d))
        sem = semaphores(nc, c, name)
        tile = sb("_tile", [P, 2, P], F32)
        tile_t = sb("_tile_t", [P, 2, P], F32)
        staged, turned, copied, product, added = (sem(n) for n in ("_staged", "_turned", "_copied", "_product", "_added"))
        HALF = NT // 2

        with nc.Block() as block:
            @block.vector
            def _(v):
                v.sem_inc(added, 2)

                def stage(i, b):
                    v.tensor_copy(tile[:, b:b + 1, :], X[:, bass.ds(2 * i + b, 1), :]).then_inc(staged, 1)

                def add(i, b):
                    v.wait_ge(product, 2 * i + b + 3)
                    v.tensor_tensor(OUT[:, bass.ds(2 * i + b, 1), :], k.psum[:, 2 + b:3 + b, 0:cols],
                                    bias.unsqueeze(1), ALU.add).then_inc(added, 1)

                pipeline(v, HALF, 2, stage, add)

            @block.tensor
            def _(pe):
                pe.sem_inc(product, 2)

                def turn(i, b):
                    pe.wait_ge(staged, 2 * i + b + 1)
                    pe.wait_ge(copied, 2 * i + b + 1)
                    pe.transpose(k.psum[:, b, 0:P], tile[:, b, :], k.ident[:]).then_inc(turned, 1)

                def multiply(i, b):
                    pe.wait_ge(copied, 2 * i + b + 3)
                    pe.wait_ge(added, 2 * i + b + 1)
                    pe.matmul(k.psum[:, 2 + b, 0:cols], tile_t[:, b, :], W, start=True, stop=True).then_inc(product, 1)

                pipeline(pe, HALF, 2, turn, multiply)

            @block.scalar
            def _(a):
                a.sem_inc(copied, 2)
                with a.Fori(0, HALF) as i:
                    for b in range(2):
                        a.wait_ge(turned, 2 * i + b + 1)
                        a.wait_ge(product, 2 * i + b + 1)
                        nc.scalar.copy(tile_t[:, b, :], k.psum[:, b, 0:P]).then_inc(copied, 1)


def vector_chain(nc, sem, v):
    n = [0]

    def link(ins):
        n[0] += 1
        ins.then_inc(sem, 1)
        v.wait_ge(sem, n[0])
    return link


def split3(link, v, parts, x):
    for n in range(3):
        link(v.tensor_copy(parts[:, :, n, :], x))
        if n < 2:
            link(v.tensor_tensor(x, x, parts[:, :, n, :], ALU.subtract))


def layer_norm(nc, link, v, Y, OUT, col, root, ask, rooted, turn):
    mean, var = col[:, 0, :], col[:, 1, :]
    wide = [P, NT, D]
    link(v.tensor_reduce(mean, Y, AX.X, ALU.add))
    link(v.tensor_scalar(mean, mean, 1.0 / D, None, ALU.mult))
    link(v.tensor_tensor(Y, Y, mean.unsqueeze(2).to_broadcast(wide), ALU.subtract))
    link(v.tensor_tensor(OUT, Y, Y, ALU.mult))
    link(v.tensor_reduce(var, OUT, AX.X, ALU.add))
    link(v.tensor_scalar(var, var, 1.0 / D, EPS, ALU.mult, ALU.add))
    v.sem_inc(ask, 1)
    v.wait_ge(rooted, turn)
    link(v.reciprocal(var, root))
    link(v.tensor_tensor(OUT, Y, var.unsqueeze(2).to_broadcast(wide), ALU.mult))


def phase_conv_edges(nc, k, table, agg, before):
    with ExitStack() as c:
        sb = lambda n, s, d: c.enter_context(nc.sbuf_tensor("c0_" + n, s, d))
        sem = semaphores(nc, c, "c0_")
        idx = sb("idx", [P, U], I32)
        ea = sb("ea", [P, U, P], F32)
        rows = sb("rows", [P, U, D], F32)
        msg = sb("msg", [P, 2, G, D], F32)
        oh = sb("oh", [P, 2, G, P], F32)
        ea_in = [sem(f"ea_in{u}") for u in range(U)]
        row_in = k.row_in
        ea_free, row_free, idx_ready, pool_turn = sem("ea_free"), sem("row_free"), sem("idx_ready"), sem("pool_turn")
        product, summed, msg_ready, oh_ready, spread, added, zero = (
            sem(n) for n in ("product", "summed", "msg_ready", "oh_ready", "spread", "added", "zero"))
        with nc.Block() as block:
            @block.sync
            def _(sp):
                with sp.Fori(0, ITERS) as i:
                    tile = load_steps(nc, sp, k.ek[0], i * U, ET - 1)
                    for u in range(U):
                        if u % G == 0:
                            sp.wait_ge(ea_free, GROUPS * i + u // G + 1)
                        sp.dma_start(ea[:, u, :], k.ea_t[:, bass.ds(tile[u] * P, P)]).then_inc(ea_in[u], 16)

            @block.gpsimd
            def _(g):
                with g.Fori(0, ITERS) as i:
                    for u in range(U):
                        if u % G == 0:
                            g.wait_ge(idx_ready, GROUPS * i + u // G + 1)
                            g.wait_ge(row_free, GROUPS * i + u // G + 1)
                            g.sem_inc(pool_turn, 1)
                        g.indirect_dma_start(out=rows[:, u, :], out_offset=None, in_=table,
                                             in_offset=bass.IndirectOffsetOnAxis(ap=idx[:, u:u + 1], axis=0)
                                             ).then_inc(row_in[u], 16)

            @block.tensor
            def _(pe):
                pe.sem_inc(ea_free, GROUPS)
                pe.sem_inc(spread, 2)

                def edge_product(i, j):
                    pe.wait_ge(summed, GROUPS * i + j + 1)
                    for q in range(G):
                        pe.wait_ge(ea_in[G * j + q], 16 * i + 16)
                        mm = pe.matmul(k.psum[:, j % 2, q * D:(q + 1) * D], ea[:, G * j + q, :], k.W[:, 0:D],
                                       start=True, stop=True)
                        if q == G - 1:
                            mm.then_inc(product, 1)
                    pe.wait_ge(product, GROUPS * i + j + 1)
                    pe.sem_inc(ea_free, 1)

                def sum_into_nodes(i, j):
                    pe.wait_ge(msg_ready, GROUPS * i + j + 1)
                    pe.wait_ge(oh_ready, GROUPS * i + j + 1)
                    pe.wait_ge(added, G * (GROUPS * i + j) + G)
                    for q in range(G):
                        mm = pe.matmul(k.psum[:, 2 + j % 2, q * D:(q + 1) * D], oh[:, j % 2, q, :], msg[:, j % 2, q, :],
                                       start=True, stop=True)
                    mm.then_inc(spread, 1)

                pipeline(pe, ITERS, GROUPS, edge_product, sum_into_nodes)

            @block.scalar
            def _(a):
                with a.Fori(0, ITERS) as i:
                    for j in range(GROUPS):
                        a.wait_ge(summed, GROUPS * i + j + 3)
                        nc.scalar.activation(msg[:, j % 2], msg[:, j % 2], ACT.Silu).then_inc(msg_ready, 1)

            @block.vector
            def _(v):
                v.memset(agg, 0.0).then_inc(zero, 1)
                v.wait_ge(zero, 1)
                v.sem_inc(summed, 2)
                v.sem_inc(row_free, GROUPS)
                v.sem_inc(added, 2 * G)

                def stage(i, j):
                    v.tensor_copy(idx[:, G * j:G * j + G], k.src_idx[:, bass.ds(i * U + G * j, G)]).then_inc(idx_ready, 1)

                for j in range(GROUPS):
                    stage(0, j)

                def front(i, j):
                    v.wait_ge(spread, GROUPS * i + j + 1)
                    v.tensor_tensor(oh[:, j % 2], k.lane[:].unsqueeze(1).to_broadcast([P, G, P]),
                                    k.rel_cols[:, bass.ds(i * U + G * j, G)].unsqueeze(2).to_broadcast([P, G, P]),
                                    ALU.is_equal).then_inc(oh_ready, 1)
                    v.wait_ge(product, GROUPS * i + j + 1)
                    for q in range(G):
                        v.wait_ge(row_in[G * j + q], 16 * i + 16 * (before + 1))
                    v.tensor_tensor(msg[:, j % 2].rearrange("p q d -> p (q d)"), k.psum[:, j % 2, :],
                                    rows[:, G * j:G * j + G, :].rearrange("p q d -> p (q d)"), ALU.add).then_inc(summed, 1)
                    v.wait_ge(summed, GROUPS * i + j + 3)
                    v.sem_inc(row_free, 1)
                    stage(i + 1, j)

                regs = {}

                def back(i, j):
                    if j == 0:
                        regs["node"] = load_steps(nc, v, k.ek[1], i * U, RT - 1)
                    v.wait_ge(spread, GROUPS * i + j + 3)
                    for q in range(G):
                        t = regs["node"][G * j + q]
                        v.wait_ge(added, G * (GROUPS * i + j) + q + 2 * G)
                        v.tensor_tensor(agg[:, bass.ds(t, 1), :], agg[:, bass.ds(t, 1), :],
                                        k.psum[:, 2 + j % 2:3 + j % 2, q * D:(q + 1) * D], ALU.add).then_inc(added, 1)

                pipeline(v, ITERS, GROUPS, front, back, loads=1)


def phase_conv_nodes(nc, k, H, Y, S1):
    with ExitStack() as c:
        sb = lambda n, s, d: c.enter_context(nc.sbuf_tensor("n0_" + n, s, d))
        sem = semaphores(nc, c, "n0_")
        col = sb("col", [P, 3, NT], F32)
        total = sb("total", [P, 2, D], F32)
        stat = sb("stat", [P, 3, D], F32)
        chain, ask, rooted, want, have, par = (sem(n) for n in ("chain", "ask", "rooted", "want", "have", "par"))
        wide = [P, NT, D]
        with nc.Block() as block:
            @block.sync
            def _(sp):
                for n, b in enumerate(("L0_gnn_gn_weight", "L0_gnn_gn_bias", "L0_gnn_gn_mean_scale")):
                    sp.dma_start(k.bias[:, n * D:(n + 1) * D], k.small[b].to_broadcast([P, D])).then_inc(par, 16)
                sp.dma_start(k.one[:, 0:1], k.small["L0_gnn_eps"].to_broadcast([P, 1])).then_inc(par, 16)

            @block.vector
            def _(v):
                link = vector_chain(nc, chain, v)
                gn = [k.bias[:, n * D:(n + 1) * D].unsqueeze(1).to_broadcast(wide) for n in range(3)]
                v.wait_ge(par, 64)
                link(v.tensor_scalar(k.one[:, 0:1], k.one[:, 0:1], 1.0, None, ALU.add))
                link(v.scalar_tensor_tensor(out=Y, in0=H, scalar=k.one[:, 0:1], in1=Y, op0=ALU.mult, op1=ALU.add))
                v.sem_inc(ask, 1)
                v.wait_ge(rooted, 1)
                link(v.tensor_tensor(Y, S1, k.X[:], ALU.add))
                link(v.tensor_tensor(Y[:, RT - 1:NT, :], Y[:, RT - 1:NT, :],
                                     k.is_node[:].unsqueeze(2).to_broadcast([P, NT - RT + 1, D]), ALU.mult))
                link(v.tensor_reduce(total[:, 0, :], Y.rearrange("p t d -> p d t"), AX.X, ALU.add))
                v.sem_inc(want, 1)
                v.wait_ge(have, 1)
                link(v.scalar_tensor_tensor(out=stat[:, 0, :], in0=k.psum[:, 0, 0:D], scalar=1.0 / N,
                                            in1=k.bias[:, 2 * D:3 * D], op0=ALU.mult, op1=ALU.mult))
                link(v.tensor_tensor(Y, Y, stat[:, 0, :].unsqueeze(1).to_broadcast(wide), ALU.subtract))
                link(v.tensor_tensor(S1, Y, Y, ALU.mult))
                link(v.tensor_tensor(S1[:, RT - 1:NT, :], S1[:, RT - 1:NT, :],
                                     k.is_node[:].unsqueeze(2).to_broadcast([P, NT - RT + 1, D]), ALU.mult))
                link(v.tensor_reduce(total[:, 1, :], S1.rearrange("p t d -> p d t"), AX.X, ALU.add))
                v.sem_inc(want, 1)
                v.wait_ge(have, 2)
                link(v.tensor_scalar(stat[:, 1, :], k.psum[:, 1, 0:D], 1.0 / N, EPS, ALU.mult, ALU.add))
                v.sem_inc(ask, 1)
                v.wait_ge(rooted, 2)
                link(v.reciprocal(stat[:, 1, :], stat[:, 2, :]))
                link(v.tensor_tensor(stat[:, 1, :], stat[:, 1, :], k.bias[:, 0:D], ALU.mult))
                link(v.tensor_tensor(Y, Y, stat[:, 1, :].unsqueeze(1).to_broadcast(wide), ALU.mult))
                link(v.tensor_tensor(Y, Y, gn[1], ALU.add))
                link(v.tensor_tensor(Y, Y, k.X[:], ALU.add))
                layer_norm(nc, link, v, Y, k.X[:], col, col[:, 2, :], ask, rooted, 3)

            @block.scalar
            def _(a):
                a.wait_ge(ask, 1)
                nc.scalar.activation(S1, Y, ACT.Silu).then_inc(rooted, 1)
                a.wait_ge(ask, 2)
                nc.scalar.activation(stat[:, 2, :], stat[:, 1, :], ACT.Sqrt).then_inc(rooted, 1)
                a.wait_ge(ask, 3)
                nc.scalar.activation(col[:, 2, :], col[:, 1, :], ACT.Sqrt).then_inc(rooted, 1)

            @block.tensor
            def _(pe):
                for n in range(2):
                    pe.wait_ge(want, n + 1)
                    pe.matmul(k.psum[:, n, 0:D], k.ones[:], total[:, n, :], start=True, stop=True).then_inc(have, 1)


def phase_table0(nc, k, H, S, table):
    with ExitStack() as c:
        sem = semaphores(nc, c, "t0_")
        made, landed = sem("made"), sem("landed")
        block = c.enter_context(nc.Block())

        @block.sync
        def _(sp):
            sp.dma_start(k.bias[:, 0:D], k.small["L0_gnn_be"].to_broadcast([P, D])).then_inc(landed, 16)
            sp.dma_start(k.W[:, 0:D], k.small["L0_gnn_wet"]).then_inc(landed, 16)
            sp.wait_ge(made, 1)
            sp.dma_start(table, S).then_inc(landed, 16)
            sp.wait_ge(landed, 48)

        @block.vector
        def _(v):
            v.wait_ge(landed, 32)
            v.tensor_tensor(S, H, k.bias[:, 0:D].unsqueeze(1).to_broadcast([P, NT, D]), ALU.add).then_inc(made, 1)


def phase_scores_nodes(nc, k, Hs, S, H3):
    with ExitStack() as c:
        sem = semaphores(nc, c, "s1_")
        score = c.enter_context(nc.sbuf_tensor("s1_score", [P, 2, NT], F32))
        chain = sem("chain")
        block = c.enter_context(nc.Block())

        @block.vector
        def _(v):
            link = vector_chain(nc, chain, v)
            for n in range(2):
                link(v.tensor_tensor(S, Hs, k.bias[:, n * D:(n + 1) * D].unsqueeze(1).to_broadcast([P, NT, D]), ALU.mult))
                link(v.tensor_reduce(score[:, n, :], S, AX.X, ALU.add))
            for n, parts in enumerate((k.src_score, k.dst_score)):
                for part in range(3):
                    link(v.tensor_copy(parts[:, :, part], score[:, n, :]))
                    if part < 2:
                        link(v.tensor_tensor(score[:, n, :], score[:, n, :], parts[:, :, part], ALU.subtract))
            split3(link, v, H3, Hs)


def phase_scores_edges(nc, k, scores):
    G8, PER = 8, U // 8
    WIDE = NT + 3
    with ExitStack() as c:
        sb = lambda n, s, d: c.enter_context(nc.sbuf_tensor("s_" + n, s, d))
        sem = semaphores(nc, c, "s_")
        rel = sb("rel", [P, PER, G8 * P], BF16)
        lo = sb("lo", [P, PER, G8 * P], BF16)
        is_rel = sb("is_rel", [P, PER, G8 * P], BF16)
        is_lo = sb("is_lo", [P, PER, G8 * P], BF16)
        mask = sb("mask", [P, PER, G8, WIDE], F32)
        picked = sb("picked", [P, PER, G8, WIDE], F32)
        rel_in = [sem(f"rel_in{n}") for n in range(PER)]
        lo_in = [sem(f"lo_in{n}") for n in range(PER)]
        rel_used, lo_used, mask_ready, product, read, reduced, preset, sp_turn = (
            sem(n) for n in ("rel_used", "lo_used", "mask_ready", "product", "read", "reduced", "preset", "sp_turn"))
        rel_flat = k.rel_rows.rearrange("(o s) e -> o (s e)", o=1)
        lo_flat = k.lo_rows.rearrange("(o s) e -> o (s e)", o=1)
        with nc.Block() as block:
            @block.sync
            def _(sp):
                with sp.Fori(0, ITERS) as i:
                    for j in range(PER):
                        at = bass.ds(sp.snap((i * U + j * G8) * P), G8 * P)
                        sp.wait_ge(rel_used, PER * i + j + 1)
                        sp.sem_inc(sp_turn, 1)
                        sp.dma_start(rel[:, j, :], rel_flat[:, at].to_broadcast([P, G8 * P])).then_inc(rel_in[j], 16)
                        sp.wait_ge(lo_used, PER * i + j + 1)
                        sp.sem_inc(sp_turn, 1)
                        sp.dma_start(lo[:, j, :], lo_flat[:, at].to_broadcast([P, G8 * P])).then_inc(lo_in[j], 16)

            @block.tensor
            def _(pe):
                with pe.Fori(0, ITERS) as i:
                    node = load_steps(nc, pe, k.ek[1], i * U, RT - 1)
                    for j in range(PER):
                        pe.wait_ge(rel_used, PER * i + j + 1 + PER)
                        pe.wait_ge(lo_used, PER * i + j + 1 + PER)
                        pe.wait_ge(read, PER * i + j + 1)
                        for q in range(G8):
                            cols = k.psum[:, j, q * WIDE:(q + 1) * WIDE]
                            for part in range(3):
                                pe.matmul(cols[:, 0:NT], is_lo[:, j, q * P:(q + 1) * P], k.src_score[:, :, part],
                                          start=(part == 0), stop=(part == 2))
                            mm = pe.matmul(cols[:, NT:WIDE], is_rel[:, j, q * P:(q + 1) * P],
                                           k.dst_score[:, bass.ds(node[j * G8 + q], 1), :], start=True, stop=True)
                        mm.then_inc(product, 1)

            @block.vector
            def _(v):
                v.memset(mask[:, :, :, NT:WIDE], 1.0).then_inc(preset, 1)
                v.sem_inc(rel_used, PER)
                v.sem_inc(lo_used, PER)
                v.sem_inc(read, PER)
                v.wait_ge(preset, 1)

                def matrices(i, j):
                    v.wait_ge(rel_in[j], 16 * i + 16)
                    v.tensor_scalar(is_rel[:, j, :], rel[:, j, :], k.part[:, 0:1], None, ALU.is_equal).then_inc(rel_used, 1)
                    v.wait_ge(lo_in[j], 16 * i + 16)
                    v.tensor_scalar(is_lo[:, j, :], lo[:, j, :], k.part[:, 0:1], None, ALU.is_equal).then_inc(lo_used, 1)

                def make_mask(i, j):
                    v.tensor_tensor(mask[:, j, :, 0:NT], k.lane[:, 0:NT].unsqueeze(1).to_broadcast([P, G8, NT]),
                                    k.hi_cols[:, bass.ds(i * U + G8 * j, G8)].unsqueeze(2).to_broadcast([P, G8, NT]),
                                    ALU.is_equal).then_inc(mask_ready, 1)

                def pick(i, j):
                    n = PER * i + j
                    v.wait_ge(product, n + 1)
                    v.wait_ge(mask_ready, n + 1)
                    v.tensor_tensor(picked[:, j].rearrange("p q n -> p (q n)"), k.psum[:, j, 0:G8 * WIDE],
                                    mask[:, j].rearrange("p q n -> p (q n)"), ALU.mult).then_inc(read, 1)

                def reduce(i, j):
                    n = PER * i + j
                    v.wait_ge(read, n + 1 + PER)
                    v.tensor_reduce(scores[:, bass.ds(i * U + G8 * j, G8)], picked[:, j], AX.X, ALU.add).then_inc(reduced, 1)

                pipeline(v, ITERS, PER, reduce, matrices, pick, make_mask, lags=(2, 0, 1, 0))
                v.wait_ge(reduced, PER * ITERS)


def phase_softmax(nc, k, scores):
    with ExitStack() as c:
        sb = lambda n, s, d: c.enter_context(nc.sbuf_tensor("x_" + n, s, d))
        sem = semaphores(nc, c, "x_")
        a = sb("a", [P, STEPS], F32)
        live = sb("live", [P, STEPS], F32)
        m = sb("m", [P, 8], F32)
        landed, chain, ask, told, expd = (sem(n) for n in ("landed", "chain", "ask", "told", "expd"))
        rel, src, e = k.rel_cols[:, 0:STEPS], k.src_cols[:, 0:STEPS], scores[:, 0:STEPS]
        with nc.Block() as block:
            @block.sync
            def _(sp):
                sp.dma_start(m[:, 0:1], k.small["L1_gnn_a_b"].to_broadcast([P, 1])).then_inc(landed, 16)
                sp.wait_ge(landed, 16)

            @block.vector
            def _(v):
                link = vector_chain(nc, chain, v)
                v.wait_ge(landed, 16)
                link(v.tensor_scalar(live[:], rel, 0.0, None, ALU.is_ge))
                link(v.scalar_tensor_tensor(out=live[:], in0=rel, scalar=float(P), in1=live[:], op0=ALU.is_lt, op1=ALU.mult))
                link(v.scalar_tensor_tensor(out=live[:], in0=src, scalar=float(N), in1=live[:], op0=ALU.is_lt, op1=ALU.mult))
                link(v.tensor_scalar(e, e, m[:, 0:1], None, ALU.add))
                link(v.tensor_scalar(a[:], e, 0.01, None, ALU.mult))
                link(v.tensor_tensor(e, e, a[:], ALU.max))
                link(v.tensor_tensor(e, e, live[:], ALU.mult))
                link(v.tensor_scalar(a[:], live[:], -1.0, -NEG, ALU.add, ALU.mult))
                link(v.tensor_tensor(e, e, a[:], ALU.add))
                link(v.tensor_reduce(m[:, 1:2], e, AX.X, ALU.max))
                v.sem_inc(ask, 1)
                v.wait_ge(told, 1)
                link(v.tensor_reduce(m[0:1, 2:3], k.psum[0:1, 0, 0:P], AX.X, ALU.max))
                v.sem_inc(ask, 1)
                v.wait_ge(told, 2)
                link(v.tensor_scalar(m[:, 3:4], k.psum[:, 1, 0:1], -1.0, None, ALU.mult))
                v.sem_inc(ask, 1)
                v.wait_ge(told, 3)
                link(v.reciprocal(m[:, 5:6], k.psum[:, 2, 0:1]))
                link(v.tensor_scalar(e, e, m[:, 5:6], None, ALU.mult))

            @block.scalar
            def _(act):
                act.wait_ge(ask, 3)
                nc.scalar.activation(e, e, ACT.Exp, bias=m[:, 3:4], accum_out=m[:, 4:5]).then_inc(expd, 1)

            @block.tensor
            def _(pe):
                pe.wait_ge(ask, 1)
                pe.matmul(k.psum[0:1, 0, 0:P], m[:, 1:2], k.ident[:], start=True, stop=True).then_inc(told, 1)
                pe.wait_ge(ask, 2)
                pe.matmul(k.psum[:, 1, 0:1], k.ones[0:1, :], m[0:1, 2:3], start=True, stop=True).then_inc(told, 1)
                pe.wait_ge(expd, 1)
                pe.matmul(k.psum[:, 2, 0:1], k.ones[:], m[:, 4:5], start=True, stop=True).then_inc(told, 1)


def phase_attend(nc, k, weights, H3, accs, room):
    with ExitStack() as c:
        sb = lambda n, s, d: c.enter_context(nc.sbuf_tensor("a_" + n, s, d))
        sem = semaphores(nc, c, "a_")
        rel = sb("rel", [P, GROUPS, G * P], BF16)
        out_rows = room[:, 0:U * D].rearrange("p (u d) -> p u d", d=D)
        src = room[:, U * D:2 * U * D].rearrange("p (j e) -> p j e", j=GROUPS)
        oht = sb("oht", [P, 2, G * P], BF16)
        same = sb("same", [P, 2, G, P], F32)
        col = sb("col", [P, 2, 2, G], F32)
        junk = sb("junk", [P, P], F32)
        count = sb("count", [P, 2, G], F32)
        away = sb("away", [P, 2, G], F32)
        msg = sb("msg", [P, 2, G, D], F32)
        idx = sb("idx", [P, U], I32)
        zero = sb("zero", [P, D], F32)
        rel_in = [sem(f"rel_in{n}") for n in range(GROUPS)]
        src_in = [sem(f"src_in{n}") for n in range(GROUPS)]
        acc_done = k.acc_done
        zeroed, oht_ready, same_ready, product, msg_ready, merged, rows_ready, idx_ready, rows_free, pool_turn, chain, col_ready = (
            sem(n) for n in ("zeroed", "oht_ready", "same_ready", "product", "msg_ready", "merged", "rows_ready",
                             "idx_ready", "rows_free", "pool_turn", "chain", "col_ready"))
        sp_turn = sem("sp_turn")
        rel_flat = k.rel_rows.rearrange("(o s) e -> o (s e)", o=1)
        src_flat = k.src_rows.rearrange("(o s) e -> o (s e)", o=1)
        with nc.Block() as block:
            @block.sync
            def _(sp):
                with sp.Fori(0, ITERS) as i:
                    for j in range(GROUPS):
                        at = bass.ds(sp.snap((i * U + j * G) * P), G * P)
                        sp.wait_ge(oht_ready, GROUPS * i + j + 1)
                        sp.sem_inc(sp_turn, 1)
                        sp.dma_start(rel[:, j, :], rel_flat[:, at].to_broadcast([P, G * P])).then_inc(rel_in[j], 16)
                        sp.wait_ge(same_ready, GROUPS * i + j + 1)
                        sp.sem_inc(sp_turn, 1)
                        sp.dma_start(src[:, j, :], src_flat[:, at].to_broadcast([P, G * P])).then_inc(src_in[j], 16)

            @block.vector
            def _(v):
                v.memset(zero[:], 0.0).then_inc(zeroed, 1)
                v.sem_inc(oht_ready, GROUPS)
                v.sem_inc(same_ready, GROUPS)
                with v.Fori(0, ITERS) as i:
                    for j in range(GROUPS):
                        h, n = j % 2, GROUPS * i + j
                        steps = bass.ds(i * U + G * j, G)
                        v.wait_ge(merged, n + 1)
                        v.tensor_copy(col[:, h, 0, :], weights[:, steps]).then_inc(col_ready, 1)
                        v.tensor_copy(col[:, h, 1, :], k.src_cols[:, steps]).then_inc(col_ready, 1)
                        v.wait_ge(rel_in[j], 16 * i + 16)
                        v.tensor_scalar(oht[:, h, :], rel[:, j, :], k.part[:, 0:1], None, ALU.is_equal).then_inc(oht_ready, 1)
                        v.wait_ge(src_in[j], 16 * i + 16)
                        v.wait_ge(col_ready, 2 * n + 2)
                        rows = src[:, j, :].rearrange("p (q e) -> p q e", e=P)
                        for q in range(G):
                            v.scalar_tensor_tensor(out=junk[:], in0=rows[:, q, :], scalar=col[:, h, 1, q:q + 1], in1=k.before[:],
                                                   op0=ALU.is_equal, op1=ALU.mult,
                                                   accum_out=count[:, h, q:q + 1]).then_inc(chain, 1)
                            v.wait_ge(chain, 7 * n + q + 1)
                        v.tensor_tensor(away[:, h], k.trash[:], col[:, h, 1, :], ALU.subtract).then_inc(chain, 1)
                        v.tensor_tensor(same[:, h], rows, col[:, h, 1, :].unsqueeze(2).to_broadcast([P, G, P]),
                                        ALU.is_equal).then_inc(same_ready, 1)
                        v.wait_ge(chain, 7 * n + 5)
                        v.scalar_tensor_tensor(out=away[:, h], in0=count[:, h], scalar=0.0, in1=away[:, h],
                                               op0=ALU.is_gt, op1=ALU.mult).then_inc(chain, 1)
                        v.wait_ge(chain, 7 * n + 6)
                        v.wait_ge(rows_free, n + 1)
                        v.tensor_tensor(idx[:, G * j:G * j + G], away[:, h], col[:, h, 1, :], ALU.add).then_inc(chain, 1)
                        v.wait_ge(chain, 7 * n + 7)
                        v.sem_inc(idx_ready, 1)

            @block.tensor
            def _(pe):
                pe.sem_inc(merged, 2)
                regs = {}

                def expand(i, j):
                    if j == 0:
                        regs["node"] = load_steps(nc, pe, k.ek[1], i * U, RT - 1)
                    n = GROUPS * i + j
                    pe.wait_ge(oht_ready, n + 1 + GROUPS)
                    pe.wait_ge(msg_ready, n + 1)
                    for q in range(G):
                        for part in range(3):
                            mm = pe.matmul(k.psum[:, j % 2, q * D:(q + 1) * D], oht[:, j % 2, q * P:(q + 1) * P],
                                           H3[:, bass.ds(regs["node"][G * j + q], 1), part, :],
                                           start=(part == 0), stop=(part == 2))
                    mm.then_inc(product, 1)

                def merge(i, j):
                    n = GROUPS * i + j
                    pe.wait_ge(msg_ready, n + 3)
                    pe.wait_ge(same_ready, n + 1 + GROUPS)
                    pe.wait_ge(rows_ready, n + 1)
                    for q in range(G):
                        mm = pe.matmul(k.psum[:, 2 + j % 2, q * D:(q + 1) * D], same[:, j % 2, q, :], msg[:, j % 2, q, :],
                                       start=True, stop=True)
                    mm.then_inc(merged, 1)

                pipeline(pe, ITERS, GROUPS, expand, merge)

            @block.scalar
            def _(a):
                a.sem_inc(msg_ready, 2)
                a.sem_inc(rows_ready, 2)

                def scale(i, j):
                    n = GROUPS * i + j
                    a.wait_ge(product, n + 1)
                    a.wait_ge(col_ready, 2 * n + 2)
                    a.wait_ge(merged, n + 1)
                    for q in range(G):
                        ins = nc.scalar.activation(msg[:, j % 2, q, :], k.psum[:, j % 2, q * D:(q + 1) * D], ACT.Copy,
                                                   scale=col[:, j % 2, 0, q:q + 1])
                    ins.then_inc(msg_ready, 1)

                def copy(i, j):
                    n = GROUPS * i + j
                    a.wait_ge(merged, n + 3)
                    a.wait_ge(rows_free, n + 1)
                    nc.scalar.copy(out_rows[:, G * j:G * j + G, :].rearrange("p q d -> p (q d)"),
                                   k.psum[:, 2 + j % 2, :]).then_inc(rows_ready, 1)

                pipeline(a, ITERS, GROUPS, scale, copy)

            @block.gpsimd
            def _(g):
                g.sem_inc(rows_free, GROUPS - 1)
                g.wait_ge(zeroed, 1)
                for n in range(ACCS):
                    g.dma_start(accs[n].rearrange("(t p) d -> p t d", p=P),
                                zero[:].unsqueeze(1).to_broadcast([P, AROWS // P, D])).then_inc(acc_done[n], 16)
                with g.Fori(0, ITERS) as i:
                    for u in range(U):
                        n = GROUPS * i + u // G
                        if u % G == 0:
                            g.wait_ge(idx_ready, n + 1)
                            g.wait_ge(rows_ready, n + 3)
                        g.wait_ge(acc_done[u % ACCS], 16 * ((U // ACCS) * i + u // ACCS + 1))
                        g.sem_inc(rows_free if u % G == G - 1 else pool_turn, 1)
                        g.indirect_dma_start(out=accs[u % ACCS], out_offset=bass.IndirectOffsetOnAxis(ap=idx[:, u:u + 1], axis=0),
                                             in_=out_rows[:, u, :], in_offset=None, compute_op=ALU.add
                                             ).then_inc(acc_done[u % ACCS], 16)
                for n in range(ACCS):
                    g.wait_ge(acc_done[n], 16 * (STEPS // ACCS + 1))


def phase_attend_nodes(nc, k, accs, Y, S, Z):
    with ExitStack() as c:
        sem = semaphores(nc, c, "b_")
        col = c.enter_context(nc.sbuf_tensor("b_col", [P, 3, NT], F32))
        landed = [sem(f"landed{n}") for n in range(ACCS)]
        chain, ask, rooted = sem("chain"), sem("ask"), sem("rooted")
        bufs = [Y, S, *Z]
        with nc.Block() as block:
            @block.sync
            def _(sp):
                for n in range(ACCS):
                    sp.dma_start(bufs[n], accs[n][0:NP, :].rearrange("(t p) d -> p t d", p=P)).then_inc(landed[n], 16)

            @block.vector
            def _(v):
                link = vector_chain(nc, chain, v)
                for n in range(ACCS):
                    v.wait_ge(landed[n], 16)
                    link(v.tensor_tensor(Y, Y, bufs[n] if n else k.X[:], ALU.add))
                layer_norm(nc, link, v, Y, k.X[:], col, col[:, 2, :], ask, rooted, 1)

            @block.scalar
            def _(a):
                a.wait_ge(ask, 1)
                nc.scalar.activation(col[:, 2, :], col[:, 1, :], ACT.Sqrt).then_inc(rooted, 1)


def phase_split(nc, k, name, x, parts, scale):
    with ExitStack() as c:
        sem = semaphores(nc, c, name)
        chain = sem("chain")
        block = c.enter_context(nc.Block())

        @block.vector
        def _(v):
            link = vector_chain(nc, chain, v)
            if scale != 1.0:
                link(v.tensor_scalar(x, x, scale, None, ALU.mult))
            split3(link, v, parts, x)


def phase_heads_edges(nc, k, table, Q3, agg, AW, room, before):
    with ExitStack() as c:
        sb = lambda n, s, d: c.enter_context(nc.sbuf_tensor("h_" + n, s, d))
        sem = semaphores(nc, c, "h_")
        idx = sb("idx", [P, U], I32)
        rows = room[:, 0:U * 2 * D].rearrange("p (u d) -> p u d", d=2 * D)
        rel = sb("rel", [P, GROUPS, G * P], BF16)
        oht = sb("oht", [P, 2, G * P], BF16)
        oh = sb("oh", [P, 2, G, P], F32)
        kq = sb("kq", [P, G, D], F32)
        score = sb("score", [P, 2, G, HEADS], F32)
        msg = sb("msg", [P, 2, G, AW], F32)
        rel_in = [sem(f"rel_in{n}") for n in range(GROUPS)]
        row_in = k.row_in
        idx_ready, pool_turn, sp_turn = sem("idx_ready"), sem("pool_turn"), sem("sp_turn")
        oht_ready, oh_ready, product, kq_ready, clipped, weighed, msg_ready, spread, added, zero, chain = (
            sem(n) for n in ("oht_ready", "oh_ready", "product", "kq_ready", "clipped", "weighed", "msg_ready", "spread",
                             "added", "zero", "chain"))
        rel_flat = k.rel_rows.rearrange("(o s) e -> o (s e)", o=1)
        sums = lambda j, q: k.psum[:, 2 + 2 * (j % 2) + q // 2, (q % 2) * AW:(q % 2 + 1) * AW]
        with nc.Block() as block:
            @block.sync
            def _(sp):
                with sp.Fori(0, ITERS) as i:
                    for j in range(GROUPS):
                        at = bass.ds(sp.snap((i * U + j * G) * P), G * P)
                        sp.wait_ge(oht_ready, GROUPS * i + j + 1)
                        sp.sem_inc(sp_turn, 1)
                        sp.dma_start(rel[:, j, :], rel_flat[:, at].to_broadcast([P, G * P])).then_inc(rel_in[j], 16)

            @block.gpsimd
            def _(g):
                with g.Fori(0, ITERS) as i:
                    for u in range(U):
                        if u % G == 0:
                            g.wait_ge(idx_ready, GROUPS * i + u // G + 1)
                            g.wait_ge(msg_ready, GROUPS * i + u // G + 1)
                            g.sem_inc(pool_turn, 1)
                        g.indirect_dma_start(out=rows[:, u, :], out_offset=None, in_=table,
                                             in_offset=bass.IndirectOffsetOnAxis(ap=idx[:, u:u + 1], axis=0)
                                             ).then_inc(row_in[u], 16)

            @block.tensor
            def _(pe):
                regs = {}

                def expand(i, j):
                    if j == 0:
                        regs["node"] = load_steps(nc, pe, k.ek[1], i * U, RT - 1)
                    n = GROUPS * i + j
                    pe.wait_ge(oht_ready, n + 1 + GROUPS)
                    pe.wait_ge(kq_ready, n + 1)
                    for q in range(G):
                        for part in range(3):
                            mm = pe.matmul(k.psum[:, j % 2, q * D:(q + 1) * D], oht[:, j % 2, q * P:(q + 1) * P],
                                           Q3[:, bass.ds(regs["node"][G * j + q], 1), part, :],
                                           start=(part == 0), stop=(part == 2))
                    mm.then_inc(product, 1)

                def sum_into_nodes(i, j):
                    n = GROUPS * i + j
                    pe.wait_ge(msg_ready, n + 1 + GROUPS)
                    pe.wait_ge(oh_ready, n + 1)
                    pe.wait_ge(added, G * n + G)
                    for q in range(G):
                        mm = pe.matmul(sums(j, q), oh[:, j % 2, q, :], msg[:, j % 2, q, :], start=True, stop=True)
                    mm.then_inc(spread, 1)

                pipeline(pe, ITERS, GROUPS, expand, sum_into_nodes, lags=(0, 2))

            @block.scalar
            def _(a):
                with a.Fori(0, ITERS) as i:
                    for j in range(GROUPS):
                        n = GROUPS * i + j
                        a.wait_ge(clipped, n + 1)
                        a.wait_ge(spread, n + 1)
                        nc.scalar.activation(msg[:, j % 2, :, D:D + HEADS], score[:, j % 2], ACT.Exp).then_inc(weighed, 1)

            @block.vector
            def _(v):
                v.memset(agg, 0.0).then_inc(zero, 1)
                v.memset(msg[:, :, :, AW - 1:AW], 1.0).then_inc(zero, 1)
                v.wait_ge(zero, 2)
                v.sem_inc(oht_ready, GROUPS)
                v.sem_inc(kq_ready, 2)
                v.sem_inc(msg_ready, GROUPS)
                v.sem_inc(spread, 2)
                v.sem_inc(added, 2 * G)

                def stage(i, j):
                    v.tensor_copy(idx[:, G * j:G * j + G], k.src_idx[:, bass.ds(i * U + G * j, G)]).then_inc(idx_ready, 1)

                for j in range(GROUPS):
                    stage(0, j)

                def expand_matrix(i, j):
                    v.wait_ge(rel_in[j], 16 * i + 16)
                    v.tensor_scalar(oht[:, j % 2, :], rel[:, j, :], k.part[:, 0:1], None, ALU.is_equal).then_inc(oht_ready, 1)

                def sum_matrix(i, j):
                    v.wait_ge(spread, GROUPS * i + j + 1)
                    v.tensor_tensor(oh[:, j % 2], k.lane[:].unsqueeze(1).to_broadcast([P, G, P]),
                                    k.rel_cols[:, bass.ds(i * U + G * j, G)].unsqueeze(2).to_broadcast([P, G, P]),
                                    ALU.is_equal).then_inc(oh_ready, 1)

                def key_times_query(i, j):
                    v.wait_ge(product, GROUPS * i + j + 1)
                    for q in range(G):
                        v.wait_ge(row_in[G * j + q], 16 * i + 16 * (before + 1))
                    v.tensor_tensor(kq[:], k.psum[:, j % 2, :].rearrange("p (q d) -> p q d", d=D),
                                    rows[:, G * j:G * j + G, 0:D], ALU.mult).then_inc(kq_ready, 1)

                def sum_of_head(i, j):
                    n = GROUPS * i + j
                    v.wait_ge(kq_ready, n + 3)
                    v.tensor_reduce(score[:, j % 2].rearrange("p q h -> p (q h)"),
                                    kq[:].rearrange("p q (h e) -> p (q h) e", e=HD), AX.X, ALU.add).then_inc(chain, 1)

                def clip(i, j):
                    v.wait_ge(chain, GROUPS * i + j + 1)
                    v.tensor_scalar(score[:, j % 2], score[:, j % 2], -5.0, 5.0, ALU.max, ALU.min).then_inc(clipped, 1)

                def messages(i, j):
                    v.wait_ge(weighed, GROUPS * i + j + 1)
                    v.tensor_tensor(msg[:, j % 2, :, 0:D].rearrange("p q (h e) -> p q h e", e=HD),
                                    rows[:, G * j:G * j + G, D:2 * D].rearrange("p q (h e) -> p q h e", e=HD),
                                    msg[:, j % 2, :, D:D + HEADS].unsqueeze(3).to_broadcast([P, G, HEADS, HD]),
                                    ALU.mult).then_inc(msg_ready, 1)
                    stage(i + 1, j)

                regs = {}

                def add(q):
                    def add_one(i, j):
                        if j == 0 and q == 0:
                            regs["node"] = load_steps(nc, v, k.ek[1], i * U, RT - 1)
                        n = GROUPS * i + j
                        if q == 0:
                            v.wait_ge(spread, n + 3)
                        t = bass.ds(regs["node"][G * j + q], 1)
                        v.wait_ge(added, G * n + q + 2 * G)
                        v.tensor_tensor(agg[:, t, :], agg[:, t, :], sums(j, q).unsqueeze(1), ALU.add).then_inc(added, 1)
                    return add_one

                pipeline(v, ITERS, GROUPS, expand_matrix, add(0), key_times_query, add(1), sum_of_head, add(2), clip,
                         messages, add(3), sum_matrix, lags=(0, 4, 1, 4, 1, 4, 1, 2, 4, 1), loads=4)


def phase_heads_nodes(nc, k, agg, AW, Y, S):
    with ExitStack() as c:
        sem = semaphores(nc, c, "g_")
        col = c.enter_context(nc.sbuf_tensor("g_col", [P, 3, NT], F32))
        chain, ask, rooted = sem("chain"), sem("ask"), sem("rooted")
        inv = S.rearrange("p t d -> p (t d)")[:, 0:NT * HEADS].rearrange("p (t h) -> p t h", h=HEADS)
        with nc.Block() as block:
            @block.vector
            def _(v):
                link = vector_chain(nc, chain, v)
                link(v.tensor_copy(k.degree[:], agg[:, :, AW - 1]))
                link(v.tensor_scalar(inv, agg[:, :, D:D + HEADS], 1e-30, None, ALU.max))
                link(v.reciprocal(inv, inv))
                link(v.tensor_tensor(Y.rearrange("p t (h e) -> p t h e", e=HD),
                                     agg[:, :, 0:D].rearrange("p t (h e) -> p t h e", e=HD),
                                     inv.unsqueeze(3).to_broadcast([P, NT, HEADS, HD]), ALU.mult))
                link(v.tensor_tensor(Y, Y, k.X[:], ALU.add))
                layer_norm(nc, link, v, Y, k.X[:], col, col[:, 2, :], ask, rooted, 1)

            @block.scalar
            def _(a):
                a.wait_ge(ask, 1)
                nc.scalar.activation(col[:, 2, :], col[:, 1, :], ACT.Sqrt).then_inc(rooted, 1)


def phase_relation_edges(nc, k, table, D3, agg, before):
    with ExitStack() as c:
        sb = lambda n, s, d: c.enter_context(nc.sbuf_tensor("r_" + n, s, d))
        sem = semaphores(nc, c, "r_")
        room = k.X[:].rearrange("p t d -> p (t d)")
        rows = room[:, 0:U * HID].rearrange("p (u d) -> p u d", d=HID)
        msg = room[:, U * HID:U * HID + 2 * G * HID].rearrange("p (h q d) -> p h q d", h=2, d=HID)
        idx = sb("idx", [P, U], I32)
        ea = sb("ea", [P, U, P], F32)
        rel = sb("rel", [P, GROUPS, G * P], BF16)
        oht = sb("oht", [P, 2, G * P], BF16)
        oh = sb("oh", [P, 2, G, P], F32)
        ea_in = [sem(f"ea_in{u}") for u in range(U)]
        rel_in = [sem(f"rel_in{n}") for n in range(GROUPS)]
        row_in = k.row_in
        idx_ready, pool_turn, sp_turn = sem("idx_ready"), sem("pool_turn"), sem("sp_turn")
        oht_ready, oh_ready, product, summed, msg_ready, spread, added, zero = (
            sem(n) for n in ("oht_ready", "oh_ready", "product", "summed", "msg_ready", "spread", "added", "zero"))
        rel_flat = k.rel_rows.rearrange("(o s) e -> o (s e)", o=1)
        hidden = lambda j, q: k.psum[:, 2 * (j % 2) + q // 2, (q % 2) * HID:(q % 2 + 1) * HID]
        sums = lambda j, q: k.psum[:, 4 + 2 * (j % 2) + q // 2, (q % 2) * HID:(q % 2 + 1) * HID]
        with nc.Block() as block:
            @block.sync
            def _(sp):
                with sp.Fori(0, ITERS) as i:
                    tile = load_steps(nc, sp, k.ek[0], i * U, ET - 1)
                    for u in range(U):
                        j = u // G
                        if u % G == 0:
                            at = bass.ds(sp.snap((i * U + u) * P), G * P)
                            sp.wait_ge(oht_ready, GROUPS * i + j + 1)
                            sp.sem_inc(sp_turn, 1)
                            sp.dma_start(rel[:, j, :], rel_flat[:, at].to_broadcast([P, G * P])).then_inc(rel_in[j], 16)
                            sp.wait_ge(product, GROUPS * i + j + 1)
                            sp.sem_inc(sp_turn, 1)
                        sp.dma_start(ea[:, u, :], k.ea_t[:, bass.ds(tile[u] * P, P)]).then_inc(ea_in[u], 16)

            @block.gpsimd
            def _(g):
                with g.Fori(0, ITERS) as i:
                    for u in range(U):
                        if u % G == 0:
                            g.wait_ge(idx_ready, GROUPS * i + u // G + 1)
                            g.wait_ge(summed, 2 * (GROUPS * i + u // G) + 2)
                            g.sem_inc(pool_turn, 1)
                        g.indirect_dma_start(out=rows[:, u, :], out_offset=None, in_=table,
                                             in_offset=bass.IndirectOffsetOnAxis(ap=idx[:, u:u + 1], axis=0)
                                             ).then_inc(row_in[u], 16)

            @block.tensor
            def _(pe):
                pe.sem_inc(product, GROUPS)
                regs = {}

                def hidden_product(i, j):
                    if j == 0:
                        regs["node"] = load_steps(nc, pe, k.ek[1], i * U, RT - 1)
                    n = GROUPS * i + j
                    pe.wait_ge(summed, 2 * n + 6)
                    pe.wait_ge(oht_ready, n + 1 + GROUPS)
                    for q in range(G):
                        pe.wait_ge(ea_in[G * j + q], 16 * i + 16)
                        pe.matmul(hidden(j, q), ea[:, G * j + q, :], k.W[:, 0:HID], start=True, stop=False)
                        for part in range(3):
                            mm = pe.matmul(hidden(j, q), oht[:, j % 2, q * P:(q + 1) * P],
                                           D3[:, bass.ds(regs["node"][G * j + q], 1), part, :],
                                           start=False, stop=(part == 2))
                        if q == G - 1:
                            mm.then_inc(product, 1)

                def sum_into_nodes(i, j):
                    n = GROUPS * i + j
                    pe.wait_ge(msg_ready, n + 1)
                    pe.wait_ge(oh_ready, n + 1)
                    pe.wait_ge(added, G * n + G)
                    for q in range(G):
                        mm = pe.matmul(sums(j, q), oh[:, j % 2, q, :], msg[:, j % 2, q, :], start=True, stop=True)
                    mm.then_inc(spread, 1)

                pipeline(pe, ITERS, GROUPS, hidden_product, sum_into_nodes, lags=(0, 2))

            @block.scalar
            def _(a):
                with a.Fori(0, ITERS) as i:
                    for j in range(GROUPS):
                        a.wait_ge(summed, 2 * (GROUPS * i + j) + 10)
                        nc.scalar.activation(msg[:, j % 2], msg[:, j % 2], ACT.Relu).then_inc(msg_ready, 1)

            @block.vector
            def _(v):
                v.memset(agg, 0.0).then_inc(zero, 1)
                v.wait_ge(zero, 1)
                v.sem_inc(oht_ready, GROUPS)
                v.sem_inc(summed, 2 * GROUPS)
                v.sem_inc(spread, 2)
                v.sem_inc(added, 2 * G)

                def stage(i, j):
                    v.tensor_copy(idx[:, G * j:G * j + G], k.src_idx[:, bass.ds(i * U + G * j, G)]).then_inc(idx_ready, 1)

                for j in range(GROUPS):
                    stage(0, j)

                def expand_matrix(i, j):
                    v.wait_ge(rel_in[j], 16 * i + 16)
                    v.tensor_scalar(oht[:, j % 2, :], rel[:, j, :], k.part[:, 0:1], None, ALU.is_equal).then_inc(oht_ready, 1)

                def sum_matrix(i, j):
                    v.wait_ge(spread, GROUPS * i + j + 1)
                    v.tensor_tensor(oh[:, j % 2], k.lane[:].unsqueeze(1).to_broadcast([P, G, P]),
                                    k.rel_cols[:, bass.ds(i * U + G * j, G)].unsqueeze(2).to_broadcast([P, G, P]),
                                    ALU.is_equal).then_inc(oh_ready, 1)

                def add_rows(h):
                    def add_half(i, j):
                        if h == 0:
                            v.wait_ge(product, GROUPS * i + j + 1 + GROUPS)
                        for q in (2 * h, 2 * h + 1):
                            v.wait_ge(row_in[G * j + q], 16 * i + 16 * (before + 1))
                        v.tensor_tensor(msg[:, j % 2, 2 * h:2 * h + 2, :].rearrange("p q d -> p (q d)"),
                                        k.psum[:, 2 * (j % 2) + h, :],
                                        rows[:, G * j + 2 * h:G * j + 2 * h + 2, :].rearrange("p q d -> p (q d)"),
                                        ALU.add).then_inc(summed, 1)
                        if h == 1:
                            stage(i + 1, j)
                    return add_half

                regs = {}

                def add_sums(q):
                    def add_one(i, j):
                        if j == 0 and q == 0:
                            regs["node"] = load_steps(nc, v, k.ek[1], i * U, RT - 1)
                        n = GROUPS * i + j
                        if q == 0:
                            v.wait_ge(spread, n + 3)
                        t = bass.ds(regs["node"][G * j + q], 1)
                        v.wait_ge(added, G * n + q + 2 * G)
                        v.tensor_tensor(agg[:, t, :], agg[:, t, :], sums(j, q).unsqueeze(1), ALU.add).then_inc(added, 1)
                    return add_one

                pipeline(v, ITERS, GROUPS, expand_matrix, add_sums(0), sum_matrix, add_sums(1), add_rows(0), add_sums(2),
                         add_rows(1), add_sums(3), lags=(0, 3, 1, 3, 1, 3, 1, 3), loads=3)


def phase_update_nodes(nc, k, name, ap, agg, Y):
    with ExitStack() as c:
        sb = lambda n, s, d: c.enter_context(nc.sbuf_tensor("u_" + n, s, d))
        sem = semaphores(nc, c, "u_")
        w_in = sb("w_in", [P, 3, HID], F32)
        b_in = sb("b_in", [P, HID], F32)
        re2t = sb("re2t", [P, HID], F32)
        re_b2 = sb("re_b2", [P, 1], F32)
        w_deg = sb("w_deg", [1, HID], F32)
        w_out = sb("w_out", [P, 2, D], F32)
        b_hid = sb("b_hid", [P, 2], F32)
        tile = sb("tile", [P, 2, 3 * P], F32)
        deg = sb("deg", [P, 2], F32)
        tile_t = sb("tile_t", [P, 2, 3 * P], F32)
        deg_t = sb("deg_t", [1, 2, P], F32)
        hid = sb("hid", [P, 2, 2, P], F32)
        landed, folded, fold_copied, staged, turned, copied, hidden, active, product, added, chain = (
            sem(n) for n in ("landed", "folded", "fold_copied", "staged", "turned", "copied", "hidden", "active", "product",
                             "added", "chain"))
        HALF = NT // 2
        with nc.Block() as block:
            @block.sync
            def _(sp):
                with nc.allow_non_contiguous_dma(reason="bias vectors onto the partitions"):
                    sp.dma_start(w_in[:, 0, :], ap["L3_gnn_ea_w1"][0:D, :]).then_inc(landed, 16)
                    sp.dma_start(b_in[:], ap["L3_gnn_ea_w1"][D:2 * D, :]).then_inc(landed, 16)
                    sp.dma_start(re2t[:], ap["L3_gnn_re_w2t"]).then_inc(landed, 16)
                    sp.dma_start(re_b2[:], ap["L3_gnn_re_b2"].rearrange("o d -> d o")).then_inc(landed, 16)
                    for h in range(2):
                        sp.dma_start(w_out[:, h, :], ap["L3_gnn_ea_w2"][h * P:(h + 1) * P, :]).then_inc(landed, 16)
                        sp.dma_start(b_hid[:, h:h + 1], ap["L3_gnn_ea_b1"][:, h * P:(h + 1) * P].rearrange("o d -> d o")).then_inc(landed, 16)
                    sp.dma_start(k.bias[:, 0:D], ap["L3_gnn_ea_b2"].to_broadcast([P, D])).then_inc(landed, 16)
                sp.wait_ge(landed, 144)

            @block.tensor
            def _(pe):
                pe.sem_inc(product, 2)
                pe.wait_ge(landed, 144)
                for h in range(2):
                    pe.matmul(k.psum[:, 6, h * HID:(h + 1) * HID], re2t[:, h * P:(h + 1) * P], b_in[:], start=True, stop=True)
                pe.matmul(k.psum[0:1, 7, 0:HID], re_b2[:], b_in[:], start=True, stop=True).then_inc(folded, 1)

                def turn(i, b):
                    n = 2 * i + b
                    pe.wait_ge(staged, 3 * n + 3)
                    pe.wait_ge(copied, 2 * n + 2)
                    for f in range(3):
                        pe.transpose(k.psum[:, b, f * P:(f + 1) * P], tile[:, b, f * P:(f + 1) * P], k.ident[:])
                    pe.matmul(k.psum[0:1, b, 3 * P:4 * P], deg[:, b:b + 1], k.ident[:], start=True, stop=True).then_inc(turned, 1)

                def hide(i, b):
                    n = 2 * i + b
                    pe.wait_ge(copied, 2 * n + 6)
                    pe.wait_ge(fold_copied, 2)
                    pe.wait_ge(active, n + 1)
                    for h in range(2):
                        half = slice(h * P, (h + 1) * P)
                        for f in range(3):
                            pe.matmul(k.psum[:, 2 + b, half], w_in[:, f, half], tile_t[:, b, f * P:(f + 1) * P],
                                      start=(f == 0), stop=False)
                        mm = pe.matmul(k.psum[:, 2 + b, half], w_deg[0:1, half], deg_t[0:1, b, :], start=False, stop=True)
                    mm.then_inc(hidden, 1)

                def out(i, b):
                    n = 2 * i + b
                    pe.wait_ge(active, n + 3)
                    pe.wait_ge(added, n + 1)
                    pe.matmul(k.psum[:, 4 + b, 0:D], hid[:, b, 0, :], w_out[:, 0, :], start=True, stop=False)
                    pe.matmul(k.psum[:, 4 + b, 0:D], hid[:, b, 1, :], w_out[:, 1, :], start=False, stop=True).then_inc(product, 1)

                pipeline(pe, HALF, 2, turn, hide, out)

            @block.scalar
            def _(a):
                a.sem_inc(active, 2)
                a.wait_ge(landed, 144)

                def activate(i, b):
                    n = 2 * i + b
                    a.wait_ge(hidden, n + 1)
                    a.wait_ge(product, n + 1)
                    for h in range(2):
                        ins = nc.scalar.activation(hid[:, b, h, :], k.psum[:, 2 + b, h * P:(h + 1) * P], ACT.Relu,
                                                   bias=b_hid[:, h:h + 1])
                    ins.then_inc(active, 1)

                with a.Fori(0, HALF) as i:
                    for b in range(2):
                        activate(i, b)

            @block.vector
            def _(v):
                v.wait_ge(folded, 1)
                v.tensor_copy(w_in[:, 1:3, :], k.psum[:, 6, :].rearrange("p (h d) -> p h d", h=2)).then_inc(fold_copied, 1)
                v.tensor_copy(w_deg[:], k.psum[0:1, 7, 0:HID]).then_inc(fold_copied, 1)
                v.sem_inc(copied, 4)
                v.sem_inc(added, 2)

                def stage(i, b):
                    t = bass.ds(2 * i + b, 1)
                    v.tensor_copy(tile[:, b:b + 1, 0:P], k.X[:, t, :]).then_inc(staged, 1)
                    v.tensor_copy(tile[:, b:b + 1, P:3 * P], agg[:, t, :]).then_inc(staged, 1)
                    v.tensor_copy(deg[:, b:b + 1], k.degree[:, t]).then_inc(staged, 1)

                def copy(i, b):
                    n = 2 * i + b
                    v.wait_ge(turned, n + 1)
                    v.tensor_copy(tile_t[:, b, :], k.psum[:, b, 0:3 * P]).then_inc(copied, 1)
                    v.tensor_copy(deg_t[0:1, b, :], k.psum[0:1, b, 3 * P:4 * P]).then_inc(copied, 1)

                def add(i, b):
                    v.wait_ge(product, 2 * i + b + 3)
                    t = bass.ds(2 * i + b, 1)
                    v.tensor_tensor(Y[:, t, :], k.psum[:, 4 + b:5 + b, 0:D], k.bias[:, 0:D].unsqueeze(1), ALU.add).then_inc(added, 1)

                pipeline(v, HALF, 2, stage, copy, add)


def phase_last_norm(nc, k, Y, out):
    with ExitStack() as c:
        sem = semaphores(nc, c, "z_")
        col = c.enter_context(nc.sbuf_tensor("z_col", [P, 3, NT], F32))
        chain, ask, rooted, done, stored = sem("chain"), sem("ask"), sem("rooted"), sem("done"), sem("stored")
        with nc.Block() as block:
            @block.vector
            def _(v):
                link = vector_chain(nc, chain, v)
                link(v.tensor_tensor(Y, Y, k.X[:], ALU.add))
                layer_norm(nc, link, v, Y, k.X[:], col, col[:, 2, :], ask, rooted, 1)
                v.sem_inc(done, 1)

            @block.scalar
            def _(a):
                a.wait_ge(ask, 1)
                nc.scalar.activation(col[:, 2, :], col[:, 1, :], ACT.Sqrt).then_inc(rooted, 1)

            @block.sync
            def _(sp):
                sp.wait_ge(done, 1)
                full = N // P
                sp.dma_start(out[0:full * P, :].rearrange("(t p) d -> p t d", p=P), k.X[:, 0:full, :]).then_inc(stored, 16)
                sp.dma_start(out[full * P:N, :], k.X[0:N - full * P, full, :]).then_inc(stored, 16)
                sp.wait_ge(stored, 32)


TRANSPOSED = {"L0_gnn_w1t": "L0_gnn_w1", "L0_gnn_wet": "L0_gnn_we", "L3_gnn_re_w2t": "L3_gnn_re_w2"}
AS_THEY_ARE = ("L1_gnn_W_w", "L2_gnn_Wq", "L2_gnn_Wk", "L2_gnn_Wv", "L3_gnn_re_w1", "L3_gnn_ea_w1", "L3_gnn_ea_w2")
ROWS = ("L0_gnn_b1", "L0_gnn_be", "L0_gnn_eps", "L0_gnn_gn_weight", "L0_gnn_gn_bias", "L0_gnn_gn_mean_scale",
        "L1_gnn_W_b", "L1_gnn_a_w", "L1_gnn_a_b", "L2_gnn_bq", "L2_gnn_bk", "L2_gnn_bv", "L3_gnn_re_b1",
        "L3_gnn_re_b2", "L3_gnn_ea_b1", "L3_gnn_ea_b2")


def load(nc, name, pairs):
    with ExitStack() as c:
        landed = semaphores(nc, c, name)("landed")
        block = c.enter_context(nc.Block())

        @block.sync
        def _(sp):
            for to, of in pairs:
                sp.dma_start(to, of).then_inc(landed, 16)
            sp.wait_ge(landed, 16 * len(pairs))


def clear(nc, what):
    with ExitStack() as c:
        cleared = semaphores(nc, c, "clear_")("cleared")
        block = c.enter_context(nc.Block())

        @block.vector
        def _(v):
            v.memset(what, 0.0).then_inc(cleared, 1)
            v.wait_ge(cleared, 1)


def build(nc, ap, out):
    k = Kit()
    k.small = ap
    k.ea_t, k.src, k.dst = ap["ea_t"], ap["src"], ap["dst"]
    dram = lambda n, s, d: nc.dram_tensor(n, s, d, kind="Internal").ap()
    k.row_dram = dram("row_dram", (1, 2 * ET), F32)
    k.ek_dram = dram("ek_dram", (2, ST), I32)
    k.rel_rows = dram("rel_rows", (ST, P), BF16)
    k.src_rows = dram("src_rows", (ST, P), F32)
    k.lo_rows = dram("lo_rows", (ST, P), BF16)
    table0 = dram("table0", (NP, D), F32)
    table_kv = dram("table_kv", (NP, 2 * D), F32)
    table_ps = dram("table_ps", (NP, HID), F32)
    x_dram = dram("x_dram", (NP, D), F32)
    accs = [dram(f"acc{n}", (AROWS, D), F32) for n in range(ACCS)]
    tiled = lambda t: t.rearrange("(t p) d -> p t d", p=P)
    with ExitStack() as c:
        sb = lambda n, s, d: c.enter_context(nc.sbuf_tensor(n, s, d))
        k.psum = c.enter_context(nc.psum_tensor("psum", [P, 8, 512], F32))
        k.lane_i, k.part_i = sb("lane_i", [P, P], I32), sb("part_i", [P, 1], I32)
        k.trash_i, k.trash = sb("trash_i", [P, G], I32), sb("trash", [P, G], F32)
        k.lane, k.part, k.one = sb("lane", [P, P], F32), sb("part", [P, 1], F32), sb("one", [P, 1], F32)
        k.ident, k.before, k.ones = sb("ident", [P, P], F32), sb("before", [P, P], F32), sb("ones", [P, P], F32)
        k.degree = sb("degree", [P, NT], F32)
        k.is_node = sb("is_node", [P, NT - RT + 1], F32)
        k.rel_cols, k.src_cols, k.src_idx = sb("rel_cols", [P, ST], F32), sb("src_cols", [P, ST], F32), sb("src_idx", [P, ST], I32)
        k.hi_cols = sb("hi_cols", [P, ST], F32)
        k.ek = [sb("edge_tile", [1, ST], I32), sb("node_tile", [1, ST], I32)]
        k.W, k.bias = sb("W", [P, 512], F32), sb("bias", [P, 512], F32)
        k.row_in = [c.enter_context(nc.semaphore(f"row_in{u}")) for u in range(U)]
        k.acc_done = [c.enter_context(nc.semaphore(f"acc_done{n}")) for n in range(ACCS)]
        k.gathered = c.enter_context(nc.semaphore("gathered"))
        k.turn_free = c.enter_context(nc.semaphore("turn_free"))
        phase_tables(nc, k)
        k.X = sb("X", [P, NT, D], F32)
        R1 = sb("R1", [P, NT, 256], F32)
        R3 = sb("R3", [P, NT * 3 * 256], BF16)
        r1 = R1[:].rearrange("p t d -> p (t d)")
        r3 = R3[:].bitcast(F32)
        half1 = lambda b: r1[:, b * NT * D:(b + 1) * NT * D].rearrange("p (t d) -> p t d", d=D)
        half3 = lambda b: r3[:, b * NT * D:(b + 1) * NT * D].rearrange("p (t d) -> p t d", d=D)
        tile1 = lambda n: ap[n].to_broadcast([P, ap[n].shape[1]])

        load(nc, "ld_x", [(k.X[:], tiled(ap["x"])), (k.W[:, 0:D], ap["L0_gnn_w1t"]), (k.bias[:, 0:D], tile1("L0_gnn_b1"))])
        H = half3(0)
        phase_linear(nc, k, "l0", k.X[:], k.W[:, 0:D], D, k.bias[:, 0:D], H)
        phase_table0(nc, k, H, half1(0), tiled(table0))
        agg = half1(0)
        phase_conv_edges(nc, k, table0, agg, 0)
        phase_conv_nodes(nc, k, H, agg, half1(1))

        load(nc, "ld_1", [(k.W[:, 0:D], ap["L1_gnn_W_w"]), (k.bias[:, 0:D], tile1("L1_gnn_W_b"))])
        phase_linear(nc, k, "l1", k.X[:], k.W[:, 0:D], D, k.bias[:, 0:D], half1(0))
        H3 = R3[:, 0:NT * 3 * D].rearrange("p (t n d) -> p t n d", n=3, d=D)
        with ExitStack() as c1:
            k.src_score = c1.enter_context(nc.sbuf_tensor("src_score", [P, NT, 3], BF16))
            k.dst_score = c1.enter_context(nc.sbuf_tensor("dst_score", [P, NT, 3], BF16))
            scores = r3[:, 3 * NT * D // 2:][:, 0:ST]
            load(nc, "ld_a", [(k.bias[:, 0:2 * D], tile1("L1_gnn_a_w"))])
            phase_scores_nodes(nc, k, half1(0), half1(1), H3)
            phase_scores_edges(nc, k, scores)
            phase_softmax(nc, k, scores)
        phase_attend(nc, k, scores, H3, accs, r1)
        phase_attend_nodes(nc, k, accs, half1(0), half1(1), (half3(0), half3(1)))

        load(nc, "ld_2", [(k.W[:, 0:D], ap["L2_gnn_Wk"]), (k.W[:, D:2 * D], ap["L2_gnn_Wv"]), (k.W[:, 2 * D:3 * D], ap["L2_gnn_Wq"]),
                          (k.bias[:, 0:D], tile1("L2_gnn_bk")), (k.bias[:, D:2 * D], tile1("L2_gnn_bv")),
                          (k.bias[:, 2 * D:3 * D], tile1("L2_gnn_bq"))])
        phase_linear(nc, k, "l2", k.X[:], k.W[:, 0:2 * D], 2 * D, k.bias[:, 0:2 * D], R1[:])
        load(nc, "st_2", [(tiled(table_kv), R1[:])])
        phase_linear(nc, k, "l3", k.X[:], k.W[:, 2 * D:3 * D], D, k.bias[:, 2 * D:3 * D], half1(0))
        phase_split(nc, k, "q_split", half1(0), H3, HD ** -0.5)
        AW = D + HEADS + 1
        agg2 = r1[:, 0:NT * AW].rearrange("p (t w) -> p t w", w=AW)
        phase_heads_edges(nc, k, table_kv, H3, agg2, AW, r3[:, 3 * NT * D // 2:], ITERS)
        phase_heads_nodes(nc, k, agg2, AW, half3(0), half3(1))

        load(nc, "ld_3", [(k.W[:, 0:HID], ap["L3_gnn_re_w1"][0:D, :]), (k.W[:, HID:2 * HID], ap["L3_gnn_re_w1"][D:2 * D, :]),
                          (k.bias[:, HID:2 * HID], tile1("L3_gnn_re_b1")), (tiled(x_dram), k.X[:])])
        clear(nc, k.bias[:, 0:HID])
        phase_linear(nc, k, "l4", k.X[:], k.W[:, 0:HID], HID, k.bias[:, 0:HID], R1[:])
        load(nc, "st_3", [(tiled(table_ps), R1[:])])
        phase_linear(nc, k, "l5", k.X[:], k.W[:, HID:2 * HID], HID, k.bias[:, HID:2 * HID], R1[:])
        D3 = R3[:].rearrange("p (t n d) -> p t n d", n=3, d=HID)
        phase_split(nc, k, "d_split", R1[:], D3, 1.0)
        load(nc, "ld_4", [(k.W[:, 0:HID], ap["L3_gnn_re_w1"][2 * D:3 * D, :])])
        phase_relation_edges(nc, k, table_ps, D3, R1[:], 2 * ITERS)
        load(nc, "ld_5", [(k.X[:], tiled(x_dram))])
        phase_update_nodes(nc, k, "u", ap, R1[:], half3(0))
        phase_last_norm(nc, k, half3(0), out)


def layout(inputs):
    x = np.zeros((NP, D), np.float32)
    x[:N] = inputs["x"]
    ea_t = np.zeros((D, EP), np.float32)
    ea_t[:, :E] = np.asarray(inputs["edge_attr_128"]).T
    arrays = {"x": x, "ea_t": ea_t}
    for name in ("src", "dst"):
        padded = np.full((EP,), PAD_NODE, np.int32)
        padded[:E] = inputs[name]
        arrays[name] = padded.reshape(ET, P)
    for to, of in TRANSPOSED.items():
        arrays[to] = np.ascontiguousarray(np.asarray(inputs[of]).T)
    for name in AS_THEY_ARE:
        arrays[name] = np.ascontiguousarray(inputs[name])
    for name in ROWS:
        arrays[name] = np.asarray(inputs[name]).reshape(1, -1)
    return arrays


def kernel(**inputs):
    import concourse.bacc as bacc
    from concourse.bass_utils import run_bass_kernel_spmd

    arrays = layout(inputs)
    nc = bacc.Bacc("TRN2", target_bir_lowering=False, num_devices=1)
    ap = {name: nc.dram_tensor("in_" + name, a.shape, mybir.dt.from_np(a.dtype), kind="ExternalInput").ap()
          for name, a in arrays.items()}
    out = nc.dram_tensor("out", (N, D), F32, kind="ExternalOutput").ap()
    build(nc, ap, out)
    r = run_bass_kernel_spmd(nc, [{"in_" + name: a for name, a in arrays.items()}], core_ids=[0])
    return r.results[0]["out"]
```

```python
from contextlib import ExitStack

import numpy as np

import concourse.bass as bass
from concourse import mybir
from concourse.alu_op_type import AluOpType as ALU

F32 = mybir.dt.float32
BF16 = mybir.dt.bfloat16
I32 = mybir.dt.int32
ACT = mybir.ActivationFunctionType
AX = mybir.AxisListType

P = 128
N, E, D = 6250, 100000, 128
HID = 256
HEADS, HD = 8, 16
NT = 50
NP = NT * P
RT = (N + P - 1) // P
ET = (E + P - 1) // P
EP = ET * P
PAD_NODE = RT * P - 1
G = 4
GROUPS = 4
U = G * GROUPS
ITERS = -(-(ET + RT - 1) // U)
STEPS = ITERS * U
SB = -(-(STEPS + U) // P)
ST = SB * P
ACCS = 4
AROWS = NP + P
EPS = 1e-5
NEG = -3.0e38


def semaphores(nc, c, prefix):
    taken = []

    def take(name):
        taken.append(nc.alloc_semaphore(prefix + name))
        return taken[-1]

    def give_back():
        nc.clear_and_free_semaphores(taken)
        nc.all_engine_barrier()

    c.callback(give_back)
    return take


class Kit:
    pass


def pipeline(eng, iters, per, *stages, lags=None, loads=0):
    lags = lags or range(len(stages))
    last = max(lags)
    begin = loads + per * max(0, -(-(last - loads) // per))
    rounds = (iters * per - begin) // per

    def fixed(turns):
        for t in turns:
            for stage, lag in zip(stages, lags):
                if 0 <= t - lag < iters * per:
                    stage(*divmod(t - lag, per))

    fixed(range(begin))
    with eng.Fori(0, rounds) as m:
        for t in range(begin, begin + per):
            for stage, lag in zip(stages, lags):
                stage(m + (t - lag) // per, (t - lag) % per)
    fixed(range(begin + rounds * per, iters * per + last))


def load_steps(nc, eng, row, first, top):
    _, vals = nc.values_load_multi_w_load_instructions(
        row[0:1, bass.ds(first, U)], engines=[eng.engine], min_val=0, max_val=top,
        skip_runtime_bounds_check_because="the step table is clamped to this range when it is made")
    return vals


def phase_tables(nc, k):
    with ExitStack() as c:
        sb = lambda n, s, d: c.enter_context(nc.sbuf_tensor(n, s, d))
        sem = semaphores(nc, c, "t_")
        ends = sb("t_ends", [1, 2, ET], I32)
        tiles = sb("t_tiles", [1, 2, ET], I32)
        tf = sb("t_tf", [1, 2, ET], F32)
        length = sb("t_length", [1, ET], F32)
        nought = sb("t_nought", [1, ET], F32)
        upto = sb("t_upto", [1, ET], F32)
        pair = sb("t_pair", [1, 2, ET], F32)
        shift = sb("t_shift", [1, ET + 1], F32)
        wide = sb("t_wide", [P, 2, ET], F32)
        junk = sb("t_junk", [P, ET], F32)
        step_i = sb("t_step_i", [P, SB], I32)
        step_no = sb("t_step_no", [P, SB], F32)
        at_edge = sb("t_at_edge", [P, SB], F32)
        at_node = sb("t_at_node", [P, SB], F32)
        edge_i = sb("t_edge_i", [P, SB], I32)
        ek = sb("t_ek", [P, 2, SB], I32)
        base = sb("t_base", [P, SB], F32)
        srcg = sb("t_srcg", [P, SB, P], I32)
        dstg = sb("t_dstg", [P, SB, P], I32)
        srcf = sb("t_srcf", [P, SB, P], F32)
        relf = sb("t_relf", [P, SB, P], F32)
        relh = sb("t_relh", [P, SB, P], BF16)
        lof = sb("t_lof", [P, SB, P], BF16)
        hi_idx = sb("t_hi_idx", [P, ST], I32)
        loi = sb("t_loi", [P, SB, P], I32)
        loaded, spread, rows, gathered = sem("loaded"), sem("spread"), sem("rows"), k.gathered
        weighted, edges_known = sem("weighted"), sem("edges_known")
        chain, stored, turned, const, got = sem("chain"), sem("stored"), sem("turned"), sem("const"), sem("got")
        conv, tables = sem("conv"), sem("tables")
        with nc.Block() as block:
            @block.sync
            def _(sp):
                with nc.allow_non_contiguous_dma(reason="first and last edge of each tile"):
                    for n, col in ((0, 0), (1, P - 1)):
                        sp.dma_start(ends[0:1, n, :], k.dst[:, col:col + 1].rearrange("e o -> o e")).then_inc(loaded, 16)
                small = [(k.w[n][:].rearrange("p (r d) -> p r d", d=k.small[n].shape[1]),
                          k.small[n].rearrange("(r p) d -> p r d", p=P)) for n in RESIDENT]
                small += [(k.kv[:, 0:D], k.small["L2_gnn_Wk"]), (k.kv[:, D:2 * D], k.small["L2_gnn_Wv"])]
                small += [(k.b[n][:], k.small[n].to_broadcast([P, k.small[n].shape[1]])) for n in ROWS_RESIDENT]
                small += [(k.kv_b[:, h * D:(h + 1) * D], k.small[n].to_broadcast([P, D]))
                          for h, n in enumerate(("L2_gnn_bk", "L2_gnn_bv"))]
                small += [(k.one_eps[:], k.small["L0_gnn_eps"].to_broadcast([P, 1])),
                          (k.X[:], k.small["x"].rearrange("(t p) d -> p t d", p=P))]
                for to, of in small:
                    sp.dma_start(to, of).then_inc(weighted, 16)
                sp.wait_ge(rows, 1)
                sp.dma_start(k.row_dram, pair[0:1, :, :].rearrange("o a e -> o (a e)")).then_inc(stored, 16)
                sp.wait_ge(stored, 16)
                sp.dma_start(wide[:].rearrange("p a e -> p (a e)"), k.row_dram.to_broadcast([P, 2 * ET])).then_inc(spread, 16)
                sp.wait_ge(tables, 1)
                with nc.allow_non_contiguous_dma(reason="a column per block of steps"):
                    for n in range(2):
                        sp.dma_start(k.ek_dram[n].rearrange("(j p) -> p j", p=P), ek[:, n, :]).then_inc(stored, 16)
                sp.wait_ge(stored, 48)
                for n in range(2):
                    sp.dma_start(k.ek[n][0:1, :], k.ek_dram[n:n + 1, :]).then_inc(got, 16)
                sp.wait_ge(conv, 3)
                sp.dma_start(k.rel_rows.rearrange("(j p) e -> p j e", p=P), relh[:]).then_inc(stored, 16)
                sp.dma_start(k.src_rows.rearrange("(j p) e -> p j e", p=P), srcf[:]).then_inc(stored, 16)
                sp.dma_start(k.lo_rows.rearrange("(j p) e -> p j e", p=P), lof[:]).then_inc(stored, 16)
                sp.wait_ge(stored, 96)
                sp.wait_ge(got, 32)

            @block.gpsimd
            def _(g):
                g.iota(step_i[:], pattern=[[P, SB]], base=0, channel_multiplier=1).then_inc(const, 1)
                g.iota(k.lane_i[:], pattern=[[1, P]], base=0, channel_multiplier=0).then_inc(const, 1)
                g.iota(k.part_i[:], pattern=[[0, 1]], base=0, channel_multiplier=1).then_inc(const, 1)
                g.iota(k.trash_i[:], pattern=[[0, G]], base=NP, channel_multiplier=1).then_inc(const, 1)
                for j in range(SB):
                    if j == 0:
                        g.wait_ge(edges_known, 1)
                    for t, (to, of) in enumerate(((srcg, k.src), (dstg, k.dst))):
                        g.indirect_dma_start(out=to[:, j, :], out_offset=None, in_=of,
                                             in_offset=bass.IndirectOffsetOnAxis(ap=edge_i[:, j:j + 1], axis=0)
                                             ).then_inc(gathered, 16)

            @block.vector
            def _(v):
                n = [0]

                def link(ins):
                    n[0] += 1
                    ins.then_inc(chain, 1)
                    v.wait_ge(chain, n[0])

                v.wait_ge(const, 4)
                link(v.tensor_copy(step_no[:], step_i[:]))
                link(v.tensor_copy(k.lane[:], k.lane_i[:]))
                link(v.tensor_copy(k.part[:], k.part_i[:]))
                link(v.tensor_copy(k.trash[:], k.trash_i[:]))
                link(v.tensor_scalar(k.ident[:], k.lane[:], k.part[:, 0:1], None, ALU.is_equal))
                link(v.tensor_scalar(k.before[:], k.lane[:], k.part[:, 0:1], None, ALU.is_lt))
                link(v.memset(k.ones[:], 1.0))
                link(v.memset(nought[:], 0.0))
                link(v.memset(k.is_node[:], 0.0))
                link(v.tensor_scalar(k.is_node[:, 0:1], k.part[:, 0:1], float(N - (RT - 1) * P), None, ALU.is_lt))
                v.wait_ge(loaded, 32)
                link(v.tensor_scalar(tiles[:], ends[:], 7, None, ALU.arith_shift_right))
                link(v.tensor_copy(tf[:], tiles[:]))
                link(v.tensor_tensor(length[:], tf[:, 1, :], tf[:, 0, :], ALU.subtract))
                link(v.tensor_scalar(length[:], length[:], 1.0, None, ALU.add))
                link(v.tensor_tensor_scan(upto[:], length[:], nought[:], 0.0, ALU.add, ALU.add))
                link(v.tensor_tensor(pair[:, 0, :], upto[:], length[:], ALU.subtract))
                link(v.memset(shift[:, 0:1], 0.0))
                link(v.tensor_tensor(shift[:, 1:ET + 1], tf[:, 0, :], pair[:, 0, :], ALU.subtract))
                link(v.tensor_tensor(pair[:, 1, :], shift[:, 1:ET + 1], shift[:, 0:ET], ALU.subtract))
                v.sem_inc(rows, 1)
                v.wait_ge(spread, 16)
                for j in range(SB):
                    link(v.tensor_scalar(junk[:], wide[:, 0, :], step_no[:, j:j + 1], 0.0, ALU.is_le, ALU.add,
                                         accum_out=at_edge[:, j:j + 1]))
                link(v.tensor_scalar(edge_i[:], at_edge[:], -1.0, None, ALU.add))
                v.sem_inc(edges_known, 1)
                for j in range(SB):
                    link(v.scalar_tensor_tensor(out=junk[:], in0=wide[:, 0, :], scalar=step_no[:, j:j + 1], in1=wide[:, 1, :],
                                                op0=ALU.is_le, op1=ALU.mult, accum_out=at_node[:, j:j + 1]))
                link(v.tensor_tensor(at_node[:], at_node[:], step_no[:], ALU.add))
                link(v.tensor_scalar(base[:], at_node[:], -float(P), None, ALU.mult))
                link(v.tensor_copy(ek[:, 0, :], edge_i[:]))
                link(v.tensor_scalar(ek[:, 1, :], at_node[:], float(RT - 1), None, ALU.min))
                v.sem_inc(tables, 1)
                v.wait_ge(gathered, 16 * 2 * SB)
                link(v.tensor_scalar(loi[:], srcg[:], P - 1, None, ALU.bitwise_and))
                link(v.tensor_copy(lof[:], loi[:]))
                link(v.tensor_copy(srcf[:], srcg[:]))
                for j in range(SB):
                    link(v.tensor_scalar(relf[:, j, :], dstg[:, j, :], base[:, j:j + 1], None, ALU.add))
                link(v.tensor_copy(relh[:], relf[:]))
                v.sem_inc(conv, 3)
                for j in range(SB):
                    v.wait_ge(turned, 2 * j + 2)
                    link(v.tensor_copy(k.rel_cols[:, j * P:(j + 1) * P], k.psum[:, 2 * (j % 2), 0:P]))
                    link(v.tensor_copy(k.src_cols[:, j * P:(j + 1) * P], k.psum[:, 2 * (j % 2) + 1, 0:P]))
                    v.sem_inc(k.turn_free, 1)
                link(v.tensor_copy(k.src_idx[:], k.src_cols[:]))
                link(v.tensor_scalar(hi_idx[:], k.src_idx[:], 7, None, ALU.arith_shift_right))
                link(v.tensor_copy(k.hi_cols[:], hi_idx[:]))
                v.wait_ge(weighted, 16 * (len(RESIDENT) + len(ROWS_RESIDENT) + 6))
                link(v.tensor_tensor(k.table_b[:], k.b["L0_gnn_b1"][:], k.b["L0_gnn_be"][:], ALU.add))
                link(v.tensor_scalar(k.one_eps[:], k.one_eps[:], 1.0, None, ALU.add))
                link(v.tensor_scalar(k.b["L2_gnn_bq"][:], k.b["L2_gnn_bq"][:], HD ** -0.5, None, ALU.mult))
                link(v.memset(k.none[:], 0.0))

            @block.tensor
            def _(pe):
                pe.wait_ge(conv, 3)
                for j in range(SB):
                    if j >= 2:
                        pe.wait_ge(k.turn_free, j - 1)
                    pe.transpose(k.psum[:, 2 * (j % 2), 0:P], relf[:, j, :], k.ident[:]).then_inc(turned, 1)
                    pe.transpose(k.psum[:, 2 * (j % 2) + 1, 0:P], srcf[:, j, :], k.ident[:]).then_inc(turned, 1)


SIZES = (4, 4, 2)
BASES = (0, 4, 8)
ROUND = sum(SIZES)
ROUNDS = NT // ROUND
NG = len(SIZES)


def phase_linear(nc, k, name, X, W, cols, bias, OUT, tables=(), also=None, scale=1.0, parts=None, extra=()):
    with ExitStack() as c:
        sb = lambda n, s, d: c.enter_context(nc.sbuf_tensor(name + n, s, d))
        sem = semaphores(nc, c, name)
        tile = sb("_tile", [P, NG, 4, P], F32)
        tile_t = sb("_tile_t", [P, NG, 4, P], F32)
        staged, turned, copied, product, added, stored = (
            sem(n) for n in ("_staged", "_turned", "_copied", "_product", "_added", "_stored"))
        parted = [sem(f"_parted{n}") for n in range(3)]
        reduced = [sem(f"_reduced{n}") for n in range(2)]
        kinds = [(bias, OUT)] + [(b, to) for b, to, _ in tables if to is not None]
        kinds += [(bias, also)] if also is not None else []
        tiles = lambda i, j: bass.ds(ROUND * i + BASES[j], SIZES[j])
        fit = 512 // cols
        banks = (3, 5, 7) if cols > P else (3, 4, 5)

        with nc.Block() as block:
            @block.vector
            def _(v):
                v.sem_inc(added, NG * len(kinds))

                def stage(i, j):
                    v.tensor_copy(tile[:, j, 0:SIZES[j], :], X[:, tiles(i, j), :]).then_inc(staged, 1)

                def add(i, j):
                    v.wait_ge(product, NG * i + j + 1 + NG)
                    for b, to in kinds:
                        for at in range(0, SIZES[j], fit):
                            n = min(fit, SIZES[j] - at)
                            to_n = to[:, bass.ds(ROUND * i + BASES[j] + at, n), :]
                            of_n = k.psum[:, banks[j] + at // fit, 0:n * cols].rearrange("p (t d) -> p t d", d=cols)
                            b_n = b.unsqueeze(1).to_broadcast([P, n, cols])
                            if scale == 1.0:
                                ins = v.tensor_tensor(to_n, of_n, b_n, ALU.add)
                            else:
                                ins = v.scalar_tensor_tensor(out=to_n, in0=of_n, scalar=scale, in1=b_n, op0=ALU.mult, op1=ALU.add)
                        ins.then_inc(added, 1)

                def take_off(part):
                    def take(i, j):
                        v.wait_ge(parted[part], NG * i + j + 1)
                        v.tensor_tensor(OUT[:, tiles(i, j), :], OUT[:, tiles(i, j), :], parts[:, tiles(i, j), part, :],
                                        ALU.subtract).then_inc(reduced[part], 1)
                    return take

                if parts is None:
                    pipeline(v, ROUNDS, NG, stage, add, lags=(0, 2))
                else:
                    pipeline(v, ROUNDS, NG, stage, add, take_off(0), take_off(1), lags=(0, 2, 4, 6))

            @block.tensor
            def _(pe):
                pe.sem_inc(product, NG)

                def turn(i, j):
                    n = NG * i + j
                    pe.wait_ge(staged, n + 1)
                    pe.wait_ge(copied, n + 1)
                    for q in range(SIZES[j]):
                        mm = pe.transpose(k.psum[:, j, q * P:(q + 1) * P], tile[:, j, q, :], k.ident[:])
                    mm.then_inc(turned, 1)

                def multiply(i, j):
                    n = NG * i + j
                    pe.wait_ge(copied, n + 1 + NG)
                    pe.wait_ge(added, len(kinds) * (n + 1))
                    for q in range(SIZES[j]):
                        mm = pe.matmul(k.psum[:, banks[j] + q // fit, (q % fit) * cols:(q % fit + 1) * cols],
                                       tile_t[:, j, q, :], W, start=True, stop=True)
                    mm.then_inc(product, 1)

                pipeline(pe, ROUNDS, NG, turn, multiply)

            @block.scalar
            def _(a):
                a.sem_inc(copied, NG)

                def copy(i, j):
                    n = NG * i + j
                    a.wait_ge(turned, n + 1)
                    a.wait_ge(product, n + 1)
                    nc.scalar.copy(tile_t[:, j, 0:SIZES[j], :].rearrange("p q d -> p (q d)"),
                                   k.psum[:, j, 0:SIZES[j] * P]).then_inc(copied, 1)

                def make(part):
                    def make_part(i, j):
                        if part == 0:
                            a.wait_ge(added, len(kinds) * (NG * i + j + 1 + NG))
                        else:
                            a.wait_ge(reduced[part - 1], NG * i + j + 1)
                        nc.scalar.copy(parts[:, tiles(i, j), part, :], OUT[:, tiles(i, j), :]).then_inc(parted[part], 1)
                    return make_part

                if parts is None:
                    pipeline(a, ROUNDS, NG, copy)
                else:
                    pipeline(a, ROUNDS, NG, copy, make(0), make(1), make(2), lags=(0, 3, 5, 7))

            @block.sync
            def _(sp):
                for to, of in extra:
                    sp.dma_start(to, of).then_inc(stored, 16)
                if tables:
                    def store(i, j):
                        sp.wait_ge(added, len(kinds) * (NG * i + j + 1 + NG))
                        for _, to, table in tables:
                            sp.dma_start(table[:, tiles(i, j), :], (OUT if to is None else to)[:, tiles(i, j), :]
                                         ).then_inc(stored, 16)

                    pipeline(sp, ROUNDS, NG, store)
                if tables or extra:
                    sp.wait_ge(stored, 16 * (len(tables) * NG * ROUNDS + len(extra)))


def vector_chain(nc, sem, v):
    n = [0]

    def link(ins):
        n[0] += 1
        ins.then_inc(sem, 1)
        v.wait_ge(sem, n[0])
    return link


class Norm:
    CUTS = (slice(0, NT // 2), slice(NT // 2, NT))

    def __init__(self, nc, c, sem, name):
        self.nc = nc
        sb = lambda n: c.enter_context(nc.sbuf_tensor(name + n, [P, NT], F32))
        self.mean, self.var, self.root = sb("mean"), sb("var"), sb("root")
        self.centred, self.squared, self.ask, self.rooted, self.done = (
            sem(n) for n in ("centred", "squared", "ask", "rooted", "done"))

    def vector(self, link, v, Y, OUT):
        mean, var = self.mean[:], self.var[:]
        wide = lambda col, cut: col[:, cut].unsqueeze(2).to_broadcast([P, NT // 2, D])
        link(v.tensor_reduce(mean, Y, AX.X, ALU.add))
        link(v.tensor_scalar(mean, mean, 1.0 / D, None, ALU.mult))
        for cut in self.CUTS:
            v.tensor_tensor(Y[:, cut, :], Y[:, cut, :], wide(mean, cut), ALU.subtract).then_inc(self.centred, 1)
        for n, cut in enumerate(self.CUTS):
            v.wait_ge(self.squared, n + 1)
            link(v.tensor_reduce(var[:, cut], OUT[:, cut, :], AX.X, ALU.add))
        link(v.tensor_scalar(var, var, 1.0 / D, EPS, ALU.mult, ALU.add))
        v.sem_inc(self.ask, 1)
        v.wait_ge(self.rooted, 1)
        link(v.reciprocal(var, self.root[:]))
        for cut in self.CUTS:
            v.tensor_tensor(OUT[:, cut, :], Y[:, cut, :], wide(var, cut), ALU.mult).then_inc(self.done, 1)

    def scalar(self, a, Y, OUT):
        for n, cut in enumerate(self.CUTS):
            a.wait_ge(self.centred, n + 1)
            self.nc.scalar.activation(OUT[:, cut, :], Y[:, cut, :], ACT.Square).then_inc(self.squared, 1)
        a.wait_ge(self.ask, 1)
        self.nc.scalar.activation(self.root[:], self.var[:], ACT.Sqrt).then_inc(self.rooted, 1)


def phase_conv_edges(nc, k, table, agg, room, before):
    with ExitStack() as c:
        sb = lambda n, s, d: c.enter_context(nc.sbuf_tensor("c0_" + n, s, d))
        sem = semaphores(nc, c, "c0_")
        idx = sb("idx", [P, U], I32)
        ea = room[:, 0:U * P].rearrange("p (u e) -> p u e", e=P)
        rows = room[:, U * P:U * (P + D)].rearrange("p (u d) -> p u d", d=D)
        msg = sb("msg", [P, 2, G, D], F32)
        oh = sb("oh", [P, 2, G, P], F32)
        ea_in = [sem(f"ea_in{u}") for u in range(U)]
        row_in = k.row_in
        ea_free, row_free, idx_ready, pool_turn = sem("ea_free"), sem("row_free"), sem("idx_ready"), sem("pool_turn")
        product, summed, msg_ready, oh_ready, spread, added, zero = (
            sem(n) for n in ("product", "summed", "msg_ready", "oh_ready", "spread", "added", "zero"))
        with nc.Block() as block:
            @block.sync
            def _(sp):
                with sp.Fori(0, ITERS) as i:
                    tile = load_steps(nc, sp, k.ek[0], i * U, ET - 1)
                    for u in range(U):
                        if u % G == 0:
                            sp.wait_ge(ea_free, GROUPS * i + u // G + 1)
                        sp.dma_start(ea[:, u, :], k.ea_t[:, bass.ds(tile[u] * P, P)]).then_inc(ea_in[u], 16)

            @block.gpsimd
            def _(g):
                with g.Fori(0, ITERS) as i:
                    for u in range(U):
                        if u % G == 0:
                            g.wait_ge(idx_ready, GROUPS * i + u // G + 1)
                            g.wait_ge(row_free, GROUPS * i + u // G + 1)
                            g.sem_inc(pool_turn, 1)
                        g.indirect_dma_start(out=rows[:, u, :], out_offset=None, in_=table,
                                             in_offset=bass.IndirectOffsetOnAxis(ap=idx[:, u:u + 1], axis=0)
                                             ).then_inc(row_in[u], 16)

            @block.tensor
            def _(pe):
                pe.sem_inc(ea_free, GROUPS)
                pe.sem_inc(spread, 2)

                def edge_product(i, j):
                    pe.wait_ge(summed, GROUPS * i + j + 1)
                    for q in range(G):
                        pe.wait_ge(ea_in[G * j + q], 16 * i + 16)
                        mm = pe.matmul(k.psum[:, j % 2, q * D:(q + 1) * D], ea[:, G * j + q, :], k.w["L0_gnn_wet"][:],
                                       start=True, stop=True)
                        if q == G - 1:
                            mm.then_inc(product, 1)
                    pe.wait_ge(product, GROUPS * i + j + 1)
                    pe.sem_inc(ea_free, 1)

                def sum_into_nodes(i, j):
                    pe.wait_ge(msg_ready, GROUPS * i + j + 1)
                    pe.wait_ge(oh_ready, GROUPS * i + j + 1)
                    pe.wait_ge(added, G * (GROUPS * i + j) + G)
                    for q in range(G):
                        mm = pe.matmul(k.psum[:, 2 + j % 2, q * D:(q + 1) * D], oh[:, j % 2, q, :], msg[:, j % 2, q, :],
                                       start=True, stop=True)
                    mm.then_inc(spread, 1)

                pipeline(pe, ITERS, GROUPS, edge_product, sum_into_nodes)

            @block.scalar
            def _(a):
                with a.Fori(0, ITERS) as i:
                    for j in range(GROUPS):
                        a.wait_ge(summed, GROUPS * i + j + 3)
                        nc.scalar.activation(msg[:, j % 2], msg[:, j % 2], ACT.Silu).then_inc(msg_ready, 1)

            @block.vector
            def _(v):
                v.memset(agg, 0.0).then_inc(zero, 1)
                v.wait_ge(zero, 1)
                v.sem_inc(summed, 2)
                v.sem_inc(row_free, GROUPS)
                v.sem_inc(added, 2 * G)

                def stage(i, j):
                    v.tensor_copy(idx[:, G * j:G * j + G], k.src_idx[:, bass.ds(i * U + G * j, G)]).then_inc(idx_ready, 1)

                for j in range(GROUPS):
                    stage(0, j)

                def front(i, j):
                    v.wait_ge(spread, GROUPS * i + j + 1)
                    v.tensor_tensor(oh[:, j % 2], k.lane[:].unsqueeze(1).to_broadcast([P, G, P]),
                                    k.rel_cols[:, bass.ds(i * U + G * j, G)].unsqueeze(2).to_broadcast([P, G, P]),
                                    ALU.is_equal).then_inc(oh_ready, 1)
                    v.wait_ge(product, GROUPS * i + j + 1)
                    for q in range(G):
                        v.wait_ge(row_in[G * j + q], 16 * i + 16 * (before + 1))
                    v.tensor_tensor(msg[:, j % 2].rearrange("p q d -> p (q d)"), k.psum[:, j % 2, :],
                                    rows[:, G * j:G * j + G, :].rearrange("p q d -> p (q d)"), ALU.add).then_inc(summed, 1)
                    v.wait_ge(summed, GROUPS * i + j + 3)
                    v.sem_inc(row_free, 1)
                    stage(i + 1, j)

                regs = {}

                def back(i, j):
                    if j == 0:
                        regs["node"] = load_steps(nc, v, k.ek[1], i * U, RT - 1)
                    v.wait_ge(spread, GROUPS * i + j + 3)
                    for q in range(G):
                        t = regs["node"][G * j + q]
                        v.wait_ge(added, G * (GROUPS * i + j) + q + 2 * G)
                        v.tensor_tensor(agg[:, bass.ds(t, 1), :], agg[:, bass.ds(t, 1), :],
                                        k.psum[:, 2 + j % 2:3 + j % 2, q * D:(q + 1) * D], ALU.add).then_inc(added, 1)

                pipeline(v, ITERS, GROUPS, front, back, loads=1)


def phase_conv_nodes(nc, k, H, Y, S1):
    with ExitStack() as c:
        sb = lambda n, s, d: c.enter_context(nc.sbuf_tensor("n0_" + n, s, d))
        sem = semaphores(nc, c, "n0_")
        norm = Norm(nc, c, sem, "n0_")
        total = sb("total", [P, 2, D], F32)
        stat = sb("stat", [P, 3, D], F32)
        chain, ask, rooted, want, have = (sem(n) for n in ("chain", "ask_act", "told", "want", "have"))
        wide = [P, NT, D]
        with nc.Block() as block:
            @block.vector
            def _(v):
                link = vector_chain(nc, chain, v)
                link(v.scalar_tensor_tensor(out=Y, in0=H, scalar=k.one_eps[:, 0:1], in1=Y, op0=ALU.mult, op1=ALU.add))
                v.sem_inc(ask, 1)
                v.wait_ge(rooted, 1)
                link(v.tensor_tensor(Y, S1, k.X[:], ALU.add))
                link(v.tensor_tensor(Y[:, RT - 1:NT, :], Y[:, RT - 1:NT, :],
                                     k.is_node[:].unsqueeze(2).to_broadcast([P, NT - RT + 1, D]), ALU.mult))
                link(v.tensor_reduce(total[:, 0, :], Y.rearrange("p t d -> p d t"), AX.X, ALU.add))
                v.sem_inc(want, 1)
                v.wait_ge(have, 1)
                link(v.scalar_tensor_tensor(out=stat[:, 0, :], in0=k.psum[:, 0, 0:D], scalar=1.0 / N,
                                            in1=k.b["L0_gnn_gn_mean_scale"][:], op0=ALU.mult, op1=ALU.mult))
                link(v.tensor_tensor(Y, Y, stat[:, 0, :].unsqueeze(1).to_broadcast(wide), ALU.subtract))
                link(v.tensor_tensor(S1, Y, Y, ALU.mult))
                link(v.tensor_tensor(S1[:, RT - 1:NT, :], S1[:, RT - 1:NT, :],
                                     k.is_node[:].unsqueeze(2).to_broadcast([P, NT - RT + 1, D]), ALU.mult))
                link(v.tensor_reduce(total[:, 1, :], S1.rearrange("p t d -> p d t"), AX.X, ALU.add))
                v.sem_inc(want, 1)
                v.wait_ge(have, 2)
                link(v.tensor_scalar(stat[:, 1, :], k.psum[:, 1, 0:D], 1.0 / N, EPS, ALU.mult, ALU.add))
                v.sem_inc(ask, 1)
                v.wait_ge(rooted, 2)
                link(v.reciprocal(stat[:, 1, :], stat[:, 2, :]))
                link(v.tensor_tensor(stat[:, 1, :], stat[:, 1, :], k.b["L0_gnn_gn_weight"][:], ALU.mult))
                link(v.tensor_tensor(Y, Y, stat[:, 1, :].unsqueeze(1).to_broadcast(wide), ALU.mult))
                link(v.tensor_tensor(Y, Y, k.b["L0_gnn_gn_bias"][:].unsqueeze(1).to_broadcast(wide), ALU.add))
                link(v.tensor_tensor(Y, Y, k.X[:], ALU.add))
                norm.vector(link, v, Y, k.X[:])

            @block.scalar
            def _(a):
                a.wait_ge(ask, 1)
                nc.scalar.activation(S1, Y, ACT.Silu).then_inc(rooted, 1)
                a.wait_ge(ask, 2)
                nc.scalar.activation(stat[:, 2, :], stat[:, 1, :], ACT.Sqrt).then_inc(rooted, 1)
                norm.scalar(a, Y, k.X[:])

            @block.tensor
            def _(pe):
                for n in range(2):
                    pe.wait_ge(want, n + 1)
                    pe.matmul(k.psum[:, n, 0:D], k.ones[:], total[:, n, :], start=True, stop=True).then_inc(have, 1)


def phase_scores_nodes(nc, k, Hs, S):
    with ExitStack() as c:
        sem = semaphores(nc, c, "s1_")
        score = c.enter_context(nc.sbuf_tensor("s1_score", [P, 2, NT], F32))
        chain = sem("chain")
        block = c.enter_context(nc.Block())

        @block.vector
        def _(v):
            link = vector_chain(nc, chain, v)
            for n in range(2):
                link(v.tensor_tensor(S, Hs, k.b["L1_gnn_a_w"][:, n * D:(n + 1) * D].unsqueeze(1).to_broadcast([P, NT, D]), ALU.mult))
                link(v.tensor_reduce(score[:, n, :], S, AX.X, ALU.add))
            for n, parts in enumerate((k.src_score, k.dst_score)):
                for part in range(3):
                    link(v.tensor_copy(parts[:, :, part], score[:, n, :]))
                    if part < 2:
                        link(v.tensor_tensor(score[:, n, :], score[:, n, :], parts[:, :, part], ALU.subtract))


def phase_scores_edges(nc, k, scores, room):
    G8, PER = 8, U // 8
    WIDE = NT + 3
    with ExitStack() as c:
        sb = lambda n, s, d: c.enter_context(nc.sbuf_tensor("s_" + n, s, d))
        sem = semaphores(nc, c, "s_")
        rel = sb("rel", [P, PER, G8 * P], BF16)
        lo = sb("lo", [P, PER, G8 * P], BF16)
        is_rel = sb("is_rel", [P, PER, G8 * P], BF16)
        is_lo = sb("is_lo", [P, PER, G8 * P], BF16)
        size = PER * G8 * WIDE
        mask, picked = (room[:, n * size:(n + 1) * size].rearrange("p (j q n) -> p j q n", j=PER, q=G8) for n in range(2))
        rel_in = [sem(f"rel_in{n}") for n in range(PER)]
        lo_in = [sem(f"lo_in{n}") for n in range(PER)]
        rel_used, lo_used, mask_ready, product, read, reduced, preset, sp_turn = (
            sem(n) for n in ("rel_used", "lo_used", "mask_ready", "product", "read", "reduced", "preset", "sp_turn"))
        rel_flat = k.rel_rows.rearrange("(o s) e -> o (s e)", o=1)
        lo_flat = k.lo_rows.rearrange("(o s) e -> o (s e)", o=1)
        with nc.Block() as block:
            @block.sync
            def _(sp):
                with sp.Fori(0, ITERS) as i:
                    for j in range(PER):
                        at = bass.ds(sp.snap((i * U + j * G8) * P), G8 * P)
                        sp.wait_ge(rel_used, PER * i + j + 1)
                        sp.sem_inc(sp_turn, 1)
                        sp.dma_start(rel[:, j, :], rel_flat[:, at].to_broadcast([P, G8 * P])).then_inc(rel_in[j], 16)
                        sp.wait_ge(lo_used, PER * i + j + 1)
                        sp.sem_inc(sp_turn, 1)
                        sp.dma_start(lo[:, j, :], lo_flat[:, at].to_broadcast([P, G8 * P])).then_inc(lo_in[j], 16)

            @block.tensor
            def _(pe):
                with pe.Fori(0, ITERS) as i:
                    node = load_steps(nc, pe, k.ek[1], i * U, RT - 1)
                    for j in range(PER):
                        pe.wait_ge(rel_used, PER * i + j + 1 + PER)
                        pe.wait_ge(lo_used, PER * i + j + 1 + PER)
                        pe.wait_ge(read, PER * i + j + 1)
                        for q in range(G8):
                            cols = k.psum[:, j, q * WIDE:(q + 1) * WIDE]
                            for part in range(3):
                                pe.matmul(cols[:, 0:NT], is_lo[:, j, q * P:(q + 1) * P], k.src_score[:, :, part],
                                          start=(part == 0), stop=(part == 2))
                            mm = pe.matmul(cols[:, NT:WIDE], is_rel[:, j, q * P:(q + 1) * P],
                                           k.dst_score[:, bass.ds(node[j * G8 + q], 1), :], start=True, stop=True)
                        mm.then_inc(product, 1)

            @block.vector
            def _(v):
                v.memset(mask[:, :, :, NT:WIDE], 1.0).then_inc(preset, 1)
                v.sem_inc(rel_used, PER)
                v.sem_inc(lo_used, PER)
                v.sem_inc(read, PER)
                v.wait_ge(preset, 1)

                def matrices(i, j):
                    v.wait_ge(rel_in[j], 16 * i + 16)
                    v.tensor_scalar(is_rel[:, j, :], rel[:, j, :], k.part[:, 0:1], None, ALU.is_equal).then_inc(rel_used, 1)
                    v.wait_ge(lo_in[j], 16 * i + 16)
                    v.tensor_scalar(is_lo[:, j, :], lo[:, j, :], k.part[:, 0:1], None, ALU.is_equal).then_inc(lo_used, 1)

                def make_mask(i, j):
                    v.tensor_tensor(mask[:, j, :, 0:NT], k.lane[:, 0:NT].unsqueeze(1).to_broadcast([P, G8, NT]),
                                    k.hi_cols[:, bass.ds(i * U + G8 * j, G8)].unsqueeze(2).to_broadcast([P, G8, NT]),
                                    ALU.is_equal).then_inc(mask_ready, 1)

                def pick(i, j):
                    n = PER * i + j
                    v.wait_ge(product, n + 1)
                    v.wait_ge(mask_ready, n + 1)
                    v.tensor_tensor(picked[:, j].rearrange("p q n -> p (q n)"), k.psum[:, j, 0:G8 * WIDE],
                                    mask[:, j].rearrange("p q n -> p (q n)"), ALU.mult).then_inc(read, 1)

                def reduce(i, j):
                    n = PER * i + j
                    v.wait_ge(read, n + 1 + PER)
                    v.tensor_reduce(scores[:, bass.ds(i * U + G8 * j, G8)], picked[:, j], AX.X, ALU.add).then_inc(reduced, 1)

                pipeline(v, ITERS, PER, reduce, matrices, pick, make_mask, lags=(2, 0, 1, 0))
                v.wait_ge(reduced, PER * ITERS)


def phase_softmax(nc, k, scores):
    with ExitStack() as c:
        sb = lambda n, s, d: c.enter_context(nc.sbuf_tensor("x_" + n, s, d))
        sem = semaphores(nc, c, "x_")
        a = sb("a", [P, STEPS], F32)
        live = sb("live", [P, STEPS], F32)
        m = sb("m", [P, 8], F32)
        landed, chain, ask, told, expd = (sem(n) for n in ("landed", "chain", "ask", "told", "expd"))
        rel, src, e = k.rel_cols[:, 0:STEPS], k.src_cols[:, 0:STEPS], scores[:, 0:STEPS]
        with nc.Block() as block:
            @block.sync
            def _(sp):
                sp.dma_start(m[:, 0:1], k.small["L1_gnn_a_b"].to_broadcast([P, 1])).then_inc(landed, 16)
                sp.wait_ge(landed, 16)

            @block.vector
            def _(v):
                link = vector_chain(nc, chain, v)
                v.wait_ge(landed, 16)
                link(v.tensor_scalar(live[:], rel, 0.0, None, ALU.is_ge))
                link(v.scalar_tensor_tensor(out=live[:], in0=rel, scalar=float(P), in1=live[:], op0=ALU.is_lt, op1=ALU.mult))
                link(v.scalar_tensor_tensor(out=live[:], in0=src, scalar=float(N), in1=live[:], op0=ALU.is_lt, op1=ALU.mult))
                link(v.tensor_scalar(e, e, m[:, 0:1], None, ALU.add))
                link(v.tensor_scalar(a[:], e, 0.01, None, ALU.mult))
                link(v.tensor_tensor(e, e, a[:], ALU.max))
                link(v.tensor_tensor(e, e, live[:], ALU.mult))
                link(v.tensor_scalar(a[:], live[:], -1.0, -NEG, ALU.add, ALU.mult))
                link(v.tensor_tensor(e, e, a[:], ALU.add))
                link(v.tensor_reduce(m[:, 1:2], e, AX.X, ALU.max))
                v.sem_inc(ask, 1)
                v.wait_ge(told, 1)
                link(v.tensor_reduce(m[0:1, 2:3], k.psum[0:1, 0, 0:P], AX.X, ALU.max))
                v.sem_inc(ask, 1)
                v.wait_ge(told, 2)
                link(v.tensor_scalar(m[:, 3:4], k.psum[:, 1, 0:1], -1.0, None, ALU.mult))
                v.sem_inc(ask, 1)
                v.wait_ge(told, 3)
                link(v.reciprocal(m[:, 5:6], k.psum[:, 2, 0:1]))
                link(v.tensor_scalar(e, e, m[:, 5:6], None, ALU.mult))

            @block.scalar
            def _(act):
                act.wait_ge(ask, 3)
                nc.scalar.activation(e, e, ACT.Exp, bias=m[:, 3:4], accum_out=m[:, 4:5]).then_inc(expd, 1)

            @block.tensor
            def _(pe):
                pe.wait_ge(ask, 1)
                pe.matmul(k.psum[0:1, 0, 0:P], m[:, 1:2], k.ident[:], start=True, stop=True).then_inc(told, 1)
                pe.wait_ge(ask, 2)
                pe.matmul(k.psum[:, 1, 0:1], k.ones[0:1, :], m[0:1, 2:3], start=True, stop=True).then_inc(told, 1)
                pe.wait_ge(expd, 1)
                pe.matmul(k.psum[:, 2, 0:1], k.ones[:], m[:, 4:5], start=True, stop=True).then_inc(told, 1)


def phase_attend(nc, k, weights, H3, accs, room):
    with ExitStack() as c:
        sb = lambda n, s, d: c.enter_context(nc.sbuf_tensor("a_" + n, s, d))
        sem = semaphores(nc, c, "a_")
        rel = sb("rel", [P, GROUPS, G * P], BF16)
        out_rows = room[:, 0:U * D].rearrange("p (u d) -> p u d", d=D)
        src = room[:, U * D:2 * U * D].rearrange("p (j e) -> p j e", j=GROUPS)
        same, msg = (room[:, 2 * U * D + n * U * P:2 * U * D + (n + 1) * U * P].rearrange("p (j q e) -> p j q e", j=GROUPS, q=G)
                     for n in range(2))
        oht = sb("oht", [P, GROUPS, G * P], BF16)
        col = sb("col", [P, GROUPS, 2, G], F32)
        junk = sb("junk", [P, P], F32)
        count = sb("count", [P, GROUPS, G], F32)
        away = sb("away", [P, GROUPS, G], F32)
        idx = sb("idx", [P, U], I32)
        zero = sb("zero", [P, D], F32)
        rel_in = [sem(f"rel_in{n}") for n in range(GROUPS)]
        src_in = [sem(f"src_in{n}") for n in range(GROUPS)]
        acc_done = k.acc_done
        zeroed, oht_ready, same_ready, product, msg_ready, merged, rows_ready, idx_ready, rows_free, pool_turn, chain, col_ready = (
            sem(n) for n in ("zeroed", "oht_ready", "same_ready", "product", "msg_ready", "merged", "rows_ready",
                             "idx_ready", "rows_free", "pool_turn", "chain", "col_ready"))
        sp_turn = sem("sp_turn")
        rel_flat = k.rel_rows.rearrange("(o s) e -> o (s e)", o=1)
        src_flat = k.src_rows.rearrange("(o s) e -> o (s e)", o=1)
        with nc.Block() as block:
            @block.sync
            def _(sp):
                with sp.Fori(0, ITERS) as i:
                    for j in range(GROUPS):
                        at = bass.ds(sp.snap((i * U + j * G) * P), G * P)
                        sp.wait_ge(oht_ready, GROUPS * i + j + 1)
                        sp.sem_inc(sp_turn, 1)
                        sp.dma_start(rel[:, j, :], rel_flat[:, at].to_broadcast([P, G * P])).then_inc(rel_in[j], 16)
                        sp.wait_ge(same_ready, GROUPS * i + j + 1)
                        sp.sem_inc(sp_turn, 1)
                        sp.dma_start(src[:, j, :], src_flat[:, at].to_broadcast([P, G * P])).then_inc(src_in[j], 16)

            @block.vector
            def _(v):
                v.memset(zero[:], 0.0).then_inc(zeroed, 1)
                v.sem_inc(oht_ready, GROUPS)
                v.sem_inc(same_ready, GROUPS)
                with v.Fori(0, ITERS) as i:
                    for j in range(GROUPS):
                        h, n = j, GROUPS * i + j
                        steps = bass.ds(i * U + G * j, G)
                        v.wait_ge(merged, n + 1)
                        v.tensor_copy(col[:, h, 0, :], weights[:, steps]).then_inc(col_ready, 1)
                        v.tensor_copy(col[:, h, 1, :], k.src_cols[:, steps]).then_inc(col_ready, 1)
                        v.wait_ge(rel_in[j], 16 * i + 16)
                        v.tensor_scalar(oht[:, h, :], rel[:, j, :], k.part[:, 0:1], None, ALU.is_equal).then_inc(oht_ready, 1)
                        v.wait_ge(src_in[j], 16 * i + 16)
                        v.wait_ge(col_ready, 2 * n + 2)
                        rows = src[:, j, :].rearrange("p (q e) -> p q e", e=P)
                        for q in range(G):
                            v.scalar_tensor_tensor(out=junk[:], in0=rows[:, q, :], scalar=col[:, h, 1, q:q + 1], in1=k.before[:],
                                                   op0=ALU.is_equal, op1=ALU.mult,
                                                   accum_out=count[:, h, q:q + 1]).then_inc(chain, 1)
                            v.wait_ge(chain, 7 * n + q + 1)
                        v.tensor_tensor(away[:, h], k.trash[:], col[:, h, 1, :], ALU.subtract).then_inc(chain, 1)
                        v.tensor_tensor(same[:, h], rows, col[:, h, 1, :].unsqueeze(2).to_broadcast([P, G, P]),
                                        ALU.is_equal).then_inc(same_ready, 1)
                        v.wait_ge(chain, 7 * n + 5)
                        v.scalar_tensor_tensor(out=away[:, h], in0=count[:, h], scalar=0.0, in1=away[:, h],
                                               op0=ALU.is_gt, op1=ALU.mult).then_inc(chain, 1)
                        v.wait_ge(chain, 7 * n + 6)
                        v.wait_ge(rows_free, n + 1)
                        v.tensor_tensor(idx[:, G * j:G * j + G], away[:, h], col[:, h, 1, :], ALU.add).then_inc(chain, 1)
                        v.wait_ge(chain, 7 * n + 7)
                        v.sem_inc(idx_ready, 1)

            @block.tensor
            def _(pe):
                pe.sem_inc(merged, GROUPS)
                regs = {}

                def expand(i, j):
                    if j == 0:
                        regs["node"] = load_steps(nc, pe, k.ek[1], i * U, RT - 1)
                    n = GROUPS * i + j
                    pe.wait_ge(oht_ready, n + 1 + GROUPS)
                    pe.wait_ge(msg_ready, n + 1)
                    for q in range(G):
                        for part in range(3):
                            mm = pe.matmul(k.psum[:, j, q * D:(q + 1) * D], oht[:, j, q * P:(q + 1) * P],
                                           H3[:, bass.ds(regs["node"][G * j + q], 1), part, :],
                                           start=(part == 0), stop=(part == 2))
                    mm.then_inc(product, 1)

                def merge(i, j):
                    n = GROUPS * i + j
                    pe.wait_ge(msg_ready, n + 1 + GROUPS)
                    pe.wait_ge(same_ready, n + 1 + GROUPS)
                    pe.wait_ge(rows_ready, n + 1)
                    for q in range(G):
                        mm = pe.matmul(k.psum[:, GROUPS + j, q * D:(q + 1) * D], same[:, j, q, :], msg[:, j, q, :],
                                       start=True, stop=True)
                    mm.then_inc(merged, 1)

                pipeline(pe, ITERS, GROUPS, expand, merge)

            @block.scalar
            def _(a):
                a.sem_inc(msg_ready, GROUPS)
                a.sem_inc(rows_ready, GROUPS)

                def scale(i, j):
                    n = GROUPS * i + j
                    a.wait_ge(product, n + 1)
                    a.wait_ge(col_ready, 2 * n + 2)
                    a.wait_ge(merged, n + 1)
                    for q in range(G):
                        ins = nc.scalar.activation(msg[:, j, q, :], k.psum[:, j, q * D:(q + 1) * D], ACT.Copy,
                                                   scale=col[:, j, 0, q:q + 1])
                    ins.then_inc(msg_ready, 1)

                def copy(i, j):
                    n = GROUPS * i + j
                    a.wait_ge(merged, n + 1 + GROUPS)
                    a.wait_ge(rows_free, n + 1)
                    nc.scalar.copy(out_rows[:, G * j:G * j + G, :].rearrange("p q d -> p (q d)"),
                                   k.psum[:, GROUPS + j, :]).then_inc(rows_ready, 1)

                pipeline(a, ITERS, GROUPS, scale, copy)

            @block.gpsimd
            def _(g):
                g.sem_inc(rows_free, GROUPS - 1)
                g.wait_ge(zeroed, 1)
                for n in range(ACCS):
                    g.dma_start(accs[n].rearrange("(t p) d -> p t d", p=P),
                                zero[:].unsqueeze(1).to_broadcast([P, AROWS // P, D])).then_inc(acc_done[n], 16)
                with g.Fori(0, ITERS) as i:
                    for u in range(U):
                        n = GROUPS * i + u // G
                        if u % G == 0:
                            g.wait_ge(idx_ready, n + 1)
                            g.wait_ge(rows_ready, n + 1 + GROUPS)
                        g.wait_ge(acc_done[u % ACCS], 16 * ((U // ACCS) * i + u // ACCS + 1))
                        g.sem_inc(rows_free if u % G == G - 1 else pool_turn, 1)
                        g.indirect_dma_start(out=accs[u % ACCS], out_offset=bass.IndirectOffsetOnAxis(ap=idx[:, u:u + 1], axis=0),
                                             in_=out_rows[:, u, :], in_offset=None, compute_op=ALU.add
                                             ).then_inc(acc_done[u % ACCS], 16)
                for n in range(ACCS):
                    g.wait_ge(acc_done[n], 16 * (STEPS // ACCS + 1))


def phase_attend_nodes(nc, k, accs, Y, S, Z):
    with ExitStack() as c:
        sem = semaphores(nc, c, "b_")
        norm = Norm(nc, c, sem, "b_")
        landed = [sem(f"landed{n}") for n in range(ACCS)]
        chain = sem("chain")
        bufs = [Y, S, *Z]
        with nc.Block() as block:
            @block.sync
            def _(sp):
                for n in range(ACCS):
                    sp.dma_start(bufs[n], accs[n][0:NP, :].rearrange("(t p) d -> p t d", p=P)).then_inc(landed[n], 16)

            @block.vector
            def _(v):
                link = vector_chain(nc, chain, v)
                for n in range(ACCS):
                    v.wait_ge(landed[n], 16)
                    link(v.tensor_tensor(Y, Y, bufs[n] if n else k.X[:], ALU.add))
                norm.vector(link, v, Y, k.X[:])

            @block.scalar
            def _(a):
                norm.scalar(a, Y, k.X[:])


def phase_heads_edges(nc, k, table, Q3, agg, AW, room, before):
    with ExitStack() as c:
        sb = lambda n, s, d: c.enter_context(nc.sbuf_tensor("h_" + n, s, d))
        sem = semaphores(nc, c, "h_")
        idx = sb("idx", [P, U], I32)
        rows = room[:, 0:U * 2 * D].rearrange("p (u d) -> p u d", d=2 * D)
        rel = sb("rel", [P, GROUPS, G * P], BF16)
        oht = sb("oht", [P, 2, G * P], BF16)
        oh = sb("oh", [P, 2, G, P], F32)
        kq = sb("kq", [P, G, D], F32)
        score = sb("score", [P, 2, G, HEADS], F32)
        msg = sb("msg", [P, 2, G, AW], F32)
        rel_in = [sem(f"rel_in{n}") for n in range(GROUPS)]
        row_in = k.row_in
        idx_ready, pool_turn, sp_turn = sem("idx_ready"), sem("pool_turn"), sem("sp_turn")
        oht_ready, oh_ready, product, kq_ready, clipped, weighed, msg_ready, spread, added, zero, chain = (
            sem(n) for n in ("oht_ready", "oh_ready", "product", "kq_ready", "clipped", "weighed", "msg_ready", "spread",
                             "added", "zero", "chain"))
        rel_flat = k.rel_rows.rearrange("(o s) e -> o (s e)", o=1)
        sums = lambda j, q: k.psum[:, 2 + 2 * (j % 2) + q // 2, (q % 2) * AW:(q % 2 + 1) * AW]
        with nc.Block() as block:
            @block.sync
            def _(sp):
                with sp.Fori(0, ITERS) as i:
                    for j in range(GROUPS):
                        at = bass.ds(sp.snap((i * U + j * G) * P), G * P)
                        sp.wait_ge(oht_ready, GROUPS * i + j + 1)
                        sp.sem_inc(sp_turn, 1)
                        sp.dma_start(rel[:, j, :], rel_flat[:, at].to_broadcast([P, G * P])).then_inc(rel_in[j], 16)

            @block.gpsimd
            def _(g):
                with g.Fori(0, ITERS) as i:
                    for u in range(U):
                        if u % G == 0:
                            g.wait_ge(idx_ready, GROUPS * i + u // G + 1)
                            g.wait_ge(msg_ready, GROUPS * i + u // G + 1)
                            g.sem_inc(pool_turn, 1)
                        g.indirect_dma_start(out=rows[:, u, :], out_offset=None, in_=table,
                                             in_offset=bass.IndirectOffsetOnAxis(ap=idx[:, u:u + 1], axis=0)
                                             ).then_inc(row_in[u], 16)

            @block.tensor
            def _(pe):
                regs = {}

                def expand(i, j):
                    if j == 0:
                        regs["node"] = load_steps(nc, pe, k.ek[1], i * U, RT - 1)
                    n = GROUPS * i + j
                    pe.wait_ge(oht_ready, n + 1 + GROUPS)
                    pe.wait_ge(kq_ready, n + 1)
                    for q in range(G):
                        for part in range(3):
                            mm = pe.matmul(k.psum[:, j % 2, q * D:(q + 1) * D], oht[:, j % 2, q * P:(q + 1) * P],
                                           Q3[:, bass.ds(regs["node"][G * j + q], 1), part, :],
                                           start=(part == 0), stop=(part == 2))
                    mm.then_inc(product, 1)

                def sum_into_nodes(i, j):
                    n = GROUPS * i + j
                    pe.wait_ge(msg_ready, n + 1 + GROUPS)
                    pe.wait_ge(oh_ready, n + 1)
                    pe.wait_ge(added, G * n + G)
                    for q in range(G):
                        mm = pe.matmul(sums(j, q), oh[:, j % 2, q, :], msg[:, j % 2, q, :], start=True, stop=True)
                    mm.then_inc(spread, 1)

                pipeline(pe, ITERS, GROUPS, expand, sum_into_nodes, lags=(0, 2))

            @block.scalar
            def _(a):
                with a.Fori(0, ITERS) as i:
                    for j in range(GROUPS):
                        n = GROUPS * i + j
                        a.wait_ge(clipped, n + 1)
                        a.wait_ge(spread, n + 1)
                        nc.scalar.activation(msg[:, j % 2, :, D:D + HEADS], score[:, j % 2], ACT.Exp).then_inc(weighed, 1)

            @block.vector
            def _(v):
                v.memset(agg, 0.0).then_inc(zero, 1)
                v.memset(msg[:, :, :, AW - 1:AW], 1.0).then_inc(zero, 1)
                v.wait_ge(zero, 2)
                v.sem_inc(oht_ready, GROUPS)
                v.sem_inc(kq_ready, 2)
                v.sem_inc(msg_ready, GROUPS)
                v.sem_inc(spread, 2)
                v.sem_inc(added, 2 * G)

                def stage(i, j):
                    v.tensor_copy(idx[:, G * j:G * j + G], k.src_idx[:, bass.ds(i * U + G * j, G)]).then_inc(idx_ready, 1)

                for j in range(GROUPS):
                    stage(0, j)

                def expand_matrix(i, j):
                    v.wait_ge(rel_in[j], 16 * i + 16)
                    v.tensor_scalar(oht[:, j % 2, :], rel[:, j, :], k.part[:, 0:1], None, ALU.is_equal).then_inc(oht_ready, 1)

                def sum_matrix(i, j):
                    v.wait_ge(spread, GROUPS * i + j + 1)
                    v.tensor_tensor(oh[:, j % 2], k.lane[:].unsqueeze(1).to_broadcast([P, G, P]),
                                    k.rel_cols[:, bass.ds(i * U + G * j, G)].unsqueeze(2).to_broadcast([P, G, P]),
                                    ALU.is_equal).then_inc(oh_ready, 1)

                def key_times_query(i, j):
                    v.wait_ge(product, GROUPS * i + j + 1)
                    for q in range(G):
                        v.wait_ge(row_in[G * j + q], 16 * i + 16 * (before + 1))
                    v.tensor_tensor(kq[:], k.psum[:, j % 2, :].rearrange("p (q d) -> p q d", d=D),
                                    rows[:, G * j:G * j + G, 0:D], ALU.mult).then_inc(kq_ready, 1)

                def sum_of_head(i, j):
                    n = GROUPS * i + j
                    v.wait_ge(kq_ready, n + 3)
                    v.tensor_reduce(score[:, j % 2].rearrange("p q h -> p (q h)"),
                                    kq[:].rearrange("p q (h e) -> p (q h) e", e=HD), AX.X, ALU.add).then_inc(chain, 1)

                def clip(i, j):
                    v.wait_ge(chain, GROUPS * i + j + 1)
                    v.tensor_scalar(score[:, j % 2], score[:, j % 2], -5.0, 5.0, ALU.max, ALU.min).then_inc(clipped, 1)

                def messages(i, j):
                    v.wait_ge(weighed, GROUPS * i + j + 1)
                    v.tensor_tensor(msg[:, j % 2, :, 0:D].rearrange("p q (h e) -> p q h e", e=HD),
                                    rows[:, G * j:G * j + G, D:2 * D].rearrange("p q (h e) -> p q h e", e=HD),
                                    msg[:, j % 2, :, D:D + HEADS].unsqueeze(3).to_broadcast([P, G, HEADS, HD]),
                                    ALU.mult).then_inc(msg_ready, 1)
                    stage(i + 1, j)

                regs = {}

                def add(q):
                    def add_one(i, j):
                        if j == 0 and q == 0:
                            regs["node"] = load_steps(nc, v, k.ek[1], i * U, RT - 1)
                        n = GROUPS * i + j
                        if q == 0:
                            v.wait_ge(spread, n + 3)
                        t = bass.ds(regs["node"][G * j + q], 1)
                        v.wait_ge(added, G * n + q + 2 * G)
                        v.tensor_tensor(agg[:, t, :], agg[:, t, :], sums(j, q).unsqueeze(1), ALU.add).then_inc(added, 1)
                    return add_one

                pipeline(v, ITERS, GROUPS, expand_matrix, add(0), key_times_query, add(1), sum_of_head, add(2), clip,
                         messages, add(3), sum_matrix, lags=(0, 4, 1, 4, 1, 4, 1, 2, 4, 1), loads=4)


def phase_heads_nodes(nc, k, agg, AW, Y, S):
    with ExitStack() as c:
        sem = semaphores(nc, c, "g_")
        norm = Norm(nc, c, sem, "g_")
        chain = sem("chain")
        inv = S.rearrange("p t d -> p (t d)")[:, 0:NT * HEADS].rearrange("p (t h) -> p t h", h=HEADS)
        with nc.Block() as block:
            @block.vector
            def _(v):
                link = vector_chain(nc, chain, v)
                link(v.tensor_copy(k.degree[:], agg[:, :, AW - 1]))
                link(v.tensor_scalar(inv, agg[:, :, D:D + HEADS], 1e-30, None, ALU.max))
                link(v.reciprocal(inv, inv))
                link(v.tensor_tensor(Y.rearrange("p t (h e) -> p t h e", e=HD),
                                     agg[:, :, 0:D].rearrange("p t (h e) -> p t h e", e=HD),
                                     inv.unsqueeze(3).to_broadcast([P, NT, HEADS, HD]), ALU.mult))
                link(v.tensor_tensor(Y, Y, k.X[:], ALU.add))
                norm.vector(link, v, Y, k.X[:])

            @block.scalar
            def _(a):
                norm.scalar(a, Y, k.X[:])


def phase_relation_edges(nc, k, table, D3, agg, before):
    with ExitStack() as c:
        sb = lambda n, s, d: c.enter_context(nc.sbuf_tensor("r_" + n, s, d))
        sem = semaphores(nc, c, "r_")
        room = k.X[:].rearrange("p t d -> p (t d)")
        rows = room[:, 0:U * HID].rearrange("p (u d) -> p u d", d=HID)
        msg = room[:, U * HID:U * HID + 2 * G * HID].rearrange("p (h q d) -> p h q d", h=2, d=HID)
        idx = sb("idx", [P, U], I32)
        ea = sb("ea", [P, U, P], F32)
        rel = sb("rel", [P, GROUPS, G * P], BF16)
        oht = sb("oht", [P, 2, G * P], BF16)
        oh = sb("oh", [P, 2, G, P], F32)
        ea_in = [sem(f"ea_in{u}") for u in range(U)]
        rel_in = [sem(f"rel_in{n}") for n in range(GROUPS)]
        row_in = k.row_in
        idx_ready, pool_turn, sp_turn = sem("idx_ready"), sem("pool_turn"), sem("sp_turn")
        oht_ready, oh_ready, product, summed, msg_ready, spread, added, zero = (
            sem(n) for n in ("oht_ready", "oh_ready", "product", "summed", "msg_ready", "spread", "added", "zero"))
        rel_flat = k.rel_rows.rearrange("(o s) e -> o (s e)", o=1)
        hidden = lambda j, q: k.psum[:, 2 * (j % 2) + q // 2, (q % 2) * HID:(q % 2 + 1) * HID]
        sums = lambda j, q: k.psum[:, 4 + 2 * (j % 2) + q // 2, (q % 2) * HID:(q % 2 + 1) * HID]
        with nc.Block() as block:
            @block.sync
            def _(sp):
                with sp.Fori(0, ITERS) as i:
                    tile = load_steps(nc, sp, k.ek[0], i * U, ET - 1)
                    for u in range(U):
                        j = u // G
                        if u % G == 0:
                            at = bass.ds(sp.snap((i * U + u) * P), G * P)
                            sp.wait_ge(oht_ready, GROUPS * i + j + 1)
                            sp.sem_inc(sp_turn, 1)
                            sp.dma_start(rel[:, j, :], rel_flat[:, at].to_broadcast([P, G * P])).then_inc(rel_in[j], 16)
                            sp.wait_ge(product, GROUPS * i + j + 1)
                            sp.sem_inc(sp_turn, 1)
                        sp.dma_start(ea[:, u, :], k.ea_t[:, bass.ds(tile[u] * P, P)]).then_inc(ea_in[u], 16)

            @block.gpsimd
            def _(g):
                with g.Fori(0, ITERS) as i:
                    for u in range(U):
                        if u % G == 0:
                            g.wait_ge(idx_ready, GROUPS * i + u // G + 1)
                            g.wait_ge(summed, 2 * (GROUPS * i + u // G) + 2)
                            g.sem_inc(pool_turn, 1)
                        g.indirect_dma_start(out=rows[:, u, :], out_offset=None, in_=table,
                                             in_offset=bass.IndirectOffsetOnAxis(ap=idx[:, u:u + 1], axis=0)
                                             ).then_inc(row_in[u], 16)

            @block.tensor
            def _(pe):
                pe.sem_inc(product, GROUPS)
                regs = {}

                def hidden_product(i, j):
                    if j == 0:
                        regs["node"] = load_steps(nc, pe, k.ek[1], i * U, RT - 1)
                    n = GROUPS * i + j
                    pe.wait_ge(summed, 2 * n + 6)
                    pe.wait_ge(oht_ready, n + 1 + GROUPS)
                    for q in range(G):
                        pe.wait_ge(ea_in[G * j + q], 16 * i + 16)
                        pe.matmul(hidden(j, q), ea[:, G * j + q, :], k.w["L3_gnn_re_w1"][:, 2 * HID:3 * HID], start=True, stop=False)
                        for part in range(3):
                            mm = pe.matmul(hidden(j, q), oht[:, j % 2, q * P:(q + 1) * P],
                                           D3[:, bass.ds(regs["node"][G * j + q], 1), part, :],
                                           start=False, stop=(part == 2))
                        if q == G - 1:
                            mm.then_inc(product, 1)

                def sum_into_nodes(i, j):
                    n = GROUPS * i + j
                    pe.wait_ge(msg_ready, n + 1)
                    pe.wait_ge(oh_ready, n + 1)
                    pe.wait_ge(added, G * n + G)
                    for q in range(G):
                        mm = pe.matmul(sums(j, q), oh[:, j % 2, q, :], msg[:, j % 2, q, :], start=True, stop=True)
                    mm.then_inc(spread, 1)

                pipeline(pe, ITERS, GROUPS, hidden_product, sum_into_nodes, lags=(0, 2))

            @block.scalar
            def _(a):
                with a.Fori(0, ITERS) as i:
                    for j in range(GROUPS):
                        a.wait_ge(summed, 2 * (GROUPS * i + j) + 10)
                        nc.scalar.activation(msg[:, j % 2], msg[:, j % 2], ACT.Relu).then_inc(msg_ready, 1)

            @block.vector
            def _(v):
                v.memset(agg, 0.0).then_inc(zero, 1)
                v.wait_ge(zero, 1)
                v.sem_inc(oht_ready, GROUPS)
                v.sem_inc(summed, 2 * GROUPS)
                v.sem_inc(spread, 2)
                v.sem_inc(added, 2 * G)

                def stage(i, j):
                    v.tensor_copy(idx[:, G * j:G * j + G], k.src_idx[:, bass.ds(i * U + G * j, G)]).then_inc(idx_ready, 1)

                for j in range(GROUPS):
                    stage(0, j)

                def expand_matrix(i, j):
                    v.wait_ge(rel_in[j], 16 * i + 16)
                    v.tensor_scalar(oht[:, j % 2, :], rel[:, j, :], k.part[:, 0:1], None, ALU.is_equal).then_inc(oht_ready, 1)

                def sum_matrix(i, j):
                    v.wait_ge(spread, GROUPS * i + j + 1)
                    v.tensor_tensor(oh[:, j % 2], k.lane[:].unsqueeze(1).to_broadcast([P, G, P]),
                                    k.rel_cols[:, bass.ds(i * U + G * j, G)].unsqueeze(2).to_broadcast([P, G, P]),
                                    ALU.is_equal).then_inc(oh_ready, 1)

                def add_rows(h):
                    def add_half(i, j):
                        if h == 0:
                            v.wait_ge(product, GROUPS * i + j + 1 + GROUPS)
                        for q in (2 * h, 2 * h + 1):
                            v.wait_ge(row_in[G * j + q], 16 * i + 16 * (before + 1))
                        v.tensor_tensor(msg[:, j % 2, 2 * h:2 * h + 2, :].rearrange("p q d -> p (q d)"),
                                        k.psum[:, 2 * (j % 2) + h, :],
                                        rows[:, G * j + 2 * h:G * j + 2 * h + 2, :].rearrange("p q d -> p (q d)"),
                                        ALU.add).then_inc(summed, 1)
                        if h == 1:
                            stage(i + 1, j)
                    return add_half

                regs = {}

                def add_sums(q):
                    def add_one(i, j):
                        if j == 0 and q == 0:
                            regs["node"] = load_steps(nc, v, k.ek[1], i * U, RT - 1)
                        n = GROUPS * i + j
                        if q == 0:
                            v.wait_ge(spread, n + 3)
                        t = bass.ds(regs["node"][G * j + q], 1)
                        v.wait_ge(added, G * n + q + 2 * G)
                        v.tensor_tensor(agg[:, t, :], agg[:, t, :], sums(j, q).unsqueeze(1), ALU.add).then_inc(added, 1)
                    return add_one

                pipeline(v, ITERS, GROUPS, expand_matrix, add_sums(0), sum_matrix, add_sums(1), add_rows(0), add_sums(2),
                         add_rows(1), add_sums(3), lags=(0, 3, 1, 3, 1, 3, 1, 3), loads=3)


def phase_update_nodes(nc, k, ap, x_kept, agg, Y, room):
    with ExitStack() as c:
        sb = lambda n, s, d: c.enter_context(nc.sbuf_tensor("u_" + n, s, d))
        sem = semaphores(nc, c, "u_")
        w_in = k.w["L3_gnn_re_w1"][:].rearrange("p (f h) -> p f h", f=3)
        b_in, re2t = k.kv, k.kv_b
        re_b2 = sb("re_b2", [P, 1], F32)
        w_deg = sb("w_deg", [1, HID], F32)
        w_out = sb("w_out", [P, 2, D], F32)
        b_hid = sb("b_hid", [P, 2], F32)
        b_out = sb("b_out", [P, D], F32)
        deg_t = sb("deg_t", [NT, P], F32)
        wide = ROUND * 3 * P
        tile_all = sb("tile", [P, wide], F32)
        deg_row = room[0:1, wide:wide + NP]
        hid = room[:, wide + NP:wide + NP + 8 * P].rearrange("p (h n) -> p h n", h=2)
        of_group = lambda buf, j: buf[:, BASES[j] * 3 * P:(BASES[j] + SIZES[j]) * 3 * P].rearrange("p (f n) -> p f n", f=3)
        tile, tile_t = ([of_group(buf, j) for j in range(NG)] for buf in (tile_all, room))
        x_in, landed, folded, fold_copied, deg_turned, row_made, staged, turned, copied, hidden, active, product, added = (
            sem(n) for n in ("x_in", "landed", "folded", "fold_copied", "deg_turned", "row_made", "staged", "turned", "copied",
                             "hidden", "active", "product", "added"))
        bank = lambda j, h: (k.psum[:, (3, 5, 7)[j] + h, 0:SIZES[j] * P] if SIZES[j] == 4 else
                             k.psum[:, (3, 5, 7)[j], h * SIZES[j] * P:(h + 1) * SIZES[j] * P])
        tiles = lambda i, j: bass.ds(ROUND * i + BASES[j], SIZES[j])
        with nc.Block() as block:
            @block.sync
            def _(sp):
                with nc.allow_non_contiguous_dma(reason="bias vectors onto the partitions"):
                    sp.dma_start(w_in[:, 0, :], ap["L3_gnn_ea_w1"][0:D, :]).then_inc(landed, 16)
                    sp.dma_start(b_in[:], ap["L3_gnn_ea_w1"][D:2 * D, :]).then_inc(landed, 16)
                    sp.dma_start(re2t[:], ap["L3_gnn_re_w2t"]).then_inc(landed, 16)
                    sp.dma_start(re_b2[:], ap["L3_gnn_re_b2"].rearrange("o d -> d o")).then_inc(landed, 16)
                    for h in range(2):
                        sp.dma_start(w_out[:, h, :], ap["L3_gnn_ea_w2"][h * P:(h + 1) * P, :]).then_inc(landed, 16)
                        sp.dma_start(b_hid[:, h:h + 1], ap["L3_gnn_ea_b1"][:, h * P:(h + 1) * P].rearrange("o d -> d o")).then_inc(landed, 16)
                    sp.dma_start(b_out[:], ap["L3_gnn_ea_b2"].to_broadcast([P, D])).then_inc(landed, 16)
                sp.dma_start(k.X[:], x_kept).then_inc(x_in, 16)
                sp.wait_ge(fold_copied, 3)
                sp.dma_start(k.deg_dram, deg_t[:]).then_inc(row_made, 16)
                sp.wait_ge(row_made, 16)
                sp.dma_start(deg_row, k.deg_dram.rearrange("(o t) e -> o (t e)", o=1)).then_inc(row_made, 16)
                sp.wait_ge(row_made, 32)
                sp.wait_ge(landed, 144)

            @block.tensor
            def _(pe):
                pe.sem_inc(product, 1)
                pe.transpose(k.psum[0:NT, 5, 0:P], k.degree[:], k.ident[:]).then_inc(deg_turned, 1)
                pe.wait_ge(landed, 144)
                for h in range(2):
                    pe.matmul(k.psum[:, 3, h * HID:(h + 1) * HID], re2t[:, h * P:(h + 1) * P], b_in[:], start=True, stop=True)
                pe.matmul(k.psum[0:1, 4, 0:HID], re_b2[:], b_in[:], start=True, stop=True).then_inc(folded, 1)

                def turn(i, j):
                    n = NG * i + j
                    pe.wait_ge(staged, n + 1)
                    for f in range(3):
                        pe.wait_ge(copied, 3 * n + f + 1)
                        for q in range(SIZES[j]):
                            mm = pe.transpose(k.psum[:, f, q * P:(q + 1) * P], tile[j][:, f, q * P:(q + 1) * P], k.ident[:])
                        mm.then_inc(turned, 1)

                def hide(i, j):
                    n = NG * i + j
                    pe.wait_ge(copied, 3 * n + 6)
                    pe.wait_ge(fold_copied, 3)
                    pe.wait_ge(row_made, 32)
                    pe.wait_ge(added, n + 1)
                    for h in range(2):
                        half = slice(h * P, (h + 1) * P)
                        for f in range(3):
                            pe.matmul(bank(j, h), w_in[:, f, half], tile_t[j][:, f, :], start=(f == 0), stop=False)
                        pe.matmul(bank(j, h), w_deg[0:1, half],
                                  deg_row[:, bass.ds((ROUND * i + BASES[j]) * P, SIZES[j] * P)],
                                  start=False, stop=True).then_inc(hidden, 1)

                def out(i, j):
                    n = NG * i + j
                    pe.wait_ge(active, 2 * n + 2)
                    for q in range(SIZES[j]):
                        for h in range(2):
                            mm = pe.matmul(bank(j, 0)[:, q * D:(q + 1) * D], hid[:, h, q * P:(q + 1) * P], w_out[:, h, :],
                                           start=(h == 0), stop=(h == 1))
                    mm.then_inc(product, 1)

                pipeline(pe, ROUNDS, NG, hide, turn, out, lags=(1, 0, 2))

            @block.scalar
            def _(a):
                a.wait_ge(landed, 144)

                def activate(i, j):
                    n = NG * i + j
                    a.wait_ge(product, n + 1)
                    for h in range(2):
                        a.wait_ge(hidden, 2 * n + h + 1)
                        nc.scalar.activation(hid[:, h, 0:SIZES[j] * P], bank(j, h), ACT.Relu,
                                             bias=b_hid[:, h:h + 1]).then_inc(active, 1)

                pipeline(a, ROUNDS, NG, activate)

            @block.vector
            def _(v):
                v.wait_ge(deg_turned, 1)
                v.tensor_copy(deg_t[:], k.psum[0:NT, 5, 0:P]).then_inc(fold_copied, 1)
                v.wait_ge(folded, 1)
                v.tensor_copy(w_in[:, 1:3, :], k.psum[:, 3, :].rearrange("p (h d) -> p h d", h=2)).then_inc(fold_copied, 1)
                v.tensor_copy(w_deg[:], k.psum[0:1, 4, 0:HID]).then_inc(fold_copied, 1)
                v.sem_inc(copied, 3)
                v.sem_inc(added, NG)
                v.wait_ge(x_in, 16)

                def stage(i, j):
                    v.tensor_copy(tile[j][:, 0, :].rearrange("p (t d) -> p t d", d=P), k.X[:, tiles(i, j), :])
                    for f in range(2):
                        ins = v.tensor_copy(tile[j][:, 1 + f, :].rearrange("p (t d) -> p t d", d=P),
                                            agg[:, tiles(i, j), f * P:(f + 1) * P])
                    ins.then_inc(staged, 1)

                def copy(i, j):
                    for f in range(3):
                        v.wait_ge(turned, 3 * (NG * i + j) + f + 1)
                        v.tensor_copy(tile_t[j][:, f, :], k.psum[:, f, 0:SIZES[j] * P]).then_inc(copied, 1)

                def add(i, j):
                    v.wait_ge(product, NG * i + j + 2)
                    v.tensor_tensor(Y[:, tiles(i, j), :], bank(j, 0).rearrange("p (t d) -> p t d", d=D),
                                    b_out[:].unsqueeze(1).to_broadcast([P, SIZES[j], D]), ALU.add).then_inc(added, 1)

                pipeline(v, ROUNDS, NG, stage, copy, add, lags=(0, 1, 3))


def phase_last_norm(nc, k, Y, out):
    with ExitStack() as c:
        sem = semaphores(nc, c, "z_")
        norm = Norm(nc, c, sem, "z_")
        chain, stored = sem("chain"), sem("stored")
        with nc.Block() as block:
            @block.vector
            def _(v):
                link = vector_chain(nc, chain, v)
                link(v.tensor_tensor(Y, Y, k.X[:], ALU.add))
                norm.vector(link, v, Y, k.X[:])

            @block.scalar
            def _(a):
                norm.scalar(a, Y, k.X[:])

            @block.sync
            def _(sp):
                full = N // P
                for n, cut in enumerate(norm.CUTS):
                    sp.wait_ge(norm.done, n + 1)
                    to = min(cut.stop, full)
                    sp.dma_start(out[cut.start * P:to * P, :].rearrange("(t p) d -> p t d", p=P),
                                 k.X[:, cut.start:to, :]).then_inc(stored, 16)
                sp.dma_start(out[full * P:N, :], k.X[0:N - full * P, full, :]).then_inc(stored, 16)
                sp.wait_ge(stored, 48)


TRANSPOSED = {"L0_gnn_w1t": "L0_gnn_w1", "L0_gnn_wet": "L0_gnn_we", "L3_gnn_re_w2t": "L3_gnn_re_w2"}
AS_THEY_ARE = ("L1_gnn_W_w", "L2_gnn_Wq", "L2_gnn_Wk", "L2_gnn_Wv", "L3_gnn_re_w1", "L3_gnn_ea_w1", "L3_gnn_ea_w2")
ROWS = ("L0_gnn_b1", "L0_gnn_be", "L0_gnn_eps", "L0_gnn_gn_weight", "L0_gnn_gn_bias", "L0_gnn_gn_mean_scale",
        "L1_gnn_W_b", "L1_gnn_a_w", "L1_gnn_a_b", "L2_gnn_bq", "L2_gnn_bk", "L2_gnn_bv", "L3_gnn_re_b1",
        "L3_gnn_re_b2", "L3_gnn_ea_b1", "L3_gnn_ea_b2")


RESIDENT = ("L0_gnn_w1t", "L0_gnn_wet", "L1_gnn_W_w", "L2_gnn_Wq", "L3_gnn_re_w1")
ROWS_RESIDENT = ("L0_gnn_b1", "L0_gnn_be", "L0_gnn_gn_weight", "L0_gnn_gn_bias", "L0_gnn_gn_mean_scale",
                 "L1_gnn_W_b", "L1_gnn_a_w", "L2_gnn_bq", "L3_gnn_re_b1")


def build(nc, ap, out):
    k = Kit()
    k.small = ap
    k.ea_t, k.src, k.dst = ap["ea_t"], ap["src"], ap["dst"]
    dram = lambda n, s, d: nc.dram_tensor(n, s, d, kind="Internal").ap()
    k.row_dram = dram("row_dram", (1, 2 * ET), F32)
    k.ek_dram = dram("ek_dram", (2, ST), I32)
    k.deg_dram = dram("deg_dram", (NT, P), F32)
    k.rel_rows = dram("rel_rows", (ST, P), BF16)
    k.src_rows = dram("src_rows", (ST, P), F32)
    k.lo_rows = dram("lo_rows", (ST, P), BF16)
    table0 = dram("table0", (NP, D), F32)
    table_kv = dram("table_kv", (NP, 2 * D), F32)
    table_ps = dram("table_ps", (NP, HID), F32)
    x_dram = dram("x_dram", (NP, D), F32)
    accs = [dram(f"acc{n}", (AROWS, D), F32) for n in range(ACCS)]
    tiled = lambda t: t.rearrange("(t p) d -> p t d", p=P)
    with ExitStack() as c:
        sb = lambda n, s, d: c.enter_context(nc.sbuf_tensor(n, s, d))
        k.psum = c.enter_context(nc.psum_tensor("psum", [P, 8, 512], F32))
        k.lane_i, k.part_i = sb("lane_i", [P, P], I32), sb("part_i", [P, 1], I32)
        k.trash_i, k.trash = sb("trash_i", [P, G], I32), sb("trash", [P, G], F32)
        k.lane, k.part = sb("lane", [P, P], F32), sb("part", [P, 1], F32)
        k.ident, k.before, k.ones = sb("ident", [P, P], F32), sb("before", [P, P], F32), sb("ones", [P, P], F32)
        k.degree = sb("degree", [P, NT], F32)
        k.is_node = sb("is_node", [P, NT - RT + 1], F32)
        k.rel_cols, k.src_cols, k.src_idx = sb("rel_cols", [P, ST], F32), sb("src_cols", [P, ST], F32), sb("src_idx", [P, ST], I32)
        k.hi_cols = sb("hi_cols", [P, ST], F32)
        k.ek = [sb("edge_tile", [1, ST], I32), sb("node_tile", [1, ST], I32)]
        k.one_eps = sb("one_eps", [P, 1], F32)
        k.w = {n: sb("w_" + n, [P, ap[n].shape[0] // P * ap[n].shape[1]], F32) for n in RESIDENT}
        k.kv = sb("w_kv", [P, 2 * D], F32)
        k.b = {n: sb("b_" + n, [P, ap[n].shape[1]], F32) for n in ROWS_RESIDENT}
        k.kv_b = sb("b_kv", [P, 2 * D], F32)
        k.table_b, k.none = sb("b_table", [P, D], F32), sb("b_none", [P, HID], F32)
        k.row_in = [c.enter_context(nc.semaphore(f"row_in{u}")) for u in range(U)]
        k.acc_done = [c.enter_context(nc.semaphore(f"acc_done{n}")) for n in range(ACCS)]
        k.gathered = c.enter_context(nc.semaphore("gathered"))
        k.turn_free = c.enter_context(nc.semaphore("turn_free"))
        k.X = sb("X", [P, NT, D], F32)
        phase_tables(nc, k)
        R1 = sb("R1", [P, NT, 256], F32)
        R3 = sb("R3", [P, NT * 3 * 256], BF16)
        r1 = R1[:].rearrange("p t d -> p (t d)")
        r3 = R3[:].bitcast(F32)
        half1 = lambda b: r1[:, b * NT * D:(b + 1) * NT * D].rearrange("p (t d) -> p t d", d=D)
        half3 = lambda b: r3[:, b * NT * D:(b + 1) * NT * D].rearrange("p (t d) -> p t d", d=D)
        tile1 = lambda n: ap[n].to_broadcast([P, ap[n].shape[1]])

        H = half3(0)
        phase_linear(nc, k, "l0", k.X[:], k.w["L0_gnn_w1t"][:], D, k.b["L0_gnn_b1"][:], H,
                     tables=[(k.table_b[:], half1(0), tiled(table0))])
        agg = half1(0)
        phase_conv_edges(nc, k, table0, agg, r3[:, NT * D:], 0)
        phase_conv_nodes(nc, k, H, agg, half1(1))

        H3 = R3[:, 0:NT * 3 * D].rearrange("p (t n d) -> p t n d", n=3, d=D)
        phase_linear(nc, k, "l1", k.X[:], k.w["L1_gnn_W_w"][:], D, k.b["L1_gnn_W_b"][:], half1(0), also=half1(1), parts=H3)
        with ExitStack() as c1:
            k.src_score = c1.enter_context(nc.sbuf_tensor("src_score", [P, NT, 3], BF16))
            k.dst_score = c1.enter_context(nc.sbuf_tensor("dst_score", [P, NT, 3], BF16))
            scores = r3[:, 3 * NT * D // 2:][:, 0:ST]
            phase_scores_nodes(nc, k, half1(1), half1(0))
            phase_scores_edges(nc, k, scores, r1)
            phase_softmax(nc, k, scores)
        phase_attend(nc, k, scores, H3, accs, r1)
        phase_attend_nodes(nc, k, accs, half1(0), half1(1), (half3(0), half3(1)))

        phase_linear(nc, k, "l2", k.X[:], k.kv[:], 2 * D, k.kv_b[:], R1[:], tables=[(None, None, tiled(table_kv))])
        phase_linear(nc, k, "l3", k.X[:], k.w["L2_gnn_Wq"][:], D, k.b["L2_gnn_bq"][:], half1(0),
                     scale=HD ** -0.5, parts=H3)
        AW = D + HEADS + 1
        agg2 = r1[:, 0:NT * AW].rearrange("p (t w) -> p t w", w=AW)
        phase_heads_edges(nc, k, table_kv, H3, agg2, AW, r3[:, 3 * NT * D // 2:], ITERS)
        phase_heads_nodes(nc, k, agg2, AW, half3(0), half3(1))

        w1 = k.w["L3_gnn_re_w1"]
        phase_linear(nc, k, "l4", k.X[:], w1[:, 0:HID], HID, k.none[:], R1[:], tables=[(None, None, tiled(table_ps))],
                     extra=[(tiled(x_dram), k.X[:])])
        D3 = R3[:].rearrange("p (t n d) -> p t n d", n=3, d=HID)
        phase_linear(nc, k, "l5", k.X[:], w1[:, HID:2 * HID], HID, k.b["L3_gnn_re_b1"][:], R1[:], parts=D3)
        phase_relation_edges(nc, k, table_ps, D3, R1[:], 2 * ITERS)
        phase_update_nodes(nc, k, ap, tiled(x_dram), R1[:], half3(0), r3[:, NT * D:])
        phase_last_norm(nc, k, half3(0), out)


def layout(inputs):
    x = np.zeros((NP, D), np.float32)
    x[:N] = inputs["x"]
    ea_t = np.zeros((D, EP), np.float32)
    ea_t[:, :E] = np.asarray(inputs["edge_attr_128"]).T
    arrays = {"x": x, "ea_t": ea_t}
    for name in ("src", "dst"):
        padded = np.full((EP,), PAD_NODE, np.int32)
        padded[:E] = inputs[name]
        arrays[name] = padded.reshape(ET, P)
    for to, of in TRANSPOSED.items():
        arrays[to] = np.ascontiguousarray(np.asarray(inputs[of]).T)
    for name in AS_THEY_ARE:
        arrays[name] = np.ascontiguousarray(inputs[name])
    for name in ROWS:
        arrays[name] = np.asarray(inputs[name]).reshape(1, -1)
    return arrays


def kernel(**inputs):
    import concourse.bacc as bacc
    from concourse.bass_utils import run_bass_kernel_spmd

    arrays = layout(inputs)
    nc = bacc.Bacc("TRN2", target_bir_lowering=False, num_devices=1)
    ap = {name: nc.dram_tensor("in_" + name, a.shape, mybir.dt.from_np(a.dtype), kind="ExternalInput").ap()
          for name, a in arrays.items()}
    out = nc.dram_tensor("out", (N, D), F32, kind="ExternalOutput").ap()
    build(nc, ap, out)
    r = run_bass_kernel_spmd(nc, [{"in_" + name: a for name, a in arrays.items()}], core_ids=[0])
    return r.results[0]["out"]
```

```python
from contextlib import ExitStack

import numpy as np

import concourse.bass as bass
from concourse import mybir
from concourse.alu_op_type import AluOpType as ALU

F32 = mybir.dt.float32
BF16 = mybir.dt.bfloat16
I32 = mybir.dt.int32
ACT = mybir.ActivationFunctionType
AX = mybir.AxisListType

P = 128
N, E, D = 6250, 100000, 128
HID = 256
HEADS, HD = 8, 16
NT = 50
NP = NT * P
RT = (N + P - 1) // P
ET = (E + P - 1) // P
EP = ET * P
PAD_NODE = RT * P - 1
G = 4
GROUPS = 4
U = G * GROUPS
ITERS = 2 * -(-(ET + RT - 1) // (2 * U))
STEPS = ITERS * U
SB = -(-(STEPS + U) // P)
ST = SB * P
ACCS = 4
AROWS = NP + P
EPS = 1e-5
NEG = -3.0e38


def semaphores(nc, c, prefix):
    taken = []

    def take(name):
        taken.append(nc.alloc_semaphore(prefix + name))
        return taken[-1]

    def give_back():
        nc.clear_and_free_semaphores(taken)
        nc.all_engine_barrier()

    c.callback(give_back)
    return take


class Kit:
    pass


def pipeline(eng, iters, per, *stages, lags=None, loads=0):
    lags = lags or range(len(stages))
    last = max(lags)
    begin = loads + per * max(0, -(-(last - loads) // per))
    rounds = (iters * per - begin) // per

    def fixed(turns):
        for t in turns:
            for stage, lag in zip(stages, lags):
                if 0 <= t - lag < iters * per:
                    stage(*divmod(t - lag, per))

    fixed(range(begin))
    with eng.Fori(0, rounds) as m:
        for t in range(begin, begin + per):
            for stage, lag in zip(stages, lags):
                stage(m + (t - lag) // per, (t - lag) % per)
    fixed(range(begin + rounds * per, iters * per + last))


def load_steps(nc, eng, row, first, top):
    _, vals = nc.values_load_multi_w_load_instructions(
        row[0:1, bass.ds(first, U)], engines=[eng.engine], min_val=0, max_val=top,
        skip_runtime_bounds_check_because="the step table is clamped to this range when it is made")
    return vals


def phase_tables(nc, k):
    with ExitStack() as c:
        sb = lambda n, s, d: c.enter_context(nc.sbuf_tensor(n, s, d))
        sem = semaphores(nc, c, "t_")
        ends = sb("t_ends", [1, 2, ET], I32)
        tiles = sb("t_tiles", [1, 2, ET], I32)
        tf = sb("t_tf", [1, 2, ET], F32)
        length = sb("t_length", [1, ET], F32)
        nought = sb("t_nought", [1, ET], F32)
        upto = sb("t_upto", [1, ET], F32)
        pair = sb("t_pair", [1, 2, ET], F32)
        shift = sb("t_shift", [1, ET + 1], F32)
        wide = sb("t_wide", [P, 2, ET], F32)
        junk = sb("t_junk", [P, ET], F32)
        step_i = sb("t_step_i", [P, SB], I32)
        step_no = sb("t_step_no", [P, SB], F32)
        at_edge = sb("t_at_edge", [P, SB], F32)
        at_node = sb("t_at_node", [P, SB], F32)
        edge_i = sb("t_edge_i", [P, SB], I32)
        ek = sb("t_ek", [P, 2, SB], I32)
        base = sb("t_base", [P, SB], F32)
        srcg = sb("t_srcg", [P, SB, P], I32)
        dstg = sb("t_dstg", [P, SB, P], I32)
        srcf = sb("t_srcf", [P, SB, P], F32)
        relf = sb("t_relf", [P, SB, P], F32)
        relh = sb("t_relh", [P, SB, P], BF16)
        lof = sb("t_lof", [P, SB, P], BF16)
        hi_idx = sb("t_hi_idx", [P, ST], I32)
        loi = sb("t_loi", [P, SB, P], I32)
        loaded, spread, rows, gathered = sem("loaded"), sem("spread"), sem("rows"), k.gathered
        weighted, edges_known, copied = sem("weighted"), sem("edges_known"), sem("copied")
        chain, stored, turned, const, got = sem("chain"), sem("stored"), sem("turned"), sem("const"), sem("got")
        conv, tables = sem("conv"), sem("tables")
        with nc.Block() as block:
            @block.sync
            def _(sp):
                with nc.allow_non_contiguous_dma(reason="first and last edge of each tile"):
                    for n, col in ((0, 0), (1, P - 1)):
                        sp.dma_start(ends[0:1, n, :], k.dst[:, col:col + 1].rearrange("e o -> o e")).then_inc(loaded, 16)
                small = [(k.w[n][:].rearrange("p (r d) -> p r d", d=k.small[n].shape[1]),
                          k.small[n].rearrange("(r p) d -> p r d", p=P)) for n in RESIDENT]
                small += [(k.kv[:, 0:D], k.small["L2_gnn_Wk"]), (k.kv[:, D:2 * D], k.small["L2_gnn_Wv"])]
                small += [(k.b[n][:], k.small[n].to_broadcast([P, k.small[n].shape[1]])) for n in ROWS_RESIDENT]
                small += [(k.kv_b[:, h * D:(h + 1) * D], k.small[n].to_broadcast([P, D]))
                          for h, n in enumerate(("L2_gnn_bk", "L2_gnn_bv"))]
                small += [(k.one_eps[:], k.small["L0_gnn_eps"].to_broadcast([P, 1])),
                          (k.X[:], k.small["x"].rearrange("(t p) d -> p t d", p=P))]
                small += [(k.w_out[:], k.small["L3_gnn_ea_w2"].rearrange("(h p) d -> p h d", p=P)),
                          (k.b_out[:], k.small["L3_gnn_ea_b2"].to_broadcast([P, D]))]
                for to, of in small:
                    sp.dma_start(to, of).then_inc(weighted, 16)
                with nc.allow_non_contiguous_dma(reason="bias vectors onto the partitions"):
                    sp.dma_start(k.re_b2[:], k.small["L3_gnn_re_b2"].rearrange("o d -> d o")).then_inc(weighted, 16)
                    sp.dma_start(k.b_hid[:], k.small["L3_gnn_ea_b1"].rearrange("o (h d) -> d (o h)", d=P)).then_inc(weighted, 16)
                sp.wait_ge(tables, 1)
                with nc.allow_non_contiguous_dma(reason="a column per block of steps"):
                    for n in range(2):
                        sp.dma_start(k.ek_dram[n].rearrange("(j p) -> p j", p=P), ek[:, n, :]).then_inc(stored, 16)
                sp.wait_ge(stored, 32)
                for n in range(2):
                    sp.dma_start(k.ek[n][0:1, :], k.ek_dram[n:n + 1, :]).then_inc(got, 16)
                sp.wait_ge(conv, 3)
                sp.dma_start(k.rel_rows.rearrange("(j p) e -> p j e", p=P), relh[:]).then_inc(stored, 16)
                sp.dma_start(k.src_rows.rearrange("(j p) e -> p j e", p=P), srcf[:]).then_inc(stored, 16)
                sp.dma_start(k.lo_rows.rearrange("(j p) e -> p j e", p=P), lof[:]).then_inc(stored, 16)
                sp.wait_ge(stored, 80)
                sp.wait_ge(got, 32)

            @block.gpsimd
            def _(g):
                g.iota(step_i[:], pattern=[[P, SB]], base=0, channel_multiplier=1).then_inc(const, 1)
                g.iota(k.lane_i[:], pattern=[[1, P]], base=0, channel_multiplier=0).then_inc(const, 1)
                g.iota(k.part_i[:], pattern=[[0, 1]], base=0, channel_multiplier=1).then_inc(const, 1)
                g.iota(k.trash_i[:], pattern=[[0, G]], base=NP, channel_multiplier=1).then_inc(const, 1)
                for j in range(SB):
                    if j == 0:
                        g.wait_ge(edges_known, 1)
                    for to, of in ((srcg, k.src), (dstg, k.dst)):
                        g.indirect_dma_start(out=to[:, j, :], out_offset=None, in_=of,
                                             in_offset=bass.IndirectOffsetOnAxis(ap=edge_i[:, j:j + 1], axis=0)
                                             ).then_inc(gathered, 16)

            @block.vector
            def _(v):
                n = [0]

                def link(ins):
                    n[0] += 1
                    ins.then_inc(chain, 1)
                    v.wait_ge(chain, n[0])

                v.wait_ge(const, 4)
                link(v.tensor_copy(step_no[:], step_i[:]))
                link(v.tensor_copy(k.lane[:], k.lane_i[:]))
                link(v.tensor_copy(k.part[:], k.part_i[:]))
                link(v.tensor_scalar(k.minus_part[:], k.part[:], -1.0, None, ALU.mult))
                link(v.tensor_copy(k.trash[:], k.trash_i[:]))
                link(v.tensor_scalar(k.ident[:], k.lane[:], k.part[:, 0:1], None, ALU.is_equal))
                link(v.tensor_scalar(k.before[:], k.lane[:], k.part[:, 0:1], None, ALU.is_lt))
                link(v.memset(k.ones[:], 1.0))
                link(v.memset(nought[:], 0.0))
                link(v.memset(k.is_node[:], 0.0))
                link(v.tensor_scalar(k.is_node[:, 0:1], k.part[:, 0:1], float(N - (RT - 1) * P), None, ALU.is_lt))
                v.wait_ge(loaded, 32)
                link(v.tensor_scalar(tiles[:], ends[:], 7, None, ALU.arith_shift_right))
                link(v.tensor_copy(tf[:], tiles[:]))
                link(v.tensor_tensor(length[:], tf[:, 1, :], tf[:, 0, :], ALU.subtract))
                link(v.tensor_scalar(length[:], length[:], 1.0, None, ALU.add))
                link(v.tensor_tensor_scan(upto[:], length[:], nought[:], 0.0, ALU.add, ALU.add))
                link(v.tensor_tensor(pair[:, 0, :], upto[:], length[:], ALU.subtract))
                link(v.memset(shift[:, 0:1], 0.0))
                link(v.tensor_tensor(shift[:, 1:ET + 1], tf[:, 0, :], pair[:, 0, :], ALU.subtract))
                link(v.tensor_tensor(pair[:, 1, :], shift[:, 1:ET + 1], shift[:, 0:ET], ALU.subtract))
                v.sem_inc(rows, 1)
                v.wait_ge(spread, 1)
                v.tensor_copy(wide[:, 1, 0:512], k.psum[:, 2, :])
                link(v.tensor_copy(wide[:, 1, 512:ET], k.psum[:, 3, 0:ET - 512]))
                v.wait_ge(copied, 2)
                for j in range(SB):
                    link(v.tensor_scalar(junk[:], wide[:, 0, :], step_no[:, j:j + 1], 0.0, ALU.is_le, ALU.add,
                                         accum_out=at_edge[:, j:j + 1]))
                link(v.tensor_scalar(edge_i[:], at_edge[:], -1.0, None, ALU.add))
                v.sem_inc(edges_known, 1)
                for j in range(SB):
                    link(v.scalar_tensor_tensor(out=junk[:], in0=wide[:, 0, :], scalar=step_no[:, j:j + 1], in1=wide[:, 1, :],
                                                op0=ALU.is_le, op1=ALU.mult, accum_out=at_node[:, j:j + 1]))
                link(v.tensor_tensor(at_node[:], at_node[:], step_no[:], ALU.add))
                link(v.tensor_scalar(base[:], at_node[:], -float(P), None, ALU.mult))
                link(v.tensor_copy(ek[:, 0, :], edge_i[:]))
                link(v.tensor_scalar(ek[:, 1, :], at_node[:], float(RT - 1), None, ALU.min))
                v.sem_inc(tables, 1)
                v.wait_ge(gathered, 16 * 2 * SB)
                link(v.tensor_scalar(loi[:], srcg[:], P - 1, None, ALU.bitwise_and))
                link(v.tensor_copy(lof[:], loi[:]))
                link(v.tensor_copy(srcf[:], srcg[:]))
                for j in range(SB):
                    link(v.tensor_scalar(relf[:, j, :], dstg[:, j, :], base[:, j:j + 1], None, ALU.add))
                link(v.tensor_copy(relh[:], relf[:]))
                v.sem_inc(conv, 3)
                for j in range(SB):
                    v.wait_ge(turned, 2 * j + 2)
                    link(v.tensor_copy(k.rel_cols[:, j * P:(j + 1) * P], k.psum[:, 2 * (j % 2), 0:P]))
                    link(v.tensor_copy(k.src_cols[:, j * P:(j + 1) * P], k.psum[:, 2 * (j % 2) + 1, 0:P]))
                    v.sem_inc(k.turn_free, 1)
                link(v.tensor_copy(k.src_idx[:], k.src_cols[:]))
                link(v.tensor_scalar(hi_idx[:], k.src_idx[:], 7, None, ALU.arith_shift_right))
                link(v.tensor_copy(k.hi_cols[:], hi_idx[:]))
                v.wait_ge(weighted, 16 * (len(RESIDENT) + len(ROWS_RESIDENT) + 10))
                link(v.tensor_tensor(k.table_b[:], k.b["L0_gnn_b1"][:], k.b["L0_gnn_be"][:], ALU.add))
                link(v.tensor_scalar(k.one_eps[:], k.one_eps[:], 1.0, None, ALU.add))
                link(v.tensor_scalar(k.b["L2_gnn_bq"][:], k.b["L2_gnn_bq"][:], HD ** -0.5, None, ALU.mult))
                link(v.memset(k.none[:], 0.0))

            @block.scalar
            def _(a):
                a.wait_ge(spread, 1)
                nc.scalar.copy(wide[:, 0, 0:512], k.psum[:, 0, :]).then_inc(copied, 1)
                nc.scalar.copy(wide[:, 0, 512:ET], k.psum[:, 1, 0:ET - 512]).then_inc(copied, 1)

            @block.tensor
            def _(pe):
                pe.wait_ge(rows, 1)
                for n in range(2):
                    for b, (first, past) in enumerate(((0, 512), (512, ET))):
                        mm = pe.matmul(k.psum[:, 2 * n + b, 0:past - first], k.ones[0:1, :], pair[0:1, n, first:past],
                                       start=True, stop=True)
                mm.then_inc(spread, 1)
                pe.wait_ge(conv, 3)
                for j in range(SB):
                    if j >= 2:
                        pe.wait_ge(k.turn_free, j - 1)
                    pe.transpose(k.psum[:, 2 * (j % 2), 0:P], relf[:, j, :], k.ident[:]).then_inc(turned, 1)
                    pe.transpose(k.psum[:, 2 * (j % 2) + 1, 0:P], srcf[:, j, :], k.ident[:]).then_inc(turned, 1)


SIZES = (4, 4, 2)
BASES = (0, 4, 8)
ROUND = sum(SIZES)
ROUNDS = NT // ROUND
NG = len(SIZES)


def phase_linear(nc, k, name, X, W, cols, bias, OUT, tables=(), also=None, scale=1.0, parts=None, extra=(),
                 storing=None, after=None):
    with ExitStack() as c:
        sb = lambda n, s, d: c.enter_context(nc.sbuf_tensor(name + n, s, d))
        sem = semaphores(nc, c, name)
        tile = sb("_tile", [P, NG, 4, P], F32)
        tile_t = sb("_tile_t", [P, NG, 4, P], F32)
        staged, turned, copied, product, added, stored = (
            sem(n) for n in ("_staged", "_turned", "_copied", "_product", "_added", "_stored"))
        parted = [sem(f"_parted{n}") for n in range(3)]
        reduced = [sem(f"_reduced{n}") for n in range(2)]
        stored = storing or stored
        transfers = 16 * (len(tables) * NG * ROUNDS + len(extra))
        kinds = [(bias, OUT)] + [(b, to) for b, to, _ in tables if to is not None]
        kinds += [(bias, also)] if also is not None else []
        tiles = lambda i, j: bass.ds(ROUND * i + BASES[j], SIZES[j])
        fit = 512 // cols
        banks = (3, 5, 7) if cols > P else (3, 4, 5)

        with nc.Block() as block:
            @block.vector
            def _(v):
                v.sem_inc(added, NG * len(kinds))

                def stage(i, j):
                    v.tensor_copy(tile[:, j, 0:SIZES[j], :], X[:, tiles(i, j), :]).then_inc(staged, 1)

                def add(i, j):
                    v.wait_ge(product, NG * i + j + 1 + NG)
                    if after:
                        v.wait_ge(*after)
                    for b, to in kinds:
                        for at in range(0, SIZES[j], fit):
                            n = min(fit, SIZES[j] - at)
                            to_n = to[:, bass.ds(ROUND * i + BASES[j] + at, n), :]
                            of_n = k.psum[:, banks[j] + at // fit, 0:n * cols].rearrange("p (t d) -> p t d", d=cols)
                            b_n = b.unsqueeze(1).to_broadcast([P, n, cols])
                            if scale == 1.0:
                                ins = v.tensor_tensor(to_n, of_n, b_n, ALU.add)
                            else:
                                ins = v.scalar_tensor_tensor(out=to_n, in0=of_n, scalar=scale, in1=b_n, op0=ALU.mult, op1=ALU.add)
                        ins.then_inc(added, 1)

                def take_off(part):
                    def take(i, j):
                        v.wait_ge(parted[part], NG * i + j + 1)
                        v.tensor_tensor(OUT[:, tiles(i, j), :], OUT[:, tiles(i, j), :], parts[:, tiles(i, j), part, :],
                                        ALU.subtract).then_inc(reduced[part], 1)
                    return take

                if parts is None:
                    pipeline(v, ROUNDS, NG, stage, add, lags=(0, 2))
                else:
                    pipeline(v, ROUNDS, NG, stage, add, take_off(0), take_off(1), lags=(0, 2, 4, 6))

            @block.tensor
            def _(pe):
                pe.sem_inc(product, NG)

                def turn(i, j):
                    n = NG * i + j
                    pe.wait_ge(staged, n + 1)
                    pe.wait_ge(copied, n + 1)
                    for q in range(SIZES[j]):
                        mm = pe.transpose(k.psum[:, j, q * P:(q + 1) * P], tile[:, j, q, :], k.ident[:])
                    mm.then_inc(turned, 1)

                def multiply(i, j):
                    n = NG * i + j
                    pe.wait_ge(copied, n + 1 + NG)
                    pe.wait_ge(added, len(kinds) * (n + 1))
                    for q in range(SIZES[j]):
                        mm = pe.matmul(k.psum[:, banks[j] + q // fit, (q % fit) * cols:(q % fit + 1) * cols],
                                       tile_t[:, j, q, :], W, start=True, stop=True)
                    mm.then_inc(product, 1)

                pipeline(pe, ROUNDS, NG, turn, multiply)

            @block.scalar
            def _(a):
                a.sem_inc(copied, NG)

                def copy(i, j):
                    n = NG * i + j
                    a.wait_ge(turned, n + 1)
                    a.wait_ge(product, n + 1)
                    nc.scalar.copy(tile_t[:, j, 0:SIZES[j], :].rearrange("p q d -> p (q d)"),
                                   k.psum[:, j, 0:SIZES[j] * P]).then_inc(copied, 1)

                def make(part):
                    def make_part(i, j):
                        if part == 0:
                            a.wait_ge(added, len(kinds) * (NG * i + j + 1 + NG))
                        else:
                            a.wait_ge(reduced[part - 1], NG * i + j + 1)
                        nc.scalar.copy(parts[:, tiles(i, j), part, :], OUT[:, tiles(i, j), :]).then_inc(parted[part], 1)
                    return make_part

                if parts is None:
                    pipeline(a, ROUNDS, NG, copy)
                else:
                    pipeline(a, ROUNDS, NG, copy, make(0), make(1), make(2), lags=(0, 3, 5, 7))

            @block.sync
            def _(sp):
                for to, of in extra:
                    sp.dma_start(to, of).then_inc(stored, 16)
                if tables:
                    def store(i, j):
                        sp.wait_ge(added, len(kinds) * (NG * i + j + 1 + NG))
                        for _, to, table in tables:
                            sp.dma_start(table[:, tiles(i, j), :], (OUT if to is None else to)[:, tiles(i, j), :]
                                         ).then_inc(stored, 16)

                    pipeline(sp, ROUNDS, NG, store)
                if (tables or extra) and storing is None:
                    sp.wait_ge(stored, transfers)
    return transfers


def vector_chain(sem, v):
    n = [0]

    def link(ins):
        n[0] += 1
        ins.then_inc(sem, 1)
        v.wait_ge(sem, n[0])
    return link


class Norm:
    CUTS = (slice(0, NT // 2), slice(NT // 2, NT))

    def __init__(self, nc, c, sem, name):
        self.nc = nc
        sb = lambda n: c.enter_context(nc.sbuf_tensor(name + n, [P, NT], F32))
        self.mean, self.var, self.root = sb("mean"), sb("var"), sb("root")
        self.centred, self.squared, self.ask, self.rooted, self.done = (
            sem(n) for n in ("centred", "squared", "ask", "rooted", "done"))

    def vector(self, link, v, Y, OUT):
        mean, var = self.mean[:], self.var[:]
        wide = lambda col, cut: col[:, cut].unsqueeze(2).to_broadcast([P, NT // 2, D])
        link(v.tensor_reduce(mean, Y, AX.X, ALU.add))
        link(v.tensor_scalar(mean, mean, 1.0 / D, None, ALU.mult))
        for cut in self.CUTS:
            v.tensor_tensor(Y[:, cut, :], Y[:, cut, :], wide(mean, cut), ALU.subtract).then_inc(self.centred, 1)
        for n, cut in enumerate(self.CUTS):
            v.wait_ge(self.squared, n + 1)
            link(v.tensor_reduce(var[:, cut], OUT[:, cut, :], AX.X, ALU.add))
        link(v.tensor_scalar(var, var, 1.0 / D, EPS, ALU.mult, ALU.add))
        v.sem_inc(self.ask, 1)
        v.wait_ge(self.rooted, 1)
        link(v.reciprocal(var, self.root[:]))
        for cut in self.CUTS:
            v.tensor_tensor(OUT[:, cut, :], Y[:, cut, :], wide(var, cut), ALU.mult).then_inc(self.done, 1)

    def scalar(self, a, Y, OUT):
        for n, cut in enumerate(self.CUTS):
            a.wait_ge(self.centred, n + 1)
            self.nc.scalar.activation(OUT[:, cut, :], Y[:, cut, :], ACT.Square).then_inc(self.squared, 1)
        a.wait_ge(self.ask, 1)
        self.nc.scalar.activation(self.root[:], self.var[:], ACT.Sqrt).then_inc(self.rooted, 1)


def phase_conv_edges(nc, k, table, agg, room, before):
    with ExitStack() as c:
        sb = lambda n, s, d: c.enter_context(nc.sbuf_tensor("c0_" + n, s, d))
        sem = semaphores(nc, c, "c0_")
        idx = sb("idx", [P, U], I32)
        ea = room[:, 0:U * P].rearrange("p (u e) -> p u e", e=P)
        rows = room[:, U * P:U * (P + D)].rearrange("p (u d) -> p u d", d=D)
        msg = sb("msg", [P, 2, G, D], F32)
        oh = sb("oh", [P, 2, G, P], F32)
        ea_in = [sem(f"ea_in{u}") for u in range(U)]
        row_in = k.row_in
        ea_free, row_free, idx_ready, pool_turn = sem("ea_free"), sem("row_free"), sem("idx_ready"), sem("pool_turn")
        product, summed, msg_ready, oh_ready, spread, added, zero = (
            sem(n) for n in ("product", "summed", "msg_ready", "oh_ready", "spread", "added", "zero"))
        with nc.Block() as block:
            @block.sync
            def _(sp):
                with sp.Fori(0, ITERS) as i:
                    tile = load_steps(nc, sp, k.ek[0], i * U, ET - 1)
                    for u in range(U):
                        if u % G == 0:
                            sp.wait_ge(ea_free, GROUPS * i + u // G + 1)
                        sp.dma_start(ea[:, u, :], k.ea_t[:, bass.ds(tile[u] * P, P)]).then_inc(ea_in[u], 16)

            @block.gpsimd
            def _(g):
                with g.Fori(0, ITERS) as i:
                    for u in range(U):
                        if u % G == 0:
                            g.wait_ge(idx_ready, GROUPS * i + u // G + 1)
                            g.wait_ge(row_free, GROUPS * i + u // G + 1)
                            g.sem_inc(pool_turn, 1)
                        g.indirect_dma_start(out=rows[:, u, :], out_offset=None, in_=table,
                                             in_offset=bass.IndirectOffsetOnAxis(ap=idx[:, u:u + 1], axis=0)
                                             ).then_inc(row_in[u], 16)

            @block.tensor
            def _(pe):
                pe.sem_inc(ea_free, GROUPS)
                pe.sem_inc(spread, 2)

                def edge_product(i, j):
                    pe.wait_ge(summed, GROUPS * i + j + 1)
                    for q in range(G):
                        pe.wait_ge(ea_in[G * j + q], 16 * i + 16)
                        mm = pe.matmul(k.psum[:, j % 2, q * D:(q + 1) * D], ea[:, G * j + q, :], k.w["L0_gnn_wet"][:],
                                       start=True, stop=True)
                        if q == G - 1:
                            mm.then_inc(product, 1)
                    pe.wait_ge(product, GROUPS * i + j + 1)
                    pe.sem_inc(ea_free, 1)

                def sum_into_nodes(i, j):
                    pe.wait_ge(msg_ready, GROUPS * i + j + 1)
                    pe.wait_ge(oh_ready, GROUPS * i + j + 1)
                    pe.wait_ge(added, G * (GROUPS * i + j) + G)
                    for q in range(G):
                        mm = pe.matmul(k.psum[:, 2 + j % 2, q * D:(q + 1) * D], oh[:, j % 2, q, :], msg[:, j % 2, q, :],
                                       start=True, stop=True)
                    mm.then_inc(spread, 1)

                pipeline(pe, ITERS, GROUPS, edge_product, sum_into_nodes)

            @block.scalar
            def _(a):
                with a.Fori(0, ITERS) as i:
                    for j in range(GROUPS):
                        a.wait_ge(summed, GROUPS * i + j + 3)
                        nc.scalar.activation(msg[:, j % 2], msg[:, j % 2], ACT.Silu).then_inc(msg_ready, 1)

            @block.vector
            def _(v):
                v.memset(agg, 0.0).then_inc(zero, 1)
                v.wait_ge(zero, 1)
                v.sem_inc(summed, 2)
                v.sem_inc(row_free, GROUPS)
                v.sem_inc(added, 2 * G)

                def stage(i, j):
                    v.tensor_copy(idx[:, G * j:G * j + G], k.src_idx[:, bass.ds(i * U + G * j, G)]).then_inc(idx_ready, 1)

                for j in range(GROUPS):
                    stage(0, j)

                def front(i, j):
                    v.wait_ge(spread, GROUPS * i + j + 1)
                    v.tensor_tensor(oh[:, j % 2], k.lane[:].unsqueeze(1).to_broadcast([P, G, P]),
                                    k.rel_cols[:, bass.ds(i * U + G * j, G)].unsqueeze(2).to_broadcast([P, G, P]),
                                    ALU.is_equal).then_inc(oh_ready, 1)
                    v.wait_ge(product, GROUPS * i + j + 1)
                    for q in range(G):
                        v.wait_ge(row_in[G * j + q], 16 * i + 16 * (before + 1))
                    v.tensor_tensor(msg[:, j % 2].rearrange("p q d -> p (q d)"), k.psum[:, j % 2, :],
                                    rows[:, G * j:G * j + G, :].rearrange("p q d -> p (q d)"), ALU.add).then_inc(summed, 1)
                    v.wait_ge(summed, GROUPS * i + j + 3)
                    v.sem_inc(row_free, 1)
                    stage(i + 1, j)

                regs = {}

                def back(i, j):
                    if j == 0:
                        regs["node"] = load_steps(nc, v, k.ek[1], i * U, RT - 1)
                    v.wait_ge(spread, GROUPS * i + j + 3)
                    for q in range(G):
                        t = regs["node"][G * j + q]
                        v.wait_ge(added, G * (GROUPS * i + j) + q + 2 * G)
                        v.tensor_tensor(agg[:, bass.ds(t, 1), :], agg[:, bass.ds(t, 1), :],
                                        k.psum[:, 2 + j % 2:3 + j % 2, q * D:(q + 1) * D], ALU.add).then_inc(added, 1)

                pipeline(v, ITERS, GROUPS, front, back, loads=1)


def phase_conv_nodes(nc, k, H, Y, S1):
    with ExitStack() as c:
        sb = lambda n, s, d: c.enter_context(nc.sbuf_tensor("n0_" + n, s, d))
        sem = semaphores(nc, c, "n0_")
        norm = Norm(nc, c, sem, "n0_")
        total = sb("total", [P, 2, D], F32)
        stat = sb("stat", [P, 3, D], F32)
        chain, ask, activated, centred, squared, ask_root, rooted, x_used, x_biased, want, have = (
            sem(n) for n in ("graph_chain", "graph_ask", "activated", "graph_centred", "graph_squared", "graph_ask_root",
                             "graph_rooted", "x_used", "x_biased", "want", "have"))
        wide = [P, NT, D]
        with nc.Block() as block:
            @block.vector
            def _(v):
                link = vector_chain(chain, v)
                for cut in norm.CUTS:
                    v.scalar_tensor_tensor(out=Y[:, cut, :], in0=H[:, cut, :], scalar=k.one_eps[:, 0:1], in1=Y[:, cut, :],
                                           op0=ALU.mult, op1=ALU.add).then_inc(ask, 1)
                for n, cut in enumerate(norm.CUTS):
                    v.wait_ge(activated, n + 1)
                    link(v.tensor_tensor(Y[:, cut, :], S1[:, cut, :], k.X[:, cut, :], ALU.add))
                v.sem_inc(x_used, 1)
                link(v.tensor_tensor(Y[:, RT - 1:NT, :], Y[:, RT - 1:NT, :],
                                     k.is_node[:].unsqueeze(2).to_broadcast([P, NT - RT + 1, D]), ALU.mult))
                link(v.tensor_reduce(total[:, 0, :], Y.rearrange("p t d -> p d t"), AX.X, ALU.add))
                v.sem_inc(want, 1)
                v.wait_ge(have, 1)
                link(v.scalar_tensor_tensor(out=stat[:, 0, :], in0=k.psum[:, 0, 0:D], scalar=1.0 / N,
                                            in1=k.b["L0_gnn_gn_mean_scale"][:], op0=ALU.mult, op1=ALU.mult))
                for cut in norm.CUTS:
                    v.tensor_tensor(Y[:, cut, :], Y[:, cut, :], stat[:, 0, :].unsqueeze(1).to_broadcast([P, NT // 2, D]),
                                    ALU.subtract).then_inc(centred, 1)
                v.wait_ge(squared, 2)
                link(v.tensor_tensor(S1[:, RT - 1:NT, :], S1[:, RT - 1:NT, :],
                                     k.is_node[:].unsqueeze(2).to_broadcast([P, NT - RT + 1, D]), ALU.mult))
                link(v.tensor_reduce(total[:, 1, :], S1.rearrange("p t d -> p d t"), AX.X, ALU.add))
                v.sem_inc(want, 1)
                v.wait_ge(have, 2)
                link(v.tensor_scalar(stat[:, 1, :], k.psum[:, 1, 0:D], 1.0 / N, EPS, ALU.mult, ALU.add))
                v.sem_inc(ask_root, 1)
                v.wait_ge(rooted, 1)
                link(v.reciprocal(stat[:, 1, :], stat[:, 2, :]))
                link(v.tensor_tensor(stat[:, 1, :], stat[:, 1, :], k.b["L0_gnn_gn_weight"][:], ALU.mult))
                link(v.tensor_tensor(Y, Y, stat[:, 1, :].unsqueeze(1).to_broadcast(wide), ALU.mult))
                v.wait_ge(x_biased, 1)
                link(v.tensor_tensor(Y, Y, k.X[:], ALU.add))
                norm.vector(link, v, Y, k.X[:])

            @block.scalar
            def _(a):
                for n, cut in enumerate(norm.CUTS):
                    a.wait_ge(ask, n + 1)
                    nc.scalar.activation(S1[:, cut, :], Y[:, cut, :], ACT.Silu).then_inc(activated, 1)
                for n, cut in enumerate(norm.CUTS):
                    a.wait_ge(centred, n + 1)
                    nc.scalar.activation(S1[:, cut, :], Y[:, cut, :], ACT.Square).then_inc(squared, 1)
                a.wait_ge(ask_root, 1)
                nc.scalar.activation(stat[:, 2, :], stat[:, 1, :], ACT.Sqrt).then_inc(rooted, 1)
                norm.scalar(a, Y, k.X[:])

            @block.gpsimd
            def _(g):
                g.wait_ge(x_used, 1)
                g.tensor_tensor(k.X[:], k.X[:], k.b["L0_gnn_gn_bias"][:].unsqueeze(1).to_broadcast(wide), ALU.add).then_inc(x_biased, 1)

            @block.tensor
            def _(pe):
                for n in range(2):
                    pe.wait_ge(want, n + 1)
                    pe.matmul(k.psum[:, n, 0:D], k.ones[:], total[:, n, :], start=True, stop=True).then_inc(have, 1)


def phase_scores_nodes(nc, k, Hs, S, S2):
    with ExitStack() as c:
        sem = semaphores(nc, c, "s1_")
        score = c.enter_context(nc.sbuf_tensor("s1_score", [P, 2, NT], F32))
        chain, multiplied = sem("chain"), sem("multiplied")
        block = c.enter_context(nc.Block())
        a_w = [k.b["L1_gnn_a_w"][:, n * D:(n + 1) * D].unsqueeze(1).to_broadcast([P, NT, D]) for n in range(2)]

        @block.gpsimd
        def _(g):
            g.tensor_tensor(S2, Hs, a_w[1], ALU.mult).then_inc(multiplied, 1)

        @block.vector
        def _(v):
            link = vector_chain(chain, v)
            link(v.tensor_tensor(S, Hs, a_w[0], ALU.mult))
            link(v.tensor_reduce(score[:, 0, :], S, AX.X, ALU.add))
            v.wait_ge(multiplied, 1)
            link(v.tensor_reduce(score[:, 1, :], S2, AX.X, ALU.add))
            for n, parts in enumerate((k.src_score, k.dst_score)):
                for part in range(3):
                    link(v.tensor_copy(parts[:, :, part], score[:, n, :]))
                    if part < 2:
                        link(v.tensor_tensor(score[:, n, :], score[:, n, :], parts[:, :, part], ALU.subtract))


def phase_scores_edges(nc, k, scores, room, room16):
    G8, LONG = 8, 2 * U
    PER = LONG // G8
    TURNS = STEPS // LONG
    WIDE = NT + 3
    with ExitStack() as c:
        sem = semaphores(nc, c, "s_")
        rel, lo, is_rel, is_lo = (room16[:, n * LONG * P:(n + 1) * LONG * P].rearrange("p (j e) -> p j e", j=PER)
                                  for n in range(4))
        size = PER * G8 * WIDE
        away = room[:, 2 * size:2 * size + PER * G8 * P].rearrange("p (j e) -> p j e", j=PER)
        mask, picked = (room[:, n * size:(n + 1) * size].rearrange("p (j q n) -> p j q n", j=PER, q=G8) for n in range(2))
        rel_in = [sem(f"rel_in{n}") for n in range(PER)]
        lo_in = [sem(f"lo_in{n}") for n in range(PER)]
        rel_used, lo_used, lo_ready, mask_ready, product, read, reduced, preset, sp_turn = (
            sem(n) for n in ("rel_used", "lo_used", "lo_ready", "mask_ready", "product", "read", "reduced", "preset", "sp_turn"))
        rel_flat = k.rel_rows.rearrange("(o s) e -> o (s e)", o=1)
        lo_flat = k.lo_rows.rearrange("(o s) e -> o (s e)", o=1)
        with nc.Block() as block:
            @block.sync
            def _(sp):
                with sp.Fori(0, TURNS) as i:
                    for j in range(PER):
                        at = bass.ds(sp.snap((i * LONG + j * G8) * P), G8 * P)
                        sp.wait_ge(rel_used, PER * i + j + 1)
                        sp.sem_inc(sp_turn, 1)
                        sp.dma_start(rel[:, j, :], rel_flat[:, at].to_broadcast([P, G8 * P])).then_inc(rel_in[j], 16)
                        sp.wait_ge(lo_used, PER * i + j + 1)
                        sp.sem_inc(sp_turn, 1)
                        sp.dma_start(lo[:, j, :], lo_flat[:, at].to_broadcast([P, G8 * P])).then_inc(lo_in[j], 16)

            @block.tensor
            def _(pe):
                with pe.Fori(0, TURNS) as i:
                    for j in range(PER):
                        if j * G8 % U == 0:
                            node = load_steps(nc, pe, k.ek[1], i * LONG + j * G8, RT - 1)
                        pe.wait_ge(rel_used, PER * i + j + 1 + PER)
                        pe.wait_ge(lo_ready, PER * i + j + 1 + PER)
                        pe.wait_ge(read, PER * i + j + 1)
                        for q in range(G8):
                            cols = k.psum[:, j, q * WIDE:(q + 1) * WIDE]
                            for part in range(3):
                                pe.matmul(cols[:, 0:NT], is_lo[:, j, q * P:(q + 1) * P], k.src_score[:, :, part],
                                          start=(part == 0), stop=(part == 2))
                            mm = pe.matmul(cols[:, NT:WIDE], is_rel[:, j, q * P:(q + 1) * P],
                                           k.dst_score[:, bass.ds(node[j * G8 % U + q], 1), :], start=True, stop=True)
                        mm.then_inc(product, 1)

            @block.scalar
            def _(a):
                a.sem_inc(product, PER)
                a.sem_inc(lo_ready, PER)

                def distance(i, j):
                    a.wait_ge(lo_in[j], 16 * i + 16)
                    a.wait_ge(lo_ready, PER * i + j + 1)
                    nc.scalar.activation(away[:, j, :], lo[:, j, :], ACT.Abs, bias=k.minus_part[:, 0:1]).then_inc(lo_used, 1)

                def is_nought(i, j):
                    a.wait_ge(product, PER * i + j + 1)
                    a.wait_ge(lo_used, PER * i + j + 1 + PER)
                    nc.scalar.activation(is_lo[:, j, :], away[:, j, :], ACT.Relu, bias=k.ones[:, 0:1], scale=-1.0).then_inc(lo_ready, 1)

                pipeline(a, TURNS, PER, distance, is_nought)

            @block.vector
            def _(v):
                v.memset(mask[:, :, :, NT:WIDE], 1.0).then_inc(preset, 1)
                v.sem_inc(rel_used, PER)
                v.sem_inc(lo_used, PER)
                v.sem_inc(read, PER)
                v.wait_ge(preset, 1)

                def matrices(i, j):
                    v.wait_ge(rel_in[j], 16 * i + 16)
                    v.tensor_scalar(is_rel[:, j, :], rel[:, j, :], k.part[:, 0:1], None, ALU.is_equal).then_inc(rel_used, 1)

                def make_mask(i, j):
                    v.tensor_tensor(mask[:, j, :, 0:NT], k.lane[:, 0:NT].unsqueeze(1).to_broadcast([P, G8, NT]),
                                    k.hi_cols[:, bass.ds(i * LONG + G8 * j, G8)].unsqueeze(2).to_broadcast([P, G8, NT]),
                                    ALU.is_equal).then_inc(mask_ready, 1)

                def pick(i, j):
                    n = PER * i + j
                    v.wait_ge(product, n + 1 + PER)
                    v.wait_ge(mask_ready, n + 1)
                    v.tensor_tensor(picked[:, j].rearrange("p q n -> p (q n)"), k.psum[:, j, 0:G8 * WIDE],
                                    mask[:, j].rearrange("p q n -> p (q n)"), ALU.mult).then_inc(read, 1)

                def reduce(i, j):
                    n = PER * i + j
                    v.wait_ge(read, n + 1 + PER)
                    v.tensor_reduce(scores[:, bass.ds(i * LONG + G8 * j, G8)], picked[:, j], AX.X, ALU.add).then_inc(reduced, 1)

                pipeline(v, TURNS, PER, reduce, matrices, pick, make_mask, lags=(2, 0, 1, 0))
                v.wait_ge(reduced, PER * TURNS)


def phase_softmax(nc, k, scores):
    with ExitStack() as c:
        sb = lambda n, s, d: c.enter_context(nc.sbuf_tensor("x_" + n, s, d))
        sem = semaphores(nc, c, "x_")
        a = sb("a", [P, STEPS], F32)
        live = sb("live", [P, STEPS], F32)
        m = sb("m", [P, 8], F32)
        landed, chain, ask, told, expd = (sem(n) for n in ("landed", "chain", "ask", "told", "expd"))
        rel, src, e = k.rel_cols[:, 0:STEPS], k.src_cols[:, 0:STEPS], scores[:, 0:STEPS]
        with nc.Block() as block:
            @block.sync
            def _(sp):
                sp.dma_start(m[:, 0:1], k.small["L1_gnn_a_b"].to_broadcast([P, 1])).then_inc(landed, 16)
                sp.wait_ge(landed, 16)

            @block.vector
            def _(v):
                link = vector_chain(chain, v)
                v.wait_ge(landed, 16)
                link(v.tensor_scalar(live[:], rel, 0.0, None, ALU.is_ge))
                link(v.scalar_tensor_tensor(out=live[:], in0=rel, scalar=float(P), in1=live[:], op0=ALU.is_lt, op1=ALU.mult))
                link(v.scalar_tensor_tensor(out=live[:], in0=src, scalar=float(N), in1=live[:], op0=ALU.is_lt, op1=ALU.mult))
                link(v.tensor_scalar(e, e, m[:, 0:1], None, ALU.add))
                link(v.tensor_scalar(a[:], e, 0.01, None, ALU.mult))
                link(v.tensor_tensor(e, e, a[:], ALU.max))
                link(v.tensor_tensor(e, e, live[:], ALU.mult))
                link(v.tensor_scalar(a[:], live[:], -1.0, -NEG, ALU.add, ALU.mult))
                link(v.tensor_tensor(e, e, a[:], ALU.add))
                link(v.tensor_reduce(m[:, 1:2], e, AX.X, ALU.max))
                v.sem_inc(ask, 1)
                v.wait_ge(told, 1)
                link(v.tensor_reduce(m[0:1, 2:3], k.psum[0:1, 0, 0:P], AX.X, ALU.max))
                v.sem_inc(ask, 1)
                v.wait_ge(told, 2)
                link(v.tensor_scalar(m[:, 3:4], k.psum[:, 1, 0:1], -1.0, None, ALU.mult))
                v.sem_inc(ask, 1)
                v.wait_ge(told, 3)
                link(v.reciprocal(m[:, 5:6], k.psum[:, 2, 0:1]))
                link(v.tensor_scalar(e, e, m[:, 5:6], None, ALU.mult))

            @block.scalar
            def _(act):
                act.wait_ge(ask, 3)
                nc.scalar.activation(e, e, ACT.Exp, bias=m[:, 3:4], accum_out=m[:, 4:5]).then_inc(expd, 1)

            @block.tensor
            def _(pe):
                pe.wait_ge(ask, 1)
                pe.matmul(k.psum[0:1, 0, 0:P], m[:, 1:2], k.ident[:], start=True, stop=True).then_inc(told, 1)
                pe.wait_ge(ask, 2)
                pe.matmul(k.psum[:, 1, 0:1], k.ones[0:1, :], m[0:1, 2:3], start=True, stop=True).then_inc(told, 1)
                pe.wait_ge(expd, 1)
                pe.matmul(k.psum[:, 2, 0:1], k.ones[:], m[:, 4:5], start=True, stop=True).then_inc(told, 1)


def phase_attend(nc, k, weights, H3, accs, room):
    with ExitStack() as c:
        sb = lambda n, s, d: c.enter_context(nc.sbuf_tensor("a_" + n, s, d))
        sem = semaphores(nc, c, "a_")
        rel = sb("rel", [P, GROUPS, G * P], BF16)
        out_rows = room[:, 0:U * D].rearrange("p (u d) -> p u d", d=D)
        src = room[:, U * D:2 * U * D].rearrange("p (j e) -> p j e", j=GROUPS)
        same, msg = (room[:, 2 * U * D + n * U * P:2 * U * D + (n + 1) * U * P].rearrange("p (j q e) -> p j q e", j=GROUPS, q=G)
                     for n in range(2))
        oht = sb("oht", [P, GROUPS, G * P], BF16)
        col = sb("col", [P, GROUPS, 2, G], F32)
        junk = sb("junk", [P, P], F32)
        count = sb("count", [P, GROUPS, G], F32)
        away = sb("away", [P, GROUPS, G], F32)
        idx = sb("idx", [P, U], I32)
        zero = sb("zero", [P, D], F32)
        rel_in = [sem(f"rel_in{n}") for n in range(GROUPS)]
        src_in = [sem(f"src_in{n}") for n in range(GROUPS)]
        acc_done = k.acc_done
        zeroed, oht_ready, same_ready, product, msg_ready, merged, rows_ready, idx_ready, rows_free, pool_turn, chain, col_ready = (
            sem(n) for n in ("zeroed", "oht_ready", "same_ready", "product", "msg_ready", "merged", "rows_ready",
                             "idx_ready", "rows_free", "pool_turn", "chain", "col_ready"))
        sp_turn = sem("sp_turn")
        rel_flat = k.rel_rows.rearrange("(o s) e -> o (s e)", o=1)
        src_flat = k.src_rows.rearrange("(o s) e -> o (s e)", o=1)
        with nc.Block() as block:
            @block.sync
            def _(sp):
                with sp.Fori(0, ITERS) as i:
                    for j in range(GROUPS):
                        at = bass.ds(sp.snap((i * U + j * G) * P), G * P)
                        sp.wait_ge(oht_ready, GROUPS * i + j + 1)
                        sp.sem_inc(sp_turn, 1)
                        sp.dma_start(rel[:, j, :], rel_flat[:, at].to_broadcast([P, G * P])).then_inc(rel_in[j], 16)
                        sp.wait_ge(same_ready, GROUPS * i + j + 1)
                        sp.sem_inc(sp_turn, 1)
                        sp.dma_start(src[:, j, :], src_flat[:, at].to_broadcast([P, G * P])).then_inc(src_in[j], 16)

            @block.vector
            def _(v):
                v.memset(zero[:], 0.0).then_inc(zeroed, 1)
                v.sem_inc(oht_ready, GROUPS)
                v.sem_inc(same_ready, GROUPS)
                with v.Fori(0, ITERS) as i:
                    for j in range(GROUPS):
                        h, n = j, GROUPS * i + j
                        steps = bass.ds(i * U + G * j, G)
                        v.wait_ge(merged, n + 1)
                        v.tensor_copy(col[:, h, 0, :], weights[:, steps]).then_inc(col_ready, 1)
                        v.tensor_copy(col[:, h, 1, :], k.src_cols[:, steps]).then_inc(col_ready, 1)
                        v.wait_ge(rel_in[j], 16 * i + 16)
                        v.tensor_scalar(oht[:, h, :], rel[:, j, :], k.part[:, 0:1], None, ALU.is_equal).then_inc(oht_ready, 1)
                        v.wait_ge(src_in[j], 16 * i + 16)
                        v.wait_ge(col_ready, 2 * n + 2)
                        rows = src[:, j, :].rearrange("p (q e) -> p q e", e=P)
                        for q in range(G):
                            v.scalar_tensor_tensor(out=junk[:], in0=rows[:, q, :], scalar=col[:, h, 1, q:q + 1], in1=k.before[:],
                                                   op0=ALU.is_equal, op1=ALU.mult,
                                                   accum_out=count[:, h, q:q + 1]).then_inc(chain, 1)
                            v.wait_ge(chain, 7 * n + q + 1)
                        v.tensor_tensor(away[:, h], k.trash[:], col[:, h, 1, :], ALU.subtract).then_inc(chain, 1)
                        v.tensor_tensor(same[:, h], rows, col[:, h, 1, :].unsqueeze(2).to_broadcast([P, G, P]),
                                        ALU.is_equal).then_inc(same_ready, 1)
                        v.wait_ge(chain, 7 * n + 5)
                        v.scalar_tensor_tensor(out=away[:, h], in0=count[:, h], scalar=0.0, in1=away[:, h],
                                               op0=ALU.is_gt, op1=ALU.mult).then_inc(chain, 1)
                        v.wait_ge(chain, 7 * n + 6)
                        v.wait_ge(rows_free, n + 1)
                        v.tensor_tensor(idx[:, G * j:G * j + G], away[:, h], col[:, h, 1, :], ALU.add).then_inc(chain, 1)
                        v.wait_ge(chain, 7 * n + 7)
                        v.sem_inc(idx_ready, 1)

            @block.tensor
            def _(pe):
                pe.sem_inc(merged, GROUPS)
                regs = {}

                def expand(i, j):
                    if j == 0:
                        regs["node"] = load_steps(nc, pe, k.ek[1], i * U, RT - 1)
                    n = GROUPS * i + j
                    pe.wait_ge(oht_ready, n + 1 + GROUPS)
                    pe.wait_ge(msg_ready, n + 1)
                    for q in range(G):
                        for part in range(3):
                            mm = pe.matmul(k.psum[:, j, q * D:(q + 1) * D], oht[:, j, q * P:(q + 1) * P],
                                           H3[:, bass.ds(regs["node"][G * j + q], 1), part, :],
                                           start=(part == 0), stop=(part == 2))
                    mm.then_inc(product, 1)

                def merge(i, j):
                    n = GROUPS * i + j
                    pe.wait_ge(msg_ready, n + 1 + GROUPS)
                    pe.wait_ge(same_ready, n + 1 + GROUPS)
                    pe.wait_ge(rows_ready, n + 1)
                    for q in range(G):
                        mm = pe.matmul(k.psum[:, GROUPS + j, q * D:(q + 1) * D], same[:, j, q, :], msg[:, j, q, :],
                                       start=True, stop=True)
                    mm.then_inc(merged, 1)

                pipeline(pe, ITERS, GROUPS, expand, merge)

            @block.scalar
            def _(a):
                a.sem_inc(msg_ready, GROUPS)
                a.sem_inc(rows_ready, GROUPS)

                def scale(i, j):
                    n = GROUPS * i + j
                    a.wait_ge(product, n + 1)
                    a.wait_ge(col_ready, 2 * n + 2)
                    a.wait_ge(merged, n + 1)
                    for q in range(G):
                        ins = nc.scalar.activation(msg[:, j, q, :], k.psum[:, j, q * D:(q + 1) * D], ACT.Copy,
                                                   scale=col[:, j, 0, q:q + 1])
                    ins.then_inc(msg_ready, 1)

                def copy(i, j):
                    n = GROUPS * i + j
                    a.wait_ge(merged, n + 1 + GROUPS)
                    a.wait_ge(rows_free, n + 1)
                    nc.scalar.copy(out_rows[:, G * j:G * j + G, :].rearrange("p q d -> p (q d)"),
                                   k.psum[:, GROUPS + j, :]).then_inc(rows_ready, 1)

                pipeline(a, ITERS, GROUPS, scale, copy)

            @block.gpsimd
            def _(g):
                g.sem_inc(rows_free, GROUPS - 1)
                g.wait_ge(zeroed, 1)
                for n in range(ACCS):
                    g.dma_start(accs[n].rearrange("(t p) d -> p t d", p=P),
                                zero[:].unsqueeze(1).to_broadcast([P, AROWS // P, D])).then_inc(acc_done[n], 16)
                with g.Fori(0, ITERS) as i:
                    for u in range(U):
                        n = GROUPS * i + u // G
                        if u % G == 0:
                            g.wait_ge(idx_ready, n + 1)
                            g.wait_ge(rows_ready, n + 1 + GROUPS)
                        g.wait_ge(acc_done[u % ACCS], 16 * ((U // ACCS) * i + u // ACCS + 1))
                        g.sem_inc(rows_free if u % G == G - 1 else pool_turn, 1)
                        g.indirect_dma_start(out=accs[u % ACCS], out_offset=bass.IndirectOffsetOnAxis(ap=idx[:, u:u + 1], axis=0),
                                             in_=out_rows[:, u, :], in_offset=None, compute_op=ALU.add
                                             ).then_inc(acc_done[u % ACCS], 16)
                for n in range(ACCS):
                    g.wait_ge(acc_done[n], 16 * (STEPS // ACCS + 1))


def phase_attend_nodes(nc, k, accs, Y, S, Z):
    with ExitStack() as c:
        sem = semaphores(nc, c, "b_")
        norm = Norm(nc, c, sem, "b_")
        landed = [sem(f"landed{n}") for n in range(ACCS)]
        chain = sem("chain")
        bufs = [Y, S, *Z]
        with nc.Block() as block:
            @block.sync
            def _(sp):
                for n in range(ACCS):
                    sp.dma_start(bufs[n], accs[n][0:NP, :].rearrange("(t p) d -> p t d", p=P)).then_inc(landed[n], 16)

            @block.vector
            def _(v):
                link = vector_chain(chain, v)
                for n in range(ACCS):
                    v.wait_ge(landed[n], 16)
                    link(v.tensor_tensor(Y, Y, bufs[n] if n else k.X[:], ALU.add))
                norm.vector(link, v, Y, k.X[:])

            @block.scalar
            def _(a):
                norm.scalar(a, Y, k.X[:])


def phase_heads_edges(nc, k, table, Q3, agg, AW, room, before):
    with ExitStack() as c:
        sb = lambda n, s, d: c.enter_context(nc.sbuf_tensor("h_" + n, s, d))
        sem = semaphores(nc, c, "h_")
        idx = sb("idx", [P, U], I32)
        rows = room[:, 0:U * 2 * D].rearrange("p (u d) -> p u d", d=2 * D)
        rel = sb("rel", [P, GROUPS, G * P], BF16)
        oht = sb("oht", [P, 2, G * P], BF16)
        oh = sb("oh", [P, 2, G, P], F32)
        kq = sb("kq", [P, G, D], F32)
        score = sb("score", [P, 2, G, HEADS], F32)
        msg = sb("msg", [P, 2, G, AW], F32)
        rel_in = [sem(f"rel_in{n}") for n in range(GROUPS)]
        row_in = k.row_in
        idx_ready, pool_turn, sp_turn = sem("idx_ready"), sem("pool_turn"), sem("sp_turn")
        oht_ready, oh_ready, product, kq_ready, clipped, weighed, msg_ready, spread, added, zero, chain = (
            sem(n) for n in ("oht_ready", "oh_ready", "product", "kq_ready", "clipped", "weighed", "msg_ready", "spread",
                             "added", "zero", "chain"))
        rel_flat = k.rel_rows.rearrange("(o s) e -> o (s e)", o=1)
        sums = lambda j, q: k.psum[:, 2 + 2 * (j % 2) + q // 2, (q % 2) * AW:(q % 2 + 1) * AW]
        with nc.Block() as block:
            @block.sync
            def _(sp):
                with sp.Fori(0, ITERS) as i:
                    for j in range(GROUPS):
                        at = bass.ds(sp.snap((i * U + j * G) * P), G * P)
                        sp.wait_ge(oht_ready, GROUPS * i + j + 1)
                        sp.sem_inc(sp_turn, 1)
                        sp.dma_start(rel[:, j, :], rel_flat[:, at].to_broadcast([P, G * P])).then_inc(rel_in[j], 16)

            @block.gpsimd
            def _(g):
                with g.Fori(0, ITERS) as i:
                    for u in range(U):
                        if u % G == 0:
                            g.wait_ge(idx_ready, GROUPS * i + u // G + 1)
                            g.wait_ge(msg_ready, GROUPS * i + u // G + 1)
                            g.sem_inc(pool_turn, 1)
                        g.indirect_dma_start(out=rows[:, u, :], out_offset=None, in_=table,
                                             in_offset=bass.IndirectOffsetOnAxis(ap=idx[:, u:u + 1], axis=0)
                                             ).then_inc(row_in[u], 16)

            @block.tensor
            def _(pe):
                regs = {}

                def expand(i, j):
                    if j == 0:
                        regs["node"] = load_steps(nc, pe, k.ek[1], i * U, RT - 1)
                    n = GROUPS * i + j
                    pe.wait_ge(oht_ready, n + 1 + GROUPS)
                    pe.wait_ge(kq_ready, n + 1)
                    for q in range(G):
                        for part in range(3):
                            mm = pe.matmul(k.psum[:, j % 2, q * D:(q + 1) * D], oht[:, j % 2, q * P:(q + 1) * P],
                                           Q3[:, bass.ds(regs["node"][G * j + q], 1), part, :],
                                           start=(part == 0), stop=(part == 2))
                    mm.then_inc(product, 1)

                def sum_into_nodes(i, j):
                    n = GROUPS * i + j
                    pe.wait_ge(msg_ready, n + 1 + GROUPS)
                    pe.wait_ge(oh_ready, n + 1)
                    pe.wait_ge(added, G * n + G)
                    for q in range(G):
                        mm = pe.matmul(sums(j, q), oh[:, j % 2, q, :], msg[:, j % 2, q, :], start=True, stop=True)
                    mm.then_inc(spread, 1)

                pipeline(pe, ITERS, GROUPS, expand, sum_into_nodes, lags=(0, 2))

            @block.scalar
            def _(a):
                with a.Fori(0, ITERS) as i:
                    for j in range(GROUPS):
                        n = GROUPS * i + j
                        a.wait_ge(clipped, n + 1)
                        a.wait_ge(spread, n + 1)
                        nc.scalar.activation(msg[:, j % 2, :, D:D + HEADS], score[:, j % 2], ACT.Exp).then_inc(weighed, 1)

            @block.vector
            def _(v):
                v.memset(agg, 0.0).then_inc(zero, 1)
                v.memset(msg[:, :, :, AW - 1:AW], 1.0).then_inc(zero, 1)
                v.wait_ge(zero, 2)
                v.sem_inc(oht_ready, GROUPS)
                v.sem_inc(kq_ready, 2)
                v.sem_inc(msg_ready, GROUPS)
                v.sem_inc(spread, 2)
                v.sem_inc(added, 2 * G)

                def stage(i, j):
                    v.tensor_copy(idx[:, G * j:G * j + G], k.src_idx[:, bass.ds(i * U + G * j, G)]).then_inc(idx_ready, 1)

                for j in range(GROUPS):
                    stage(0, j)

                def expand_matrix(i, j):
                    v.wait_ge(rel_in[j], 16 * i + 16)
                    v.tensor_scalar(oht[:, j % 2, :], rel[:, j, :], k.part[:, 0:1], None, ALU.is_equal).then_inc(oht_ready, 1)

                def sum_matrix(i, j):
                    v.wait_ge(spread, GROUPS * i + j + 1)
                    v.tensor_tensor(oh[:, j % 2], k.lane[:].unsqueeze(1).to_broadcast([P, G, P]),
                                    k.rel_cols[:, bass.ds(i * U + G * j, G)].unsqueeze(2).to_broadcast([P, G, P]),
                                    ALU.is_equal).then_inc(oh_ready, 1)

                def key_times_query(i, j):
                    v.wait_ge(product, GROUPS * i + j + 1)
                    for q in range(G):
                        v.wait_ge(row_in[G * j + q], 16 * i + 16 * (before + 1))
                    v.tensor_tensor(kq[:], k.psum[:, j % 2, :].rearrange("p (q d) -> p q d", d=D),
                                    rows[:, G * j:G * j + G, 0:D], ALU.mult).then_inc(kq_ready, 1)

                def sum_of_head(i, j):
                    n = GROUPS * i + j
                    v.wait_ge(kq_ready, n + 3)
                    v.tensor_reduce(score[:, j % 2].rearrange("p q h -> p (q h)"),
                                    kq[:].rearrange("p q (h e) -> p (q h) e", e=HD), AX.X, ALU.add).then_inc(chain, 1)

                def clip(i, j):
                    v.wait_ge(chain, GROUPS * i + j + 1)
                    v.tensor_scalar(score[:, j % 2], score[:, j % 2], -5.0, 5.0, ALU.max, ALU.min).then_inc(clipped, 1)

                def messages(i, j):
                    v.wait_ge(weighed, GROUPS * i + j + 1)
                    v.tensor_tensor(msg[:, j % 2, :, 0:D].rearrange("p q (h e) -> p q h e", e=HD),
                                    rows[:, G * j:G * j + G, D:2 * D].rearrange("p q (h e) -> p q h e", e=HD),
                                    msg[:, j % 2, :, D:D + HEADS].unsqueeze(3).to_broadcast([P, G, HEADS, HD]),
                                    ALU.mult).then_inc(msg_ready, 1)
                    stage(i + 1, j)

                regs = {}

                def add(q):
                    def add_one(i, j):
                        if j == 0 and q == 0:
                            regs["node"] = load_steps(nc, v, k.ek[1], i * U, RT - 1)
                        n = GROUPS * i + j
                        if q == 0:
                            v.wait_ge(spread, n + 3)
                        t = bass.ds(regs["node"][G * j + q], 1)
                        v.wait_ge(added, G * n + q + 2 * G)
                        v.tensor_tensor(agg[:, t, :], agg[:, t, :], sums(j, q).unsqueeze(1), ALU.add).then_inc(added, 1)
                    return add_one

                pipeline(v, ITERS, GROUPS, expand_matrix, add(0), key_times_query, add(1), sum_of_head, add(2), clip,
                         messages, add(3), sum_matrix, lags=(0, 4, 1, 4, 1, 4, 1, 2, 4, 1), loads=4)


def phase_heads_nodes(nc, k, agg, AW, Y, S):
    with ExitStack() as c:
        sem = semaphores(nc, c, "g_")
        norm = Norm(nc, c, sem, "g_")
        chain = sem("chain")
        inv = S.rearrange("p t d -> p (t d)")[:, 0:NT * HEADS].rearrange("p (t h) -> p t h", h=HEADS)
        with nc.Block() as block:
            @block.vector
            def _(v):
                link = vector_chain(chain, v)
                link(v.tensor_copy(k.degree[:], agg[:, :, AW - 1]))
                link(v.tensor_scalar(inv, agg[:, :, D:D + HEADS], 1e-30, None, ALU.max))
                link(v.reciprocal(inv, inv))
                link(v.tensor_tensor(Y.rearrange("p t (h e) -> p t h e", e=HD),
                                     agg[:, :, 0:D].rearrange("p t (h e) -> p t h e", e=HD),
                                     inv.unsqueeze(3).to_broadcast([P, NT, HEADS, HD]), ALU.mult))
                link(v.tensor_tensor(Y, Y, k.X[:], ALU.add))
                norm.vector(link, v, Y, k.X[:])

            @block.scalar
            def _(a):
                norm.scalar(a, Y, k.X[:])


def phase_relation_edges(nc, k, table, D3, agg, before):
    with ExitStack() as c:
        sb = lambda n, s, d: c.enter_context(nc.sbuf_tensor("r_" + n, s, d))
        sem = semaphores(nc, c, "r_")
        room = k.X[:].rearrange("p t d -> p (t d)")
        rows = room[:, 0:U * HID].rearrange("p (u d) -> p u d", d=HID)
        msg = room[:, U * HID:U * HID + 2 * G * HID].rearrange("p (h q d) -> p h q d", h=2, d=HID)
        idx = sb("idx", [P, U], I32)
        ea = sb("ea", [P, U, P], F32)
        rel = sb("rel", [P, GROUPS, G * P], BF16)
        oht = sb("oht", [P, 2, G * P], BF16)
        oh = sb("oh", [P, 2, G, P], F32)
        ea_in = [sem(f"ea_in{u}") for u in range(U)]
        rel_in = [sem(f"rel_in{n}") for n in range(GROUPS)]
        row_in = k.row_in
        idx_ready, pool_turn, sp_turn = sem("idx_ready"), sem("pool_turn"), sem("sp_turn")
        oht_ready, oh_ready, product, summed, msg_ready, spread, added, zero = (
            sem(n) for n in ("oht_ready", "oh_ready", "product", "summed", "msg_ready", "spread", "added", "zero"))
        rel_flat = k.rel_rows.rearrange("(o s) e -> o (s e)", o=1)
        hidden = lambda j, q: k.psum[:, 2 * (j % 2) + q // 2, (q % 2) * HID:(q % 2 + 1) * HID]
        sums = lambda j, q: k.psum[:, 4 + 2 * (j % 2) + q // 2, (q % 2) * HID:(q % 2 + 1) * HID]
        with nc.Block() as block:
            @block.sync
            def _(sp):
                with sp.Fori(0, ITERS) as i:
                    tile = load_steps(nc, sp, k.ek[0], i * U, ET - 1)
                    for u in range(U):
                        j = u // G
                        if u % G == 0:
                            at = bass.ds(sp.snap((i * U + u) * P), G * P)
                            sp.wait_ge(oht_ready, GROUPS * i + j + 1)
                            sp.sem_inc(sp_turn, 1)
                            sp.dma_start(rel[:, j, :], rel_flat[:, at].to_broadcast([P, G * P])).then_inc(rel_in[j], 16)
                            sp.wait_ge(product, GROUPS * i + j + 1)
                            sp.sem_inc(sp_turn, 1)
                        sp.dma_start(ea[:, u, :], k.ea_t[:, bass.ds(tile[u] * P, P)]).then_inc(ea_in[u], 16)

            @block.gpsimd
            def _(g):
                with g.Fori(0, ITERS) as i:
                    for u in range(U):
                        if u % G == 0:
                            g.wait_ge(idx_ready, GROUPS * i + u // G + 1)
                            g.wait_ge(summed, 2 * (GROUPS * i + u // G) + 2)
                            g.sem_inc(pool_turn, 1)
                        g.indirect_dma_start(out=rows[:, u, :], out_offset=None, in_=table,
                                             in_offset=bass.IndirectOffsetOnAxis(ap=idx[:, u:u + 1], axis=0)
                                             ).then_inc(row_in[u], 16)

            @block.tensor
            def _(pe):
                pe.sem_inc(product, GROUPS)
                regs = {}

                def hidden_product(i, j):
                    if j == 0:
                        regs["node"] = load_steps(nc, pe, k.ek[1], i * U, RT - 1)
                    n = GROUPS * i + j
                    pe.wait_ge(summed, 2 * n + 6)
                    pe.wait_ge(oht_ready, n + 1 + GROUPS)
                    for q in range(G):
                        pe.wait_ge(ea_in[G * j + q], 16 * i + 16)
                        pe.matmul(hidden(j, q), ea[:, G * j + q, :], k.w["L3_gnn_re_w1"][:, 2 * HID:3 * HID], start=True, stop=False)
                        for part in range(3):
                            mm = pe.matmul(hidden(j, q), oht[:, j % 2, q * P:(q + 1) * P],
                                           D3[:, bass.ds(regs["node"][G * j + q], 1), part, :],
                                           start=False, stop=(part == 2))
                        if q == G - 1:
                            mm.then_inc(product, 1)

                def sum_into_nodes(i, j):
                    n = GROUPS * i + j
                    pe.wait_ge(msg_ready, n + 1)
                    pe.wait_ge(oh_ready, n + 1)
                    pe.wait_ge(added, G * n + G)
                    for q in range(G):
                        mm = pe.matmul(sums(j, q), oh[:, j % 2, q, :], msg[:, j % 2, q, :], start=True, stop=True)
                    mm.then_inc(spread, 1)

                pipeline(pe, ITERS, GROUPS, hidden_product, sum_into_nodes, lags=(0, 2))

            @block.scalar
            def _(a):
                with a.Fori(0, ITERS) as i:
                    for j in range(GROUPS):
                        a.wait_ge(summed, 2 * (GROUPS * i + j) + 10)
                        nc.scalar.activation(msg[:, j % 2], msg[:, j % 2], ACT.Relu).then_inc(msg_ready, 1)

            @block.vector
            def _(v):
                v.memset(agg, 0.0).then_inc(zero, 1)
                v.wait_ge(zero, 1)
                v.sem_inc(oht_ready, GROUPS)
                v.sem_inc(summed, 2 * GROUPS)
                v.sem_inc(spread, 2)
                v.sem_inc(added, 2 * G)

                def stage(i, j):
                    v.tensor_copy(idx[:, G * j:G * j + G], k.src_idx[:, bass.ds(i * U + G * j, G)]).then_inc(idx_ready, 1)

                for j in range(GROUPS):
                    stage(0, j)

                def expand_matrix(i, j):
                    v.wait_ge(rel_in[j], 16 * i + 16)
                    v.tensor_scalar(oht[:, j % 2, :], rel[:, j, :], k.part[:, 0:1], None, ALU.is_equal).then_inc(oht_ready, 1)

                def sum_matrix(i, j):
                    v.wait_ge(spread, GROUPS * i + j + 1)
                    v.tensor_tensor(oh[:, j % 2], k.lane[:].unsqueeze(1).to_broadcast([P, G, P]),
                                    k.rel_cols[:, bass.ds(i * U + G * j, G)].unsqueeze(2).to_broadcast([P, G, P]),
                                    ALU.is_equal).then_inc(oh_ready, 1)

                def add_rows(h):
                    def add_half(i, j):
                        if h == 0:
                            v.wait_ge(product, GROUPS * i + j + 1 + GROUPS)
                        for q in (2 * h, 2 * h + 1):
                            v.wait_ge(row_in[G * j + q], 16 * i + 16 * (before + 1))
                        v.tensor_tensor(msg[:, j % 2, 2 * h:2 * h + 2, :].rearrange("p q d -> p (q d)"),
                                        k.psum[:, 2 * (j % 2) + h, :],
                                        rows[:, G * j + 2 * h:G * j + 2 * h + 2, :].rearrange("p q d -> p (q d)"),
                                        ALU.add).then_inc(summed, 1)
                        if h == 1:
                            stage(i + 1, j)
                    return add_half

                regs = {}

                def add_sums(q):
                    def add_one(i, j):
                        if j == 0 and q == 0:
                            regs["node"] = load_steps(nc, v, k.ek[1], i * U, RT - 1)
                        n = GROUPS * i + j
                        if q == 0:
                            v.wait_ge(spread, n + 3)
                        t = bass.ds(regs["node"][G * j + q], 1)
                        v.wait_ge(added, G * n + q + 2 * G)
                        v.tensor_tensor(agg[:, t, :], agg[:, t, :], sums(j, q).unsqueeze(1), ALU.add).then_inc(added, 1)
                    return add_one

                pipeline(v, ITERS, GROUPS, expand_matrix, add_sums(0), sum_matrix, add_sums(1), add_rows(0), add_sums(2),
                         add_rows(1), add_sums(3), lags=(0, 3, 1, 3, 1, 3, 1, 3), loads=3)


def phase_update_nodes(nc, k, x_kept, agg, Y, room):
    with ExitStack() as c:
        sb = lambda n, s, d: c.enter_context(nc.sbuf_tensor("u_" + n, s, d))
        sem = semaphores(nc, c, "u_")
        w_in = k.w["L3_gnn_re_w1"][:].rearrange("p (f h) -> p f h", f=3)
        b_in, re2t = k.kv, k.kv_b
        w_deg = sb("w_deg", [P, 2], F32)
        w_out, b_hid, b_out, re_b2 = k.w_out, k.b_hid, k.b_out, k.re_b2
        deg_t = sb("deg_t", [NT, P], F32)
        wide = ROUND * 3 * P
        tile_all = sb("tile", [P, wide], F32)
        deg_rows = room[:, wide:wide + NP]
        hid = room[:, wide + NP:wide + NP + 8 * P].rearrange("p (h n) -> p h n", h=2)
        of_group = lambda buf, j: buf[:, BASES[j] * 3 * P:(BASES[j] + SIZES[j]) * 3 * P].rearrange("p (f n) -> p f n", f=3)
        tile, tile_t = ([of_group(buf, j) for j in range(NG)] for buf in (tile_all, room))
        weighed, folded, fold_copied, deg_turned, row_made, staged, turned, copied, hidden, active, product, added = (
            sem(n) for n in ("weighed", "folded", "fold_copied", "deg_turned", "row_made", "staged", "turned", "copied",
                             "hidden", "active", "product", "added"))
        x_in = [sem(f"x_in{n}") for n in range(2)]
        bank = lambda j, h: (k.psum[:, (3, 5, 7)[j] + h, 0:SIZES[j] * P] if SIZES[j] == 4 else
                             k.psum[:, (3, 5, 7)[j], h * SIZES[j] * P:(h + 1) * SIZES[j] * P])
        tiles = lambda i, j: bass.ds(ROUND * i + BASES[j], SIZES[j])
        with nc.Block() as block:
            @block.sync
            def _(sp):
                sp.dma_start(k.X[:, 0:ROUND, :], x_kept[:, 0:ROUND, :]).then_inc(x_in[0], 16)
                sp.wait_ge(fold_copied, 1)
                sp.dma_start(k.deg_dram, deg_t[:]).then_inc(row_made, 16)
                sp.wait_ge(row_made, 16)
                sp.dma_start(deg_rows, k.deg_dram.rearrange("(o t) e -> o (t e)", o=1).to_broadcast([P, NP])).then_inc(row_made, 16)
                sp.dma_start(k.X[:, ROUND:NT, :], x_kept[:, ROUND:NT, :]).then_inc(x_in[1], 16)

            @block.tensor
            def _(pe):
                pe.sem_inc(product, 1)
                pe.transpose(k.psum[0:NT, 5, 0:P], k.degree[:], k.ident[:]).then_inc(deg_turned, 1)
                for h in range(2):
                    pe.matmul(k.psum[:, 3, h * HID:(h + 1) * HID], re2t[:, h * P:(h + 1) * P], b_in[:], start=True, stop=True)
                for h in range(2):
                    mm = pe.matmul(k.psum[:, 4, h:h + 1], b_in[:, h * P:(h + 1) * P], re_b2[:], start=True, stop=True)
                mm.then_inc(folded, 1)

                def turn(i, j):
                    n = NG * i + j
                    pe.wait_ge(staged, n + 1)
                    for f in range(3):
                        pe.wait_ge(copied, 3 * n + f + 1)
                        for q in range(SIZES[j]):
                            mm = pe.transpose(k.psum[:, f, q * P:(q + 1) * P], tile[j][:, f, q * P:(q + 1) * P], k.ident[:])
                        mm.then_inc(turned, 1)

                def hide(i, j):
                    n = NG * i + j
                    pe.wait_ge(copied, 3 * n + 6)
                    pe.wait_ge(fold_copied, 3)
                    pe.wait_ge(added, n + 1)
                    for h in range(2):
                        half = slice(h * P, (h + 1) * P)
                        for f in range(3):
                            mm = pe.matmul(bank(j, h), w_in[:, f, half], tile_t[j][:, f, :], start=(f == 0), stop=(f == 2))
                        mm.then_inc(hidden, 1)

                def out(i, j):
                    n = NG * i + j
                    pe.wait_ge(active, 2 * n + 2)
                    for q in range(SIZES[j]):
                        for h in range(2):
                            mm = pe.matmul(bank(j, 0)[:, q * D:(q + 1) * D], hid[:, h, q * P:(q + 1) * P], w_out[:, h, :],
                                           start=(h == 0), stop=(h == 1))
                    mm.then_inc(product, 1)

                pipeline(pe, ROUNDS, NG, out, hide, turn, lags=(3, 1, 0))

            @block.scalar
            def _(a):
                def activate(i, j):
                    n = NG * i + j
                    for h in range(2):
                        a.wait_ge(weighed, 2 * n + h + 1)
                        nc.scalar.activation(hid[:, h, 0:SIZES[j] * P], hid[:, h, 0:SIZES[j] * P], ACT.Relu,
                                             bias=b_hid[:, h:h + 1]).then_inc(active, 1)

                pipeline(a, ROUNDS, NG, activate)

            @block.vector
            def _(v):
                v.wait_ge(deg_turned, 1)
                v.tensor_copy(deg_t[:], k.psum[0:NT, 5, 0:P]).then_inc(fold_copied, 1)
                v.wait_ge(folded, 1)
                v.tensor_copy(w_in[:, 1:3, :], k.psum[:, 3, :].rearrange("p (h d) -> p h d", h=2)).then_inc(fold_copied, 1)
                v.tensor_copy(w_deg[:], k.psum[:, 4, 0:2]).then_inc(fold_copied, 1)
                v.sem_inc(copied, 3)
                v.sem_inc(added, NG)
                v.wait_ge(x_in[0], 16)

                def stage(i, j):
                    if not (isinstance(i, int) and i == 0):
                        v.wait_ge(x_in[1], 16)
                    v.tensor_copy(tile[j][:, 0, :].rearrange("p (t d) -> p t d", d=P), k.X[:, tiles(i, j), :])
                    for f in range(2):
                        ins = v.tensor_copy(tile[j][:, 1 + f, :].rearrange("p (t d) -> p t d", d=P),
                                            agg[:, tiles(i, j), f * P:(f + 1) * P])
                    ins.then_inc(staged, 1)

                def copy(i, j):
                    for f in range(3):
                        v.wait_ge(turned, 3 * (NG * i + j) + f + 1)
                        v.tensor_copy(tile_t[j][:, f, :], k.psum[:, f, 0:SIZES[j] * P]).then_inc(copied, 1)

                def weigh(i, j):
                    n = NG * i + j
                    v.wait_ge(product, n + 1)
                    v.wait_ge(row_made, 32)
                    for h in range(2):
                        v.wait_ge(hidden, 2 * n + h + 1)
                        v.scalar_tensor_tensor(out=hid[:, h, 0:SIZES[j] * P],
                                               in0=deg_rows[:, bass.ds((ROUND * i + BASES[j]) * P, SIZES[j] * P)],
                                               scalar=w_deg[:, h:h + 1], in1=bank(j, h), op0=ALU.mult, op1=ALU.add).then_inc(weighed, 1)

                def add(i, j):
                    v.wait_ge(product, NG * i + j + 2)
                    v.tensor_tensor(Y[:, tiles(i, j), :], bank(j, 0).rearrange("p (t d) -> p t d", d=D),
                                    b_out[:].unsqueeze(1).to_broadcast([P, SIZES[j], D]), ALU.add).then_inc(added, 1)

                def residual(i, j):
                    v.wait_ge(added, NG * i + j + 1 + NG)
                    v.tensor_tensor(Y[:, tiles(i, j), :], Y[:, tiles(i, j), :], k.X[:, tiles(i, j), :], ALU.add)

                pipeline(v, ROUNDS, NG, add, stage, copy, weigh, residual, lags=(4, 0, 1, 2, 4))


def phase_last_norm(nc, k, Y, out):
    with ExitStack() as c:
        sem = semaphores(nc, c, "z_")
        norm = Norm(nc, c, sem, "z_")
        chain, stored = sem("chain"), sem("stored")
        with nc.Block() as block:
            @block.vector
            def _(v):
                link = vector_chain(chain, v)
                norm.vector(link, v, Y, k.X[:])

            @block.scalar
            def _(a):
                norm.scalar(a, Y, k.X[:])

            @block.sync
            def _(sp):
                full = N // P
                for n, cut in enumerate(norm.CUTS):
                    sp.wait_ge(norm.done, n + 1)
                    to = min(cut.stop, full)
                    sp.dma_start(out[cut.start * P:to * P, :].rearrange("(t p) d -> p t d", p=P),
                                 k.X[:, cut.start:to, :]).then_inc(stored, 16)
                sp.dma_start(out[full * P:N, :], k.X[0:N - full * P, full, :]).then_inc(stored, 16)
                sp.wait_ge(stored, 48)


TRANSPOSED = {"L0_gnn_w1t": "L0_gnn_w1", "L0_gnn_wet": "L0_gnn_we", "L3_gnn_re_w2t": "L3_gnn_re_w2"}
AS_THEY_ARE = ("L1_gnn_W_w", "L2_gnn_Wq", "L2_gnn_Wk", "L2_gnn_Wv", "L3_gnn_re_w1", "L3_gnn_ea_w1", "L3_gnn_ea_w2")
ROWS = ("L0_gnn_b1", "L0_gnn_be", "L0_gnn_eps", "L0_gnn_gn_weight", "L0_gnn_gn_bias", "L0_gnn_gn_mean_scale",
        "L1_gnn_W_b", "L1_gnn_a_w", "L1_gnn_a_b", "L2_gnn_bq", "L2_gnn_bk", "L2_gnn_bv", "L3_gnn_re_b1",
        "L3_gnn_re_b2", "L3_gnn_ea_b1", "L3_gnn_ea_b2")


RESIDENT = ("L0_gnn_w1t", "L0_gnn_wet", "L1_gnn_W_w", "L2_gnn_Wq", "L3_gnn_re_w1")
ROWS_RESIDENT = ("L0_gnn_b1", "L0_gnn_be", "L0_gnn_gn_weight", "L0_gnn_gn_bias", "L0_gnn_gn_mean_scale",
                 "L1_gnn_W_b", "L1_gnn_a_w", "L2_gnn_bq", "L3_gnn_re_b1")


def build(nc, ap, out):
    k = Kit()
    k.small = ap
    k.ea_t, k.src, k.dst = ap["ea_t"], ap["src"], ap["dst"]
    dram = lambda n, s, d: nc.dram_tensor(n, s, d, kind="Internal").ap()
    k.ek_dram = dram("ek_dram", (2, ST), I32)
    k.deg_dram = dram("deg_dram", (NT, P), F32)
    k.rel_rows = dram("rel_rows", (ST, P), BF16)
    k.src_rows = dram("src_rows", (ST, P), F32)
    k.lo_rows = dram("lo_rows", (ST, P), BF16)
    table0 = dram("table0", (NP, D), F32)
    table_kv = dram("table_kv", (NP, 2 * D), F32)
    table_ps = dram("table_ps", (NP, HID), F32)
    x_dram = dram("x_dram", (NP, D), F32)
    accs = [dram(f"acc{n}", (AROWS, D), F32) for n in range(ACCS)]
    tiled = lambda t: t.rearrange("(t p) d -> p t d", p=P)
    with ExitStack() as c:
        sb = lambda n, s, d: c.enter_context(nc.sbuf_tensor(n, s, d))
        k.psum = c.enter_context(nc.psum_tensor("psum", [P, 8, 512], F32))
        k.lane_i, k.part_i = sb("lane_i", [P, P], I32), sb("part_i", [P, 1], I32)
        k.trash_i, k.trash = sb("trash_i", [P, G], I32), sb("trash", [P, G], F32)
        k.lane, k.part, k.minus_part = sb("lane", [P, P], F32), sb("part", [P, 1], F32), sb("minus_part", [P, 1], F32)
        k.ident, k.before, k.ones = sb("ident", [P, P], F32), sb("before", [P, P], F32), sb("ones", [P, P], F32)
        k.degree = sb("degree", [P, NT], F32)
        k.is_node = sb("is_node", [P, NT - RT + 1], F32)
        k.rel_cols, k.src_cols, k.src_idx = sb("rel_cols", [P, ST], F32), sb("src_cols", [P, ST], F32), sb("src_idx", [P, ST], I32)
        k.hi_cols = sb("hi_cols", [P, ST], F32)
        k.ek = [sb("edge_tile", [1, ST], I32), sb("node_tile", [1, ST], I32)]
        k.one_eps = sb("one_eps", [P, 1], F32)
        k.w = {n: sb("w_" + n, [P, ap[n].shape[0] // P * ap[n].shape[1]], F32) for n in RESIDENT}
        k.kv = sb("w_kv", [P, 2 * D], F32)
        k.b = {n: sb("b_" + n, [P, ap[n].shape[1]], F32) for n in ROWS_RESIDENT}
        k.kv_b = sb("b_kv", [P, 2 * D], F32)
        k.w_out, k.b_hid = sb("w_out", [P, 2, D], F32), sb("b_hid", [P, 2], F32)
        k.b_out, k.re_b2 = sb("b_out", [P, D], F32), sb("re_b2", [P, 1], F32)
        k.table_b, k.none = sb("b_table", [P, D], F32), sb("b_none", [P, HID], F32)
        k.row_in = [c.enter_context(nc.semaphore(f"row_in{u}")) for u in range(U)]
        k.acc_done = [c.enter_context(nc.semaphore(f"acc_done{n}")) for n in range(ACCS)]
        k.gathered = c.enter_context(nc.semaphore("gathered"))
        k.kv_stored, k.ps_stored = c.enter_context(nc.semaphore("table_kv_stored")), c.enter_context(nc.semaphore("table_ps_stored"))
        k.turn_free = c.enter_context(nc.semaphore("turn_free"))
        k.X = sb("X", [P, NT, D], F32)
        phase_tables(nc, k)
        R1 = sb("R1", [P, NT, 256], F32)
        R3 = sb("R3", [P, NT * 3 * 256], BF16)
        r1 = R1[:].rearrange("p t d -> p (t d)")
        r3 = R3[:].bitcast(F32)
        half1 = lambda b: r1[:, b * NT * D:(b + 1) * NT * D].rearrange("p (t d) -> p t d", d=D)
        half3 = lambda b: r3[:, b * NT * D:(b + 1) * NT * D].rearrange("p (t d) -> p t d", d=D)

        H = half3(0)
        phase_linear(nc, k, "h0", k.X[:], k.w["L0_gnn_w1t"][:], D, k.b["L0_gnn_b1"][:], H,
                     tables=[(k.table_b[:], half1(0), tiled(table0))])
        agg = half1(0)
        phase_conv_edges(nc, k, table0, agg, r3[:, NT * D:], 0)
        phase_conv_nodes(nc, k, H, agg, half1(1))

        upper = r3[:, 3 * NT * D // 2:][:, 0:NT * D].rearrange("p (t d) -> p t d", d=D)
        H3 = R3[:, 0:NT * 3 * D].rearrange("p (t n d) -> p t n d", n=3, d=D)
        phase_linear(nc, k, "h1", k.X[:], k.w["L1_gnn_W_w"][:], D, k.b["L1_gnn_W_b"][:], half1(0), also=half1(1), parts=H3)
        with ExitStack() as c1:
            k.src_score = c1.enter_context(nc.sbuf_tensor("src_score", [P, NT, 3], BF16))
            k.dst_score = c1.enter_context(nc.sbuf_tensor("dst_score", [P, NT, 3], BF16))
            scores = r3[:, 3 * NT * D // 2:][:, 0:ST]
            phase_scores_nodes(nc, k, half1(1), half1(0), upper)
            phase_scores_edges(nc, k, scores, r1, R3[:, 3 * NT * D + 2 * ST:])
            phase_softmax(nc, k, scores)
        phase_attend(nc, k, scores, H3, accs, r1)
        phase_attend_nodes(nc, k, accs, half1(0), half1(1), (half3(0), half3(1)))

        stores = phase_linear(nc, k, "kv", k.X[:], k.kv[:], 2 * D, k.kv_b[:], R1[:], tables=[(None, None, tiled(table_kv))],
                              storing=k.kv_stored)
        phase_linear(nc, k, "q", k.X[:], k.w["L2_gnn_Wq"][:], D, k.b["L2_gnn_bq"][:], upper,
                     scale=HD ** -0.5, parts=H3, after=(k.kv_stored, stores))
        AW = D + HEADS + 1
        agg2 = r1[:, 0:NT * AW].rearrange("p (t w) -> p t w", w=AW)
        phase_heads_edges(nc, k, table_kv, H3, agg2, AW, r3[:, 3 * NT * D // 2:], ITERS)
        phase_heads_nodes(nc, k, agg2, AW, half3(0), half3(1))

        w1 = k.w["L3_gnn_re_w1"]
        stores = phase_linear(nc, k, "per_src", k.X[:], w1[:, 0:HID], HID, k.none[:], R1[:], tables=[(None, None, tiled(table_ps))],
                              extra=[(tiled(x_dram), k.X[:])], storing=k.ps_stored)
        D3 = R3[:].rearrange("p (t n d) -> p t n d", n=3, d=HID)
        phase_linear(nc, k, "per_dst", k.X[:], w1[:, HID:2 * HID], HID, k.b["L3_gnn_re_b1"][:], R1[:], parts=D3,
                     extra=[(w1[:, 0:HID], ap["L3_gnn_ea_w1"][0:D, :]), (k.kv[:], ap["L3_gnn_ea_w1"][D:2 * D, :]),
                            (k.kv_b[:], ap["L3_gnn_re_w2t"])], after=(k.ps_stored, stores))
        phase_relation_edges(nc, k, table_ps, D3, R1[:], 2 * ITERS)
        phase_update_nodes(nc, k, tiled(x_dram), R1[:], half3(0), r3[:, NT * D:])
        phase_last_norm(nc, k, half3(0), out)


def layout(inputs):
    x = np.zeros((NP, D), np.float32)
    x[:N] = inputs["x"]
    ea_t = np.zeros((D, EP), np.float32)
    ea_t[:, :E] = np.asarray(inputs["edge_attr_128"]).T
    arrays = {"x": x, "ea_t": ea_t}
    for name in ("src", "dst"):
        padded = np.full((EP,), PAD_NODE, np.int32)
        padded[:E] = inputs[name]
        arrays[name] = padded.reshape(ET, P)
    for to, of in TRANSPOSED.items():
        arrays[to] = np.ascontiguousarray(np.asarray(inputs[of]).T)
    for name in AS_THEY_ARE:
        arrays[name] = np.ascontiguousarray(inputs[name])
    for name in ROWS:
        arrays[name] = np.asarray(inputs[name]).reshape(1, -1)
    return arrays


def kernel(**inputs):
    import concourse.bacc as bacc
    from concourse.bass_utils import run_bass_kernel_spmd

    arrays = layout(inputs)
    nc = bacc.Bacc("TRN2", target_bir_lowering=False, num_devices=1)
    ap = {name: nc.dram_tensor("in_" + name, a.shape, mybir.dt.from_np(a.dtype), kind="ExternalInput").ap()
          for name, a in arrays.items()}
    out = nc.dram_tensor("out", (N, D), F32, kind="ExternalOutput").ap()
    build(nc, ap, out)
    r = run_bass_kernel_spmd(nc, [{"in_" + name: a for name, a in arrays.items()}], core_ids=[0])
    return r.results[0]["out"]
```
